# Optimizing a Trainium2 kernel written in Bass

```python
import numpy as np
import jax
import jax.numpy as jnp

def _softmax(x, axis=-1):
    return jax.nn.softmax(x, axis=axis)

def _gelu(x):
    return jax.nn.gelu(x, approximate=True)

def _silu(x):
    return jax.nn.silu(x)

def _sigmoid(x):
    return jax.nn.sigmoid(x)

def _layernorm(x, axis=-1, eps=1e-05):
    m = jnp.mean(x, axis=axis, keepdims=True)
    v = jnp.var(x, axis=axis, keepdims=True)
    return (x - m) / jnp.sqrt(v + eps)

def _scatter_add(tgt, idx, src, axis=0):
    return tgt.at[idx].add(src)

def _segment_sum(src, seg, n):
    return jax.ops.segment_sum(src, seg, n)
kernel_name = 'mk_prb_d2_jaxref_r8_60b62a'

def setup_inputs(seed: int=0):
    np.random.seed(seed)
    _w = jnp.asarray

    def _L0_attn_setup():
        import jax, jax.numpy as jnp
        import numpy as np
        import math
        BATCH = 4
        SEQ = 512
        EMBED = 128
        NUM_HEADS = 16
        HEAD_DIM = EMBED // NUM_HEADS
        WINDOW_SIZE = 128
        RADIUS = 2 * WINDOW_SIZE
        CHUNK = RADIUS
        key = jax.random.key(seed)
        ks = jax.random.split(key, 9)
        init = lambda k, shape: (0.02 * jax.random.normal(k, shape)).astype(jnp.float32)
        return {'hidden_states': jax.random.normal(ks[0], (BATCH, SEQ, EMBED), dtype=jnp.float32), 'wq': init(ks[1], (EMBED, EMBED)), 'bq': init(ks[2], (EMBED,)), 'wk': init(ks[3], (EMBED, EMBED)), 'bk': init(ks[4], (EMBED,)), 'wv': init(ks[5], (EMBED, EMBED)), 'bv': init(ks[6], (EMBED,)), 'wo': init(ks[7], (EMBED, EMBED)), 'bo': init(ks[8], (EMBED,))}
    _L0_attn_in = _L0_attn_setup()

    def _L0_ffn_setup():
        import jax, jax.numpy as jnp
        import numpy as np
        B, S, H, F, E = (2, 256, 128, 512, 8)
        key = jax.random.key(seed)
        ks = jax.random.split(key, 4)
        x = jax.random.normal(ks[0], (B, S, H), dtype=jnp.float32)
        w_router = jax.random.normal(ks[1], (H, E), dtype=jnp.float32) * 0.02
        w1 = jax.random.normal(ks[2], (E, H, F), dtype=jnp.float32) * 0.02
        b1 = jnp.zeros((E, F), dtype=jnp.float32)
        w2 = jax.random.normal(ks[3], (E, F, H), dtype=jnp.float32) * 0.02
        b2 = jnp.zeros((E, H), dtype=jnp.float32)
        return {'x': x, 'w_router': w_router, 'w1': w1, 'b1': b1, 'w2': w2, 'b2': b2}
    _L0_ffn_in = _L0_ffn_setup()

    def _L1_attn_setup():
        import jax, jax.numpy as jnp
        import numpy as np
        DIM = 128
        HEADS = 16
        DIM_HEAD = 64
        SCALE = 16.0
        EPS = 1e-05

        def layernorm(x, g):
            mean = jnp.mean(x, axis=-1, keepdims=True)
            var = jnp.var(x, axis=-1, keepdims=True)
            return (x - mean) * jax.lax.rsqrt(var + EPS) * g

        def l2norm(t):
            return t / jnp.maximum(jnp.linalg.norm(t, axis=-1, keepdims=True), 1e-12)
        key = jax.random.key(seed)
        ks = jax.random.split(key, 5)
        inner = HEADS * DIM_HEAD
        x = jax.random.normal(ks[0], (2, 256, DIM), dtype=jnp.float32)
        Wq = jax.random.normal(ks[1], (inner, DIM), dtype=jnp.float32) * 0.02
        Wkv = jax.random.normal(ks[2], (2 * DIM_HEAD, DIM), dtype=jnp.float32) * 0.02
        Wout = jax.random.normal(ks[3], (DIM, inner), dtype=jnp.float32) * 0.02
        g1 = jnp.ones((DIM,), dtype=jnp.float32)
        g2 = jnp.ones((DIM,), dtype=jnp.float32)
        return {'x': x, 'g1': g1, 'Wq': Wq, 'Wkv': Wkv, 'Wout': Wout, 'g2': g2}
    _L1_attn_in = _L1_attn_setup()

    def _L1_ffn_setup():
        import jax, jax.numpy as jnp
        import numpy as np
        DIM = 128
        HIDDEN = 384
        SCALE = 1.0 / 127.0

        def _dequant(w_int, dtype):
            return w_int.astype(dtype) * jnp.asarray(SCALE, dtype)
        key = jax.random.key(seed)
        k_x, k_g, k_u, k_d = jax.random.split(key, 4)
        x = jax.random.normal(k_x, (4, 256, DIM), dtype=jnp.float32)
        w_gate = jax.random.randint(k_g, (HIDDEN, DIM), -127, 128, dtype=jnp.int32)
        w_up = jax.random.randint(k_u, (HIDDEN, DIM), -127, 128, dtype=jnp.int32)
        w_down = jax.random.randint(k_d, (DIM, HIDDEN), -127, 128, dtype=jnp.int32)
        return {'x': x, 'w_gate': w_gate, 'w_up': w_up, 'w_down': w_down}
    _L1_ffn_in = _L1_ffn_setup()
    _d = {'L0_attn_hidden_states': _L0_attn_in['hidden_states'], 'L0_attn_wq': _L0_attn_in['wq'], 'L0_attn_bq': _L0_attn_in['bq'], 'L0_attn_wk': _L0_attn_in['wk'], 'L0_attn_bk': _L0_attn_in['bk'], 'L0_attn_wv': _L0_attn_in['wv'], 'L0_attn_bv': _L0_attn_in['bv'], 'L0_attn_wo': _L0_attn_in['wo'], 'L0_attn_bo': _L0_attn_in['bo'], 'L0_ffn_w_router': _L0_ffn_in['w_router'], 'L0_ffn_w1': _L0_ffn_in['w1'], 'L0_ffn_b1': _L0_ffn_in['b1'], 'L0_ffn_w2': _L0_ffn_in['w2'], 'L0_ffn_b2': _L0_ffn_in['b2'], 'L1_attn_g1': _L1_attn_in['g1'], 'L1_attn_Wq': _L1_attn_in['Wq'], 'L1_attn_Wkv': _L1_attn_in['Wkv'], 'L1_attn_Wout': _L1_attn_in['Wout'], 'L1_attn_g2': _L1_attn_in['g2'], 'L1_ffn_w_gate': _L1_ffn_in['w_gate'], 'L1_ffn_w_up': _L1_ffn_in['w_up'], 'L1_ffn_w_down': _L1_ffn_in['w_down']}
    _x0 = _d['L0_attn_hidden_states']
    _d['L0_attn_hidden_states'] = jax.random.normal(jax.random.fold_in(jax.random.key(seed), 1), (8, 512, 128), dtype=_x0.dtype)
    del _x0
    return _d

def reference(L0_attn_hidden_states, L0_attn_wq, L0_attn_bq, L0_attn_wk, L0_attn_bk, L0_attn_wv, L0_attn_bv, L0_attn_wo, L0_attn_bo, L0_ffn_w_router, L0_ffn_w1, L0_ffn_b1, L0_ffn_w2, L0_ffn_b2, L1_attn_g1, L1_attn_Wq, L1_attn_Wkv, L1_attn_Wout, L1_attn_g2, L1_ffn_w_gate, L1_ffn_w_up, L1_ffn_w_down):

    def _L0_attn_ref(hidden_states, wq, bq, wk, bk, wv, bv, wo, bo):
        import jax, jax.numpy as jnp
        import numpy as np
        import math
        BATCH = 4
        SEQ = 512
        EMBED = 128
        NUM_HEADS = 16
        HEAD_DIM = EMBED // NUM_HEADS
        WINDOW_SIZE = 128
        RADIUS = 2 * WINDOW_SIZE
        CHUNK = RADIUS
        B, T, E = hidden_states.shape
        H, D = (NUM_HEADS, HEAD_DIM)
        c = CHUNK
        nC = T // c

        def proj(w, b):
            y = hidden_states @ w + b
            return y.reshape(B, T, H, D).transpose(0, 2, 1, 3)
        q = proj(wq, bq)
        k = proj(wk, bk)
        v = proj(wv, bv)
        scale = jnp.sqrt(jnp.asarray(D, dtype=q.dtype))
        kp = jnp.pad(k, ((0, 0), (0, 0), (c, c), (0, 0)))
        vp = jnp.pad(v, ((0, 0), (0, 0), (c, c), (0, 0)))
        idx = jnp.arange(nC)[:, None] * c + jnp.arange(3 * c)[None, :]
        kb = kp[:, :, idx, :]
        vb = vp[:, :, idx, :]
        qb = q.reshape(B, H, nC, c, D)
        scores = jnp.einsum('bhncd,bhnkd->bhnck', qb, kb) / scale
        qpos = (jnp.arange(nC) * c)[:, None] + jnp.arange(c)
        kpos = (jnp.arange(nC) * c)[:, None] - c + jnp.arange(3 * c)
        valid = (jnp.abs(qpos[:, :, None] - kpos[:, None, :]) <= RADIUS) & (kpos[:, None, :] >= 0) & (kpos[:, None, :] < T)
        scores = jnp.where(valid[None, None], scores, -jnp.inf)
        p = jax.nn.softmax(scores, axis=-1)
        o = jnp.einsum('bhnck,bhnkd->bhncd', p, vb)
        o = o.reshape(B, H, T, D).transpose(0, 2, 1, 3).reshape(B, T, E)
        return o @ wo + bo

    def _L0_ffn_ref(x, w_router, w1, b1, w2, b2):
        import jax, jax.numpy as jnp
        import numpy as np
        B, S, H, F, E = (2, 256, 128, 512, 8)
        'Top-1 MoE layer: route -> per-expert FFN -> weighted combine.\n\n            Faithful to ExpertParallelWrapper._process_moe_layer on a single group:\n            router picks one expert per token with a routing weight; tokens are\n            dispatched to experts (here expressed as a static mask over the fixed\n            expert set), processed by the expert FFN, and scatter-combined back\n            weighted by the routing probability.\n            '
        Bs, Ss, Hs = x.shape
        n_experts = w1.shape[0]
        logits = jnp.einsum('bsh,he->bse', x, w_router)
        probs = jax.nn.softmax(logits, axis=-1)
        sel = jnp.argmax(probs, axis=-1)
        wgt = jnp.take_along_axis(probs, sel[..., None], axis=-1)[..., 0]
        xt = x.reshape(-1, Hs)
        sel_t = sel.reshape(-1)
        wgt_t = wgt.reshape(-1)
        out = jnp.zeros_like(xt)
        for e in range(n_experts):
            h = jax.nn.relu(xt @ w1[e] + b1[e])
            y = h @ w2[e] + b2[e]
            m = (sel_t == e).astype(xt.dtype) * wgt_t
            out = out + m[:, None] * y
        return out.reshape(Bs, Ss, Hs)

    def _L1_attn_ref(x, g1, Wq, Wkv, Wout, g2):
        import jax, jax.numpy as jnp
        import numpy as np
        DIM = 128
        HEADS = 16
        DIM_HEAD = 64
        SCALE = 16.0
        EPS = 1e-05

        def layernorm(x, g):
            mean = jnp.mean(x, axis=-1, keepdims=True)
            var = jnp.var(x, axis=-1, keepdims=True)
            return (x - mean) * jax.lax.rsqrt(var + EPS) * g

        def l2norm(t):
            return t / jnp.maximum(jnp.linalg.norm(t, axis=-1, keepdims=True), 1e-12)
        b, n, _ = x.shape
        xn = layernorm(x, g1)
        q = xn @ Wq.T
        kv = xn @ Wkv.T
        k, v = (kv[..., :DIM_HEAD], kv[..., DIM_HEAD:])
        q = q.reshape(b, n, HEADS, DIM_HEAD).transpose(0, 2, 1, 3)
        q = q * SCALE
        q, k = (l2norm(q), l2norm(k))
        srt = np.sqrt(SCALE).astype(np.float32)
        q, k = (q * srt, k * srt)
        sim = jnp.einsum('bhid,bjd->bhij', q, k)
        max_neg = -jnp.finfo(sim.dtype).max
        causal_mask = jnp.triu(jnp.ones((n, n), dtype=bool), 1)
        sim = jnp.where(causal_mask, max_neg, sim)
        attn = jax.nn.softmax(sim.astype(jnp.float32), axis=-1).astype(sim.dtype)
        out = jnp.einsum('bhij,bjd->bhid', attn, v)
        out = out.transpose(0, 2, 1, 3).reshape(b, n, HEADS * DIM_HEAD)
        out = out @ Wout.T
        return layernorm(out, g2)

    def _L1_ffn_ref(x, w_gate, w_up, w_down):
        import jax, jax.numpy as jnp
        import numpy as np
        DIM = 128
        HIDDEN = 384
        SCALE = 1.0 / 127.0

        def _dequant(w_int, dtype):
            return w_int.astype(dtype) * jnp.asarray(SCALE, dtype)
        wg = _dequant(w_gate, x.dtype)
        wu = _dequant(w_up, x.dtype)
        wd = _dequant(w_down, x.dtype)
        gate = jnp.einsum('bsd,hd->bsh', x, wg)
        up = jnp.einsum('bsd,hd->bsh', x, wu)
        h = jax.nn.silu(gate) * up
        return jnp.einsum('bsh,dh->bsd', h, wd)
    x = L0_attn_hidden_states
    xn = _layernorm(x, axis=-1)
    x = x + _L0_attn_ref(xn, L0_attn_wq, L0_attn_bq, L0_attn_wk, L0_attn_bk, L0_attn_wv, L0_attn_bv, L0_attn_wo, L0_attn_bo) + _L0_ffn_ref(xn, L0_ffn_w_router, L0_ffn_w1, L0_ffn_b1, L0_ffn_w2, L0_ffn_b2)
    xn = _layernorm(x, axis=-1)
    x = x + _L1_attn_ref(xn, L1_attn_g1, L1_attn_Wq, L1_attn_Wkv, L1_attn_Wout, L1_attn_g2) + _L1_ffn_ref(xn, L1_ffn_w_gate, L1_ffn_w_up, L1_ffn_w_down)
    return x

_drawn_inputs = setup_inputs


def setup_inputs(seed=0):
    import zlib

    import numpy as np

    out = dict(_drawn_inputs(seed))
    spreads = {'L0_ffn_b1': (0.0, 0.8),
     'L0_ffn_b2': (0.0, 0.332),
     'L1_attn_g1': (1.0, 0.6),
     'L1_attn_g2': (1.0, 0.6)}
    factors = {'L0_attn_wq': 8.0,
     'L0_attn_bq': 8.0,
     'L0_attn_wk': 8.0,
     'L0_attn_bk': 64.0,
     'L0_attn_wv': 8.0,
     'L0_attn_bv': 7.748,
     'L0_attn_wo': 7.518,
     'L0_ffn_w1': 3.726,
     'L0_ffn_w2': 2.932,
     'L1_attn_Wq': 64.0,
     'L1_attn_Wkv': 64.0,
     'L1_attn_Wout': 64.0,
     'L0_attn_bo': 3.538}
    for name, (base, spread) in spreads.items():
        noise = np.random.default_rng([zlib.crc32(name.encode()), seed]).standard_normal(out[name].shape)
        drawn = base * np.exp(spread * noise) if base else spread * noise
        out[name] = jnp.asarray(drawn.astype(out[name].dtype))
    for name, factor in factors.items():
        out[name] = (out[name] * factor).astype(out[name].dtype)
    return out
```

```python
from contextlib import ExitStack

import concourse.bass as bass
from concourse import mybir

ALU = mybir.AluOpType
ACT = mybir.ActivationFunctionType
AX = mybir.AxisListType
F32 = mybir.dt.float32
F32R = mybir.dt.float32r
BF16 = mybir.dt.bfloat16
I32 = mybir.dt.int32

P = 128
B = 8
T = 512
E = 128
NT = T // P
EPS = 1e-5
NEG = -1e30
LOWEST = -3e38

H0, D0 = 16, 8
HG = 4
G = H0 // HG
ROW_KLO, ROW_QLO, ROW_MAX = 8, 16, 24
QSCALE0 = D0 ** -0.5
BAND = [(0, 384, 0, 128), (0, 512, 0, 0), (0, 512, 1, 0), (128, 384, 1, 0)]
BAND_T = [(0, 384, 0), (0, 512, 384), (0, 512, 896), (128, 384, 1408)]
HALF0 = 896
PV_ORDER = (1, 2, 0, 3)

NE, F0 = 8, 512
FC = F0 // P
H1, D1 = 16, 64
NP = H1 // 2
QSCALE1, NORM_EPS, ROOT_SCALE = 16.0, 1e-12, 4.0
HID = 384
HC = HID // P
DEQUANT = 1.0 / 127.0
DR, AR = 3, 2

PER_A = dict(d_full=85, d_free=85, a_full=32, a_free=32, own=23, var=1, veps=1, rstd=1, xn=1, xcopied=1,
             k_ready=G, k_dma0=16 * HG, k_dma1=16 * HG, k_dma2=16 * HG, k_dma3=16 * HG, q_ready=G, lg=1, lge=1, gate=1, mcol=G, masked=32, pv=G, g_free=G)
PER_B = dict(d_full=10, d_free=10, a_full=16, a_free=32, gate=1)
PER_C = dict(d_full=23, d_free=23, a_full=39, a_free=39, own=24, var=3, veps=3, rstd=3, xn=1, xa=1,
             sums=5, lens=5, q_used=4, q_n=4, k_n=1, h1=3, masked=24, pv=8, g_free=1, fin=1, stored=16)
CREDITED = ("d_free", "a_free", "g_free", "q_used", "h1", "xcopied", "stored", "pv")


N_POOL, N_SETUP, N_LOADS = 41, 16, 41


class Signal:

    def __init__(self, ctx, nc, phase, name, per):
        self.name = f"{phase}_{name}"
        self.sem = ctx.enter_context(nc.semaphore(self.name))
        self.per, self.credit, self.n = per, int(name in CREDITED), 0

    def add(self, k):
        self.n += k
        return k

    def at(self, b, k):
        return b * self.per + (k + self.credit)


class Ring:

    def __init__(self, full, free, slots, reads=1):
        self.full, self.free, self.slots, self.reads = full, free, slots, reads
        self.number = {}

    def fillable(self, b, what):
        assert what not in self.number
        n = self.number[what] = len(self.number)
        return self.free.at(b, max(n - len(self.slots) + 1, 0) * self.reads)

    def slot(self, what):
        return self.slots[self.number[what] % len(self.slots)]

    def filled(self, b, what):
        return self.full.at(b, self.number[what] + 1)

    def emptied(self, b, what, before=0):
        return self.free.at(b, (self.number[what] + 1 - before) * self.reads)


def two_layers(nc, x, wq, bq, wk, bk, wv, bv, wo, bo, w_router, w1, b1, w2, b2,
               g1, wq1_t, wkv1_t, wout1_t, g2, w_gate_t, w_up_t, w_down_t, out):
    x_d = x.rearrange("b (i p) e -> p b i e", p=P)
    out_d = out.rearrange("b (i p) e -> b p i e", p=P)

    with ExitStack() as ctx:
        def sb(name, shape, dt=F32):
            return ctx.enter_context(nc.sbuf_tensor(name, shape, dt))

        def sem(name):
            return ctx.enter_context(nc.semaphore(name))

        banks_d = [ctx.enter_context(nc.psum_tensor(f"ring_d{n}", [P, T], F32)) for n in range(DR)]
        gather = ctx.enter_context(nc.psum_tensor("gather", [P, T], F32))
        banks_a = [ctx.enter_context(nc.psum_tensor(f"ring_a{n}", [P, 2 * T], F32)) for n in range(AR)]

        wq_rep, wk_rep = sb("wq_rep", [P, G, HG, 4, D0]), sb("wk_rep", [P, G, HG, 4, D0])
        wv_sb, wo_sb = sb("wv_sb", [P, E]), sb("wo_sb", [P, E])
        bq_col, bk_col, bk_in = sb("bq_col", [P, G]), sb("bk_col", [P, G]), sb("bk_in", [P, G])
        bv_all, bo_all, g2_all = sb("bv_all", [P, E]), sb("bo_all", [P, E]), sb("g2_all", [P, E])
        g1_col = sb("g1_col", [P, 1])
        router_sb = sb("router_sb", [P, NE])
        b1_sb = sb("b1_sb", [P, NE, FC])
        b2_sb = sb("b2_sb", [NE, E])
        wq1_sb = sb("wq1_sb", [P, H1 * D1])
        wkv1_sb = sb("wkv1_sb", [P, 2 * D1])
        wout1_sb = sb("wout1_sb", [P, NP, E])
        wffn = sb("wffn", [P, 3, HID])
        ident = sb("ident", [P, P])
        qlo_neg, klo_neg, ones_row = sb("qlo_neg", [P, 1]), sb("klo_neg", [P, 1]), sb("ones_row", [P, 1])
        rows4 = sb("rows4", [P, 3, HG])
        masks = sb("masks", [P, 2, T], BF16)
        rev_e = sb("rev_e", [P, NT, NE])
        pick_sum = sb("pick_sum", [P, HG, 32])
        spread = sb("spread", [P, NP, P])

        x_all = sb("x_all", [P, B, NT, E])
        xt_all = sb("xt_all", [P, B, T])
        gate_all = sb("gate_all", [P, B, NT, NE])

        xn, xn_t = sb("xn", [P, NT, E]), sb("xn_t", [P, T])
        stats, mv = sb("stats", [P, NT, 6]), sb("mv", [P, NT, 2])
        veps, rstd = sb("veps", [P, NT]), sb("rstd", [P, NT])
        exponents = sb("exponents", [P, NT + H1])
        full, hi = sb("full", [P, T]), sb("hi", [P, T], F32R)
        k_rows, q_rows = sb("k_rows", [P, G, T], F32R), sb("q_rows", [P, G, T], F32R)
        q_max = sb("q_max", [P, 2, T], F32R)
        rows = sb("rows", [P, H0, T], F32R)
        v_aug = sb("v_aug", [P, NT, H0, 32])
        dump = sb("dump", [P, 2, T], BF16)
        mx = sb("mx", [P, HG, NT])
        m_cols = sb("m_cols", [P, NT, HG, 32])
        arena = sb("arena", [P, 16384])
        o_raw, o_t = sb("o_raw", [P, T]), sb("o_t", [P, T])
        rden = sb("rden", [P, NT, HG])
        o_n, acc = sb("o_n", [P, NT, E]), sb("acc", [P, NT, E])
        lg, lge, lg2, hot = (sb(n, [P, NT, NE]) for n in ("lg", "lge", "lg2", "hot"))
        lmx, cmx, lsum, wgt = (sb(n, [P, NT]) for n in ("lmx", "cmx", "lsum", "wgt"))
        gate_m = sb("gate_m", [P, NT, NE])
        gate_t = o_raw[0:NE, :]
        xa_t = o_raw
        kf, kn = acc[:, :, 0:D1], acc[:, :, D1:2 * D1]
        ksum, klen = sb("ksum", [P, NT]), sb("klen", [P, NT])
        k_stack = k_rows[:, 0:2, :]
        q_sum, q_len, q_rn = sb("q_sum", [P, H1]), sb("q_len", [P, H1]), sb("q_rn", [P, H1])

        probs = arena[:, 0:8 * 2 * HALF0].rearrange("p (h n) -> p h n", h=8)
        w1_sb = arena[:, 0:4096].rearrange("p (e f) -> p e f", e=NE)
        w2_sb = arena[:, 4096:8192].rearrange("p (e c d) -> p e c d", e=NE, c=FC)
        hidden = arena[:, 8192:12288].rearrange("p (n c t) -> p n c t", n=2, c=FC)
        probs1 = arena[:, 0:5120].rearrange("p (n t) -> p n t", n=2)
        q_raw = arena[:, 5120:6144].rearrange("p (h d) -> p h d", h=H1)
        q_sq = arena[:, 6144:7168].rearrange("p (h d) -> p h d", h=H1)
        q_n = arena[:, 7168:8192].rearrange("p (h d) -> p h d", h=H1)
        q_nat = arena[:, 8192:10240].rearrange("p (h a d) -> p h a d", h=H1, a=2)
        o1 = arena[:, 5120:9216].rearrange("p (n t) -> p n t", n=NP)
        gu = arena[:, 10240:11776].rearrange("p (a t) -> p a t", a=3)
        h1 = arena[:, 11776:13312].rearrange("p (c t) -> p c t", c=HC)
        y1 = arena[:, 13312:13824].rearrange("p (i e) -> p i e", i=NT)
        fin = arena[:, 13824:14336].rearrange("p (i e) -> p i e", i=NT)
        xa = arena[:, 14336:14848].rearrange("p (i e) -> p i e", i=NT)
        rsum = arena[:, 14848:15360]
        k_nat = arena[:, 15360:16384].rearrange("p (a i r d) -> p a i r d", a=2, i=NT, r=2)
        wint = arena[:, 15360 - 1152:15360].bitcast(I32)
        nat = arena[:, 13000:13256].rearrange("p (a e) -> p a e", a=2)
        v1 = v_aug[:, 0:NT, 0:2, :].rearrange("p j a d -> p j (a d)")

        s_apart = [sem("apart_vector"), sem("apart_gpsimd")]
        s_win, s_w12 = sem("weights_in"), sem("experts_in")
        s_x, s_pool, s_set, s_phase = sem("x_in"), sem("pool_setup"), sem("dve_setup"), sem("phase_done")
        n_in, n_pool, n_set = [0], [0], [0]

        def signals(phase, per):
            s = {k: Signal(ctx, nc, phase, k, v) for k, v in per.items()}
            s["D"] = Ring(s["d_full"], s["d_free"], banks_d)
            s["A"] = Ring(s["a_full"], s["a_free"], banks_a, 2 if phase == "B" else 1)
            if phase == "A":
                s["k_dma"] = [s["k_dma0"], s["k_dma1"], s["k_dma2"], s["k_dma3"]]
            return s

        SA, SB, SC = signals("A", PER_A), signals("B", PER_B), signals("C", PER_C)

        def credit(eng, *names):
            for n in names:
                eng.sem_inc(n.sem, 1)

        def phase_end(eng, n):
            eng.drain().then_inc(s_phase, 1)
            eng.wait_ge(s_phase, 5 * n)

        def apart(eng):
            eng.sem_inc(s_apart[0 if eng is nc.vector else 1], 1)

        def tiles(slot):
            return slot[:, :].rearrange("p (i e) -> p i e", i=NT)

        block = ctx.enter_context(nc.Block())

        @block.tensor
        def _(pe):
            pe.wait_ge(s_pool, N_POOL)

            def mm(out, lhs, rhs, start=True, stop=True):
                return pe.matmul(out, lhs, rhs, start=start, stop=stop, skip_group_check=True)

            def turn(slot, tile_of, n=NT):
                return [pe.transpose(slot[:, i * P:(i + 1) * P], tile_of(i), ident[:]) for i in range(n)][-1]

            s = SA
            D, A = s["D"], s["A"]
            pe.wait_ge(s_set, N_SETUP)
            credit(pe, s["pv"])
            with pe.Fori(0, B) as b:
                pe.wait_ge(s["xn"].sem, s["xn"].at(b, 1))
                pe.wait_ge(D.free.sem, D.fillable(b, "xn.T"))
                sl = D.slot("xn.T")
                turn(sl, lambda i: xn[:, i, :]).then_inc(D.full.sem, D.full.add(1))
                pe.wait_ge(D.free.sem, D.emptied(b, "xn.T"))
                for g in range(G):
                    pe.wait_ge(D.free.sem, D.fillable(b, ("k", g)))
                    sl = D.slot(("k", g))
                    mm(sl[:], wk_rep[:, g].rearrange("p h c d -> p (h c d)"), xn_t[:]).then_inc(D.full.sem, D.full.add(1))
                for g in range(G):
                    pe.wait_ge(D.free.sem, D.fillable(b, ("q", g)))
                    sl = D.slot(("q", g))
                    mm(sl[:], wq_rep[:, g].rearrange("p h c d -> p (h c d)"), xn_t[:]).then_inc(D.full.sem, D.full.add(1))
                    if g == 0:
                        pe.wait_ge(D.free.sem, D.fillable(b, "v"))
                        sl = D.slot("v")
                        [mm(sl[:, i * P:(i + 1) * P], xn_t[:, i * P:(i + 1) * P], wv_sb[:])
                                                   for i in range(NT)][-1].then_inc(D.full.sem, D.full.add(1))
                pe.wait_ge(D.free.sem, D.fillable(b, "logits"))
                sl = D.slot("logits")
                [mm(sl[:, i * NE:(i + 1) * NE], xn_t[:, i * P:(i + 1) * P], router_sb[:])
                                                for i in range(NT)][-1].then_inc(D.full.sem, D.full.add(1))

                def score_rows(g, i):
                    first, many, _, _ = BAND[i]
                    for h in range(HG):
                        pe.wait_ge(D.free.sem, D.fillable(b, ("max", g, i, h)))
                        sl = D.slot(("max", g, i, h))
                        mm(
                            sl[:, 0:many], q_rows[:, g, i * P:(i + 1) * P], rows[:, HG * g + h, first:first + many]).then_inc(D.full.sem, D.full.add(1))

                def score_cols(g, h):
                    for half in range(2):
                        pe.wait_ge(A.free.sem, A.fillable(b, ("probs", HG * g + h, half)))
                        sl = A.slot(("probs", HG * g + h, half))
                        for j in (2 * half, 2 * half + 1):
                            first, many, at = BAND_T[j]
                            at += 128 if half == 0 else -HALF0
                            ins = mm(sl[:, at:at + many], rows[:, HG * g + h, j * P:(j + 1) * P],
                                     q_max[:, g % 2, first:first + many])
                        ins.then_inc(A.full.sem, A.full.add(1))

                def values(g, js):
                    if js[0] == PV_ORDER[0]:
                        pe.wait_ge(s["masked"].sem, s["masked"].at(b, 2 * HG * (g + 1)))
                        pe.wait_ge(s["g_free"].sem, s["g_free"].at(b, g))
                    for j in js:
                        first, many, at = BAND_T[j]
                        for h in range(HG):
                            ins = mm(gather[32 * h:32 * h + 32, first:first + many], v_aug[:, j, HG * g + h, :],
                                     probs[:, (HG * g + h) % 8, at:at + many],
                                     start=(j == PV_ORDER[0]), stop=(j == PV_ORDER[-1]))
                    if js[-1] == PV_ORDER[-1]:
                        ins.then_inc(s["pv"].sem, s["pv"].add(1))

                def turn_out(g):
                    pe.wait_ge(s["g_free"].sem, s["g_free"].at(b, g + 1))
                    pe.wait_ge(D.free.sem, D.fillable(b, ("o.T", g)))
                    sl = D.slot(("o.T", g))
                    turn(sl, lambda i: o_raw[:, i * P:(i + 1) * P]).then_inc(D.full.sem, D.full.add(1))

                pe.wait_ge(s["q_ready"].sem, s["q_ready"].at(b, 1))
                pe.wait_ge(s["k_dma"][0].sem, s["k_dma"][0].at(b, 16 * HG))
                for i in range(NT):
                    score_rows(0, i)
                for g in range(G):
                    pe.wait_ge(s["mcol"].sem, s["mcol"].at(b, g + 1))
                    pe.wait_ge(D.free.sem, D.fillable(b, ("q_max", g)))
                    sl = D.slot(("q_max", g))
                    turn(sl, lambda i: m_cols[:, i].rearrange("p h r -> p (h r)")).then_inc(D.full.sem, D.full.add(1))
                    if g + 1 < G:
                        pe.wait_ge(s["q_ready"].sem, s["q_ready"].at(b, g + 2))
                        pe.wait_ge(s["k_dma"][g + 1].sem, s["k_dma"][g + 1].at(b, 16 * HG))
                    for i in range(NT):
                        if g + 1 < G:
                            score_rows(g + 1, i)
                        if i == 0:
                            pe.wait_ge(D.free.sem, D.emptied(b, ("q_max", g)))
                        score_cols(g, i)
                        if g and i < 2:
                            values(g - 1, PV_ORDER[2 * i:2 * i + 2])
                    if g:
                        turn_out(g - 1)
                values(G - 1, PV_ORDER)
                turn_out(G - 1)
                pe.wait_ge(D.free.sem, D.emptied(b, ("o.T", G - 1)))
                pe.wait_ge(D.free.sem, D.fillable(b, "heads.T"))
                sl = D.slot("heads.T")
                turn(sl, lambda i: o_n[:, i, :]).then_inc(D.full.sem, D.full.add(1))
                pe.wait_ge(D.free.sem, D.emptied(b, "heads.T"))
                pe.wait_ge(D.free.sem, D.fillable(b, "attended"))
                sl = D.slot("attended")
                [mm(sl[:, i * P:(i + 1) * P], o_t[:, i * P:(i + 1) * P], wo_sb[:])
                                                  for i in range(NT)][-1].then_inc(D.full.sem, D.full.add(1))
            phase_end(pe, 1)

            s = SB
            D, A = s["D"], s["A"]
            pe.wait_ge(s_w12, 32)
            with pe.Fori(0, B) as b:
                pe.wait_ge(s["gate"].sem, s["gate"].at(b, 1))
                pe.wait_ge(D.free.sem, D.fillable(b, "gate.T"))
                sl = D.slot("gate.T")
                [
                    pe.transpose(sl[0:NE, i * P:(i + 1) * P], gate_m[:, i, :], ident[:])
                    for i in range(NT)][-1].then_inc(D.full.sem, D.full.add(1))
                pe.wait_ge(D.free.sem, D.emptied(b, "gate.T"))
                pe.wait_ge(D.free.sem, D.fillable(b, "b2"))
                sl = D.slot("b2")
                [mm(sl[:, i * P:(i + 1) * P], gate_t[:, i * P:(i + 1) * P], b2_sb[:])
                                            for i in range(NT)][-1].then_inc(D.full.sem, D.full.add(1))

                def up(e, half):
                    pe.wait_ge(A.free.sem, A.fillable(b, ("h", e, half)))
                    sl = A.slot(("h", e, half))
                    for c in (0, 1):
                        ins = mm(sl[:, c * T:(c + 1) * T],
                                 w1_sb[:, e, :].rearrange("p (f c) -> p c f", c=FC)[:, 2 * half + c],
                                 xt_all[:, bass.ds(b, 1), :].rearrange("p o t -> p (o t)"))
                    ins.then_inc(A.full.sem, A.full.add(1))

                def down(e):
                    pe.wait_ge(A.free.sem, A.emptied(b, ("h", e, 1)))
                    pe.wait_ge(D.free.sem, D.fillable(b, ("y", e)))
                    sl = D.slot(("y", e))
                    for i in range(NT):
                        for c in range(FC):
                            ins = mm(sl[:, i * P:(i + 1) * P], hidden[:, e % 2, c, i * P:(i + 1) * P], w2_sb[:, e, c, :],
                                     start=(c == 0), stop=(c == FC - 1))
                    ins.then_inc(D.full.sem, D.full.add(1))

                for e in range(NE):
                    up(e, 0)
                    up(e, 1)
                    if e:
                        down(e - 1)
                down(NE - 1)
            phase_end(pe, 2)

            s = SC
            D, A = s["D"], s["A"]
            credit(pe, s["pv"])
            with pe.Fori(0, B) as b:
                pe.wait_ge(s["xn"].sem, s["xn"].at(b, 1))
                pe.wait_ge(D.free.sem, D.fillable(b, "xn.T"))
                sl = D.slot("xn.T")
                turn(sl, lambda i: xn[:, i, :]).then_inc(D.full.sem, D.full.add(1))
                pe.wait_ge(s["xa"].sem, s["xa"].at(b, 1))
                pe.wait_ge(D.free.sem, D.fillable(b, "xa.T"))
                sl = D.slot("xa.T")
                turn(sl, lambda i: xa[:, i, :]).then_inc(D.full.sem, D.full.add(1))
                pe.wait_ge(D.free.sem, D.emptied(b, "xa.T"))
                pe.wait_ge(D.free.sem, D.fillable(b, "k|v"))
                sl = D.slot("k|v")
                [mm(sl[:, i * P:(i + 1) * P], xa_t[:, i * P:(i + 1) * P], wkv1_sb[:])
                                             for i in range(NT)][-1].then_inc(D.full.sem, D.full.add(1))

                def q_rows1(i):
                    pe.wait_ge(A.free.sem, A.fillable(b, ("q", i)))
                    sl = A.slot(("q", i))
                    [mm(sl[:, n * T:(n + 1) * T], xa_t[:, i * P:(i + 1) * P],
                                                       wq1_sb[:, n * T:(n + 1) * T]) for n in range(2)][-1].then_inc(A.full.sem, A.full.add(1))

                def gate_up(c):
                    pe.wait_ge(A.free.sem, A.fillable(b, ("gu", c)))
                    sl = A.slot(("gu", c))
                    [mm(sl[:, n * T:(n + 1) * T], wffn[:, n, c * P:(c + 1) * P], xn_t[:])
                                                     for n in range(2)][-1].then_inc(A.full.sem, A.full.add(1))

                def turn_q(i):
                    pe.wait_ge(s["q_n"].sem, s["q_n"].at(b, i + 1))
                    for n in range(2):
                        pe.wait_ge(A.free.sem, A.fillable(b, ("q.T", i, n)))
                        sl = A.slot(("q.T", i, n))
                        turn(
                            sl, lambda h: q_nat[:, 8 * n + h].rearrange("p a d -> p (a d)"), 8).then_inc(A.full.sem, A.full.add(1))

                q_rows1(0)
                gate_up(0)
                for i in range(NT):
                    if i + 1 < NT:
                        q_rows1(i + 1)
                    if 0 < i < HC:
                        gate_up(i)
                    turn_q(i)
                pe.wait_ge(s["k_n"].sem, s["k_n"].at(b, 1))
                for a in range(2):
                    pe.wait_ge(D.free.sem, D.fillable(b, ("k.T", a)))
                    sl = D.slot(("k.T", a))
                    turn(sl, lambda i: k_nat[:, a, i].rearrange("p r d -> p (r d)")).then_inc(D.full.sem, D.full.add(1))
                pe.wait_ge(s["h1"].sem, s["h1"].at(b, HC))
                pe.wait_ge(D.free.sem, D.fillable(b, "ffn"))
                sl = D.slot("ffn")
                [mm(sl[:, i * P:(i + 1) * P], h1[:, c, i * P:(i + 1) * P],
                                                wffn[:, 2, c * P:(c + 1) * P], start=(c == 0), stop=(c == HC - 1))
                                             for i in range(NT) for c in range(HC)][-1].then_inc(D.full.sem, D.full.add(1))

                def stacked(out, j, q):
                    mm(out, k_stack[:, 0, j * P:(j + 1) * P], q, stop=False)
                    return mm(out, k_stack[:, 1, j * P:(j + 1) * P], q, start=False)

                def scores(n):
                    for c in range(2):
                        pe.wait_ge(A.free.sem, A.fillable(b, ("probs", n, c)))
                        sl = A.slot(("probs", n, c))
                        stacked(sl[:, 0:512], 0, rows[:, 2 * n + c, :])
                        stacked(sl[:, 512:896], 1, rows[:, 2 * n + c, 128:512]).then_inc(A.full.sem, A.full.add(1))
                    pe.wait_ge(A.free.sem, A.fillable(b, ("probs", n, 2)))
                    sl = A.slot(("probs", n, 2))
                    stacked(sl[:, 0:512], 2, rows[:, 2 * n:2 * n + 2, 256:512])
                    stacked(sl[:, 512:768], 3, rows[:, 2 * n:2 * n + 2, 384:512]).then_inc(A.full.sem, A.full.add(1))

                def p_of(n, c, j):
                    at = ((c * 896, 512), (c * 896 + 512, 384), (1792 + c * 256, 256), (2304 + c * 128, 128))[j]
                    return probs1[:, n % 2, at[0]:at[0] + at[1]]

                def values1(n):
                    pe.wait_ge(s["masked"].sem, s["masked"].at(b, 3 * (n + 1)))
                    if n == 0:
                        pe.wait_ge(s["g_free"].sem, s["g_free"].at(b, 0))
                    pe.wait_ge(D.free.sem, D.fillable(b, ("o", n)))
                    sl = D.slot(("o", n))
                    [
                        mm(sl[D1 * c:D1 * c + D1, j * P:T], v1[:, j, :], p_of(n, c, j), start=(j == 0), stop=(j == NT - 1))
                        for j in range(NT) for c in range(2)][-1].then_inc(D.full.sem, D.full.add(1))
                    for j in range(NT):
                        for c in range(2):
                            h = 2 * n + c
                            ins = mm(gather[32 * (h % 4):32 * (h % 4) + 32, j * P:T], pick_sum[:, h // 4, :],
                                     p_of(n, c, j), start=(h < 4 and j == 0), stop=(n == NP - 1 and j == NT - 1))
                    ins.then_inc(s["pv"].sem, s["pv"].add(1))

                pe.wait_ge(D.free.sem, D.emptied(b, ("k.T", 1)))
                pe.wait_ge(A.free.sem, A.emptied(b, ("q.T", NT - 1, 1)))
                for n in range(NP + 1):
                    if n < NP:
                        scores(n)
                    if n:
                        values1(n - 1)
                pe.wait_ge(s["g_free"].sem, s["g_free"].at(b, 1))
                for n in range(NP):
                    pe.wait_ge(D.free.sem, D.fillable(b, ("1/sum", n)))
                    sl = D.slot(("1/sum", n))
                    mm(sl[:], spread[:, n, :], rsum).then_inc(D.full.sem, D.full.add(1))
                pe.wait_ge(D.free.sem, D.emptied(b, ("1/sum", NP - 1)))
                pe.wait_ge(D.free.sem, D.fillable(b, "attended"))
                sl = D.slot("attended")
                [
                    mm(sl[:, i * P:(i + 1) * P], o1[:, n, i * P:(i + 1) * P], wout1_sb[:, n, :],
                       start=(n == 0), stop=(n == NP - 1)) for i in range(NT) for n in range(NP)][-1].then_inc(D.full.sem, D.full.add(1))

        @block.sync
        def _(sp):
            def load(dst, src):
                sp.dma_start(dst, src, allow_slow_non_contiguous=True).then_inc(s_win, 16)
                n_in[0] += 16

            sp.dma_start(x_all[:, 0], x_d[:, 0]).then_inc(s_x, 16)
            load(nat[:, 0, :], wk)
            load(nat[:, 1, :], wq)
            sp.wait_ge(s_set, 4)
            for h in range(HG):
                for c in range(3):
                    r = 32 * h + D0 * c
                    load(bq_col[r:r + D0, :], bq.rearrange("(g h d) -> h d g", g=G, h=HG)[h])
                    load(bk_in[r:r + D0, :], bk.rearrange("(g h d) -> h d g", g=G, h=HG)[h])
            load(wv_sb[:], wv)
            load(wo_sb[:], wo)
            load(router_sb[:], w_router)
            for t, v in ((bv_all, bv), (bo_all, bo), (g2_all, g2)):
                load(t[:], v.rearrange("(a e) -> a e", a=1).to_broadcast([P, E]))
            load(g1_col[:], g1.rearrange("(e a) -> e a", a=1))
            for n, w in enumerate((w_gate_t, w_up_t)):
                load(wint[:, n * HID:(n + 1) * HID], w)
            load(wint[:, 2 * HID:3 * HID].rearrange("p (c e) -> p c e", c=HC), w_down_t.rearrange("(c p) e -> p c e", p=P))
            for n in range(1, B):
                sp.dma_start(x_all[:, n], x_d[:, n]).then_inc(s_x, 16)
            load(b1_sb[:], b1.rearrange("e (f c) -> f e c", c=FC))
            load(b2_sb[:], b2)
            load(wq1_sb[:], wq1_t)
            load(wkv1_sb[:], wkv1_t)
            load(wout1_sb[:], wout1_t.rearrange("(n p) e -> p n e", p=P))

            sp.wait_ge(s_pool, N_POOL)
            s = SA
            with sp.Fori(0, B) as b:
                sp.wait_ge(s["pv"].sem, s["pv"].at(b, 0))
                for g in range(G):
                    sp.wait_ge(s["k_ready"].sem, s["k_ready"].at(b, g + 1))
                    for h in range(HG):
                        sp.dma_start(rows[32 * h:32 * h + 32, HG * g + h, :].bitcast(F32),
                                                     k_rows[32 * h:32 * h + 32, g, :].bitcast(F32)).then_inc(s["k_dma"][g].sem, s["k_dma"][g].add(16))
            phase_end(sp, 1)
            sp.dma_start(w1_sb, w1.rearrange("e d f -> d e f")).then_inc(s_w12, 16)
            sp.dma_start(w2_sb, w2.rearrange("e (f c) d -> f e c d", c=FC)).then_inc(s_w12, 16)
            sp.wait_ge(s_w12, 32)
            phase_end(sp, 2)
            s = SC
            credit(sp, s["stored"])
            with sp.Fori(0, B) as b:
                sp.wait_ge(s["fin"].sem, s["fin"].at(b, 1))
                sp.dma_start(out_d[bass.ds(b, 1)].rearrange("o p i e -> (o p) i e"), fin).then_inc(s["stored"].sem, s["stored"].add(16))
            sp.wait_ge(s["stored"].sem, 16 * B + 1)

        @block.gpsimd
        def _(pool):
            def step(ins):
                ins.then_inc(s_pool, 1)
                n_pool[0] += 1
                pool.wait_ge(s_pool, n_pool[0])

            def keep(v, op, fill, base, pattern, mult):
                step(pool.affine_select(out=v, in_=v, compare_op=op, fill=fill, base=base, pattern=pattern,
                                        channel_multiplier=mult))

            for n, (row, many, val) in enumerate(((ROW_QLO, D0, -1.0), (ROW_KLO, D0, -1.0), (ROW_MAX, 2, 1.0))):
                step(pool.memset(rows4[:, n, :], val))
                keep(rows4[:, n, :], ALU.is_ge, 0.0, -row, [[-32, HG]], 1)
                keep(rows4[:, n, :], ALU.is_ge, 0.0, row + many - 1, [[32, HG]], -1)
            step(pool.memset(exponents[:, 0:NT], -0.5))
            step(pool.memset(exponents[:, NT:NT + H1], 0.5))
            step(pool.memset(ident[:], 0.0))
            keep(ident[:], ALU.not_equal, 1.0, 0, [[-1, P]], 1)
            step(pool.memset(rows[:].bitcast(F32), 0.0))
            step(pool.memset(masks[:], 0.0))
            keep(masks[:, 0, 384:512], ALU.is_ge, NEG, 0, [[-1, P]], 1)
            keep(masks[:, 1, 0:128], ALU.is_ge, NEG, 0, [[1, P]], -1)
            step(pool.iota(rev_e[:], pattern=[[0, NT], [-1, NE]], base=NE, channel_multiplier=0,
                           allow_small_or_imprecise_dtypes=True))
            step(pool.memset(m_cols[:], 0.0))
            step(pool.memset(v_aug[:], 0.0))
            step(pool.memset(v_aug[:, :, :, D0:D0 + 1], 1.0))
            step(pool.memset(pick_sum[:], 1.0))
            step(pool.memset(pick_sum[:, :, 0:HG], 0.0))
            keep(pick_sum[:, :, 0:HG], ALU.not_equal, 1.0, 0, [[1, HG], [-1, HG]], 0)
            step(pool.memset(spread[:], 0.0))
            for n in range(NP):
                for c in range(2):
                    h = 2 * n + c
                    keep(spread[:, n, D1 * c:D1 * c + D1], ALU.not_equal, 1.0, -(32 * (h % 4) + h // 4), [[0, D1]], 1)

            def root(s, k, b):
                pool.wait_ge(s["var"].sem, s["var"].at(b, k))
                apart(pool)
                pool.tensor_scalar(veps[:], mv[:, :, 1], EPS, None, ALU.add).then_inc(s["veps"].sem, s["veps"].add(1))
                pool.wait_ge(s["veps"].sem, s["veps"].at(b, k))
                pool.tensor_tensor(rstd[:], veps[:], exponents[:, 0:NT], ALU.pow).then_inc(s["rstd"].sem, s["rstd"].add(1))

            s = SA
            credit(pool, s["xcopied"])
            with pool.Fori(0, B) as b:
                root(s, 1, b)
                pool.wait_ge(s["D"].free.sem, s["D"].emptied(b, "xn.T"))
                pool.tensor_copy(xt_all[:, bass.ds(b, 1), :].rearrange("p o t -> p (o t)"), xn_t[:]).then_inc(s["xcopied"].sem, s["xcopied"].add(1))
                for h in range(H0):
                    for half in range(2):
                        pool.wait_ge(s["A"].free.sem, s["A"].emptied(b, ("probs", h, half)))
                        apart(pool)
                        at = 256 if half == 0 else HALF0
                        v = arena[:, (h % 8) * 2 * HALF0 + at:(h % 8) * 2 * HALF0 + at + 1024] \
                            .rearrange("p (j t) -> p j t", j=2)[:, :, 0:P]
                        pool.affine_select(
                            out=v, in_=v, compare_op=ALU.is_ge, fill=0.0, base=0,
                            pattern=[[0, 2], [-1 if half == 0 else 1, P]], channel_multiplier=1 if half == 0 else -1).then_inc(s["masked"].sem, s["masked"].add(1))
            phase_end(pool, 1)
            phase_end(pool, 2)
            s = SC
            with pool.Fori(0, B) as b:
                root(s, 1, b)
                root(s, 2, b)
                pool.wait_ge(s["sums"].sem, s["sums"].at(b, 1))
                pool.tensor_tensor(klen[:], ksum[:], exponents[:, NT:2 * NT], ALU.pow).then_inc(s["lens"].sem, s["lens"].add(1))
                for i in range(NT):
                    pool.wait_ge(s["sums"].sem, s["sums"].at(b, 2 + i))
                    pool.tensor_tensor(q_len[:], q_sum[:], exponents[:, NT:NT + H1], ALU.pow).then_inc(s["lens"].sem, s["lens"].add(1))
                for n in range(NP):
                    at = (n % 2) * 2560
                    for third, spans in enumerate((((0, 512),), ((896, 512),), ((1792, 256), (2304, 128)))):
                        pool.wait_ge(s["A"].free.sem, s["A"].emptied(b, ("probs", n, third)))
                        apart(pool)
                        for lo, gap in spans:
                            v = arena[:, at + lo:at + lo + 2 * gap].rearrange("p (j t) -> p j t", j=2)[:, :, 0:P]
                            ins = pool.affine_select(out=v, in_=v, compare_op=ALU.is_ge, fill=0.0, base=0,
                                                     pattern=[[0, 2], [1, P]], channel_multiplier=-1)
                        ins.then_inc(s["masked"].sem, s["masked"].add(1))
                root(s, 3, b)

        @block.scalar
        def _(act):
            s = SA
            A = s["A"]
            credit(act, s["a_free"])
            with act.Fori(0, B) as b:
                act.wait_ge(s["lg"].sem, s["lg"].at(b, 1))
                act.activation(lge[:], lg[:], ACT.Exp).then_inc(s["lge"].sem, s["lge"].add(1))
                for h in range(H0):
                    for half in range(2):
                        act.wait_ge(A.full.sem, A.filled(b, ("probs", h, half)))
                        sl = A.slot(("probs", h, half))
                        if half == 0:
                            act.wait_ge(s["pv"].sem, s["pv"].at(b, max(h // HG - 1, 0)))
                        act.activation(probs[:, h % 8, half * HALF0:(half + 1) * HALF0],
                                                   sl[:, 128:1024] if half == 0 else sl[:, 0:HALF0], ACT.Exp).then_inc(A.free.sem, A.free.add(1))
            phase_end(act, 1)

            s = SB
            A = s["A"]
            credit(act, s["a_free"])
            with act.Fori(0, B) as b:
                for e in range(NE):
                    for half in range(2):
                        act.wait_ge(A.full.sem, A.filled(b, ("h", e, half)))
                        sl = A.slot(("h", e, half))
                        if half == 0 and e > 1:
                            act.wait_ge(s["D"].full.sem, s["D"].full.at(b, s["D"].number["y", e - 2] + 1))
                        for c in (0, 1):
                            act.activation(hidden[:, e % 2, 2 * half + c, :], sl[:, c * T:(c + 1) * T],
                                                       ACT.Relu, bias=b1_sb[:, e, 2 * half + c:2 * half + c + 1]).then_inc(A.free.sem, A.free.add(1))
            phase_end(act, 2)

            s = SC
            A = s["A"]
            credit(act, s["a_free"])
            with act.Fori(0, B) as b:
                def q_copy(i):
                    act.wait_ge(A.full.sem, A.filled(b, ("q", i)))
                    sl = A.slot(("q", i))
                    act.wait_ge(s["q_used"].sem, s["q_used"].at(b, i))
                    act.activation(q_raw, sl[:], ACT.Copy)
                    act.activation(q_sq, sl[:], ACT.Square).then_inc(A.free.sem, A.free.add(1))

                def gate_up(c):
                    act.wait_ge(A.full.sem, A.filled(b, ("gu", c)))
                    sl = A.slot(("gu", c))
                    act.wait_ge(s["h1"].sem, s["h1"].at(b, c))
                    act.activation(gu[:, 0, :], sl[:, 0:T], ACT.Tanh, scale=0.5)
                    act.activation(gu[:, 1:3, :], sl[:], ACT.Copy).then_inc(A.free.sem, A.free.add(1))

                q_copy(0)
                gate_up(0)
                for i in range(NT):
                    if i + 1 < NT:
                        q_copy(i + 1)
                    if 0 < i < HC:
                        gate_up(i)
                    for n in range(2):
                        act.wait_ge(A.full.sem, A.filled(b, ("q.T", i, n)))
                        sl = A.slot(("q.T", i, n))
                        act.activation(rows[:, 8 * n:8 * n + 8, i * P:(i + 1) * P],
                                                   sl[:].rearrange("p (h t) -> p h t", h=8), ACT.Copy).then_inc(A.free.sem, A.free.add(1))
                for n in range(NP):
                    for third, (lo, hi_, width) in enumerate(((0, 896, 896), (896, 1792, 896), (1792, 2560, 768))):
                        act.wait_ge(A.full.sem, A.filled(b, ("probs", n, third)))
                        sl = A.slot(("probs", n, third))
                        if third == 0:
                            act.wait_ge(s["pv"].sem, s["pv"].at(b, max(n - 1, 0)))
                        act.activation(probs1[:, n % 2, lo:hi_], sl[:, 0:width], ACT.Exp).then_inc(A.free.sem, A.free.add(1))

        @block.vector
        def _(dve):
            def setup(ins):
                ins.then_inc(s_set, 1)
                n_set[0] += 1

            setup(dve.memset(wq_rep[:], 0.0))
            setup(dve.memset(wk_rep[:], 0.0))
            setup(dve.memset(bq_col[:], 0.0))
            setup(dve.memset(bk_in[:], 0.0))
            dve.wait_ge(s_win, 16 * N_LOADS)
            dve.wait_ge(s_set, 4)
            for n, w in ((0, wk_rep), (1, wq_rep)):
                for c in range(3):
                    setup(dve.tensor_copy(w[:, :, :, c, :], nat[:, n, :].rearrange("p (g h d) -> p g h d", g=G, h=HG)))
            dve.wait_ge(s_pool, 9)
            setup(dve.reduce_sum(qlo_neg[:], rows4[:, 0, :], AX.X))
            setup(dve.reduce_sum(klo_neg[:], rows4[:, 1, :], AX.X))
            setup(dve.reduce_sum(ones_row[:], rows4[:, 2, :], AX.X))
            dve.wait_ge(s_set, n_set[0])
            setup(dve.tensor_scalar(bk_col[:], bk_in[:], ones_row[:, 0:1], None, ALU.add))
            setup(dve.tensor_copy(wffn[:].rearrange("p a f -> p (a f)"), wint))
            dve.wait_ge(s_set, n_set[0])
            setup(dve.tensor_scalar(wffn[:].rearrange("p a f -> p (a f)"), wffn[:].rearrange("p a f -> p (a f)"), DEQUANT,
                                    None, ALU.mult))
            dve.wait_ge(s_set, n_set[0])
            dve.wait_ge(s_x, 16 * B)
            dve.wait_ge(s_pool, N_POOL)

            def normalise(s, k, src, dst, b):
                for i in range(NT):
                    ins = dve.bn_stats(stats[:, i, :], src(i))
                ins.then_inc(s["own"].sem, s["own"].add(1))
                dve.wait_ge(s["own"].sem, s["own"].at(b, s["own"].n))
                apart(dve)
                for i in range(NT):
                    ins = dve.bn_aggr(mv[:, i, :], stats[:, i, :])
                ins.then_inc(s["var"].sem, s["var"].add(1))
                dve.wait_ge(s["rstd"].sem, s["rstd"].at(b, k))
                dve.wait_ge(s["var"].sem, s["var"].at(b, k))
                for i in range(NT):
                    ins = dve.tensor_scalar(dst[:, i, :], src(i), mv[:, i, 0:1], rstd[:, i:i + 1], ALU.subtract, ALU.mult)
                return ins

            s = SA
            D = s["D"]
            credit(dve, s["d_free"], s["g_free"])
            with dve.Fori(0, B) as b:
                x_b = x_all[:, bass.ds(b, 1)].rearrange("p o i e -> p (o i) e")
                normalise(s, 1, lambda i: x_b[:, i, :], xn, b).then_inc(s["xn"].sem, s["xn"].add(1))
                dve.wait_ge(D.full.sem, D.filled(b, "xn.T"))
                sl = D.slot("xn.T")
                dve.wait_ge(s["xcopied"].sem, s["xcopied"].at(b, 0))
                dve.tensor_copy(xn_t[:], sl[:]).then_inc(D.free.sem, D.free.add(1))

                def split(which, g, col, scale, neg, dst, ready):
                    dve.wait_ge(D.full.sem, D.filled(b, (which, g)))
                    sl = D.slot((which, g))
                    if g:
                        dve.wait_ge(ready.sem, ready.at(b, g))
                    elif which == "q":
                        dve.wait_ge(s["k_ready"].sem, s["k_ready"].at(b, G))
                    ins = dve.tensor_scalar(full[:], sl[:], col[:, g:g + 1], scale, ALU.add, ALU.mult)
                    ins.then_inc(D.free.sem, D.free.add(1))
                    dve.wait_ge(D.free.sem, D.emptied(b, (which, g)))
                    dve.tensor_copy(hi[:], full[:]).then_inc(s["own"].sem, s["own"].add(1))
                    dve.wait_ge(s["own"].sem, s["own"].at(b, s["own"].n))
                    dve.scalar_tensor_tensor(out=dst[:, g, :], in0=hi[:].bitcast(F32), scalar=neg[:, 0:1],
                                                        in1=full[:], op0=ALU.mult, op1=ALU.add).then_inc(ready.sem, ready.add(1))

                for g in range(G):
                    split("k", g, bk_col, 1.0, klo_neg, k_rows, s["k_ready"])
                for g in range(G):
                    split("q", g, bq_col, QSCALE0, qlo_neg, q_rows, s["q_ready"])
                    if g == 0:
                        dve.wait_ge(D.full.sem, D.filled(b, "v"))
                        sl = D.slot("v")
                        dve.tensor_tensor(
                            v_aug[:, :, :, 0:D0], sl[:].rearrange("p (i h d) -> p i h d", i=NT, h=H0),
                            bv_all[:].rearrange("p (o h d) -> p o h d", o=1, h=H0).to_broadcast([P, NT, H0, D0]), ALU.add).then_inc(D.free.sem, D.free.add(1))
                dve.wait_ge(D.full.sem, D.filled(b, "logits"))
                sl = D.slot("logits")
                lv = sl[:, 0:NT * NE].rearrange("p (i e) -> p i e", i=NT)
                dve.reduce_max(lmx[:], lv, AX.X).then_inc(s["own"].sem, s["own"].add(1))
                dve.wait_ge(s["own"].sem, s["own"].at(b, s["own"].n))
                ins = dve.tensor_tensor(lg[:], lv, lmx[:].unsqueeze(2).to_broadcast([P, NT, NE]), ALU.subtract)
                ins.then_inc(D.free.sem, D.free.add(1))
                dve.wait_ge(D.free.sem, D.emptied(b, "logits"))
                dve.scalar_tensor_tensor(out=lg2[:], in0=lg[:], scalar=0.0, in1=rev_e[:], op0=ALU.is_ge, op1=ALU.mult).then_inc(s["own"].sem, s["own"].add(1))
                dve.wait_ge(s["own"].sem, s["own"].at(b, s["own"].n))
                dve.reduce_max(cmx[:], lg2[:], AX.X).then_inc(s["lg"].sem, s["lg"].add(1))
                dve.wait_ge(s["lg"].sem, s["lg"].at(b, 1))
                dve.tensor_tensor(hot[:], lg2[:], cmx[:].unsqueeze(2).to_broadcast([P, NT, NE]), ALU.is_equal).then_inc(s["own"].sem, s["own"].add(1))
                dve.wait_ge(s["own"].sem, s["own"].at(b, s["own"].n))
                dve.wait_ge(s["lge"].sem, s["lge"].at(b, 1))
                dve.reduce_sum(lsum[:], lge[:], AX.X).then_inc(s["own"].sem, s["own"].add(1))
                dve.wait_ge(s["own"].sem, s["own"].at(b, s["own"].n))
                dve.reciprocal(wgt[:], lsum[:]).then_inc(s["own"].sem, s["own"].add(1))
                dve.wait_ge(s["own"].sem, s["own"].at(b, s["own"].n))
                dve.tensor_tensor(gate_all[:, bass.ds(b, 1)].rearrange("p o i e -> p (o i) e"), hot[:],
                                                 wgt[:].unsqueeze(2).to_broadcast([P, NT, NE]), ALU.mult).then_inc(s["gate"].sem, s["gate"].add(1))
                dve.wait_ge(s["gate"].sem, s["gate"].at(b, 1))

                def maxima(g, i):
                    first, many, m, at = BAND[i]
                    for h in range(HG):
                        dve.wait_ge(D.full.sem, D.filled(b, ("max", g, i, h)))
                        sl = D.slot(("max", g, i, h))
                        dve.wait_ge(D.free.sem, D.emptied(b, ("max", g, i, h), 2))
                        apart(dve)
                        dve.tensor_tensor_reduce(dump[:, h % 2, 0:many], sl[:, 0:many], masks[:, m, at:at + many], 1.0,
                                                             LOWEST, ALU.add, ALU.max, mx[:, h, i:i + 1]).then_inc(D.free.sem, D.free.add(1))

                def max_parts(g):
                    dve.wait_ge(D.free.sem, D.emptied(b, ("max", g, NT - 1, HG - 1)))
                    m_hi, m_lo = (m_cols[:, :, :, ROW_MAX + r].rearrange("p i h -> p h i") for r in (0, 1))
                    dve.tensor_scalar(m_hi.bitcast(F32R), mx[:], -1.0, None, ALU.mult).then_inc(s["own"].sem, s["own"].add(1))
                    dve.wait_ge(s["own"].sem, s["own"].at(b, s["own"].n))
                    dve.scalar_tensor_tensor(out=m_lo, in0=mx[:], scalar=-1.0, in1=m_hi, op0=ALU.mult,
                                                            op1=ALU.subtract).then_inc(s["mcol"].sem, s["mcol"].add(1))

                def out_rows(g):
                    dve.wait_ge(s["pv"].sem, s["pv"].at(b, g + 1))
                    dve.tensor_copy(o_raw[:], gather[:]).then_inc(s["g_free"].sem, s["g_free"].add(1))

                def divide(g):
                    dve.wait_ge(D.full.sem, D.filled(b, ("o.T", g)))
                    sl = D.slot(("o.T", g))
                    v = sl[:].rearrange("p (i h r) -> p i h r", i=NT, h=HG)
                    if g:
                        dve.wait_ge(D.free.sem, D.emptied(b, ("o.T", g - 1)))
                    dve.reciprocal(rden[:], v[:, :, :, D0]).then_inc(s["own"].sem, s["own"].add(1))
                    dve.wait_ge(s["own"].sem, s["own"].at(b, s["own"].n))
                    dve.tensor_tensor(
                        o_n[:, :, g * HG * D0:(g + 1) * HG * D0].rearrange("p i (h d) -> p i h d", h=HG),
                        v[:, :, :, 0:D0], rden[:].unsqueeze(3).to_broadcast([P, NT, HG, D0]), ALU.mult).then_inc(D.free.sem, D.free.add(1))

                for i in range(NT):
                    maxima(0, i)
                for g in range(G):
                    max_parts(g)
                    dve.wait_ge(D.full.sem, D.filled(b, ("q_max", g)))
                    sl = D.slot(("q_max", g))
                    if g >= 2:
                        dve.wait_ge(s["A"].full.sem, s["A"].full.at(b, 2 * HG * (g - 1)))
                    dve.wait_ge(s["q_ready"].sem, s["q_ready"].at(b, g + 1))
                    dve.tensor_tensor(q_max[:, g % 2, :], sl[:], q_rows[:, g, :].bitcast(F32), ALU.add).then_inc(D.free.sem, D.free.add(1))
                    for i in range(NT):
                        if g + 1 < G:
                            maxima(g + 1, i)
                        if g and i == 2:
                            out_rows(g - 1)
                    if g:
                        divide(g - 1)
                out_rows(G - 1)
                divide(G - 1)
                dve.wait_ge(D.full.sem, D.filled(b, "heads.T"))
                sl = D.slot("heads.T")
                dve.tensor_copy(o_t[:], sl[:]).then_inc(D.free.sem, D.free.add(1))
                dve.wait_ge(D.full.sem, D.filled(b, "attended"))
                sl = D.slot("attended")
                ins = dve.tensor_tensor(acc[:], tiles(sl), bo_all[:].unsqueeze(1).to_broadcast([P, NT, E]), ALU.add)
                ins.then_inc(D.free.sem, D.free.add(1))
                dve.wait_ge(D.free.sem, D.emptied(b, "attended"))
                dve.tensor_tensor(x_b, x_b, acc[:], ALU.add).then_inc(s["own"].sem, s["own"].add(1))
                dve.wait_ge(s["own"].sem, s["own"].at(b, s["own"].n))
            phase_end(dve, 1)

            s = SB
            D = s["D"]
            credit(dve, s["d_free"])
            with dve.Fori(0, B) as b:
                x_b = x_all[:, bass.ds(b, 1)].rearrange("p o i e -> p (o i) e")
                dve.tensor_copy(gate_m[:], gate_all[:, bass.ds(b, 1)].rearrange("p o i e -> p (o i) e")).then_inc(s["gate"].sem, s["gate"].add(1))
                dve.wait_ge(D.full.sem, D.filled(b, "gate.T"))
                sl = D.slot("gate.T")
                dve.tensor_copy(gate_t, sl[0:NE, :]).then_inc(D.free.sem, D.free.add(1))
                dve.wait_ge(D.full.sem, D.filled(b, "b2"))
                sl = D.slot("b2")
                dve.tensor_tensor(acc[:], tiles(sl), x_b, ALU.add).then_inc(D.free.sem, D.free.add(1))
                dve.wait_ge(D.free.sem, D.emptied(b, "b2"))
                for e in range(NE):
                    dve.wait_ge(D.full.sem, D.filled(b, ("y", e)))
                    sl = D.slot(("y", e))
                    for i in range(NT):
                        ins = dve.scalar_tensor_tensor(out=x_b[:, i, :] if e == NE - 1 else acc[:, i, :],
                                                       in0=sl[:, i * P:(i + 1) * P], scalar=gate_m[:, i, e:e + 1],
                                                       in1=acc[:, i, :], op0=ALU.mult, op1=ALU.add)
                    ins.then_inc(D.free.sem, D.free.add(1))
                    dve.wait_ge(D.free.sem, D.emptied(b, ("y", e)))
            phase_end(dve, 2)

            s = SC
            D = s["D"]
            credit(dve, s["d_free"], s["g_free"], s["q_used"], s["h1"])
            with dve.Fori(0, B) as b:
                x_b = x_all[:, bass.ds(b, 1)].rearrange("p o i e -> p (o i) e")
                normalise(s, 1, lambda i: x_b[:, i, :], xn, b).then_inc(s["xn"].sem, s["xn"].add(1))
                dve.wait_ge(s["xn"].sem, s["xn"].at(b, 1))
                normalise(s, 2, lambda i: xn[:, i, :], xa, b).then_inc(s["xa"].sem, s["xa"].add(1))
                dve.wait_ge(D.full.sem, D.filled(b, "xn.T"))
                sl = D.slot("xn.T")
                dve.tensor_copy(xn_t[:], sl[:]).then_inc(D.free.sem, D.free.add(1))
                dve.wait_ge(D.full.sem, D.filled(b, "xa.T"))
                sl = D.slot("xa.T")
                dve.tensor_scalar(xa_t[:], sl[:], g1_col[:, 0:1], None, ALU.mult).then_inc(D.free.sem, D.free.add(1))

                dve.wait_ge(D.full.sem, D.filled(b, "k|v"))
                sl = D.slot("k|v")
                v = tiles(sl)
                dve.tensor_copy(v1, v[:, :, D1:2 * D1])
                dve.tensor_copy(kf, v[:, :, 0:D1]).then_inc(D.free.sem, D.free.add(1))
                dve.wait_ge(D.free.sem, D.emptied(b, "k|v"))
                dve.tensor_tensor(kn, kf, kf, ALU.mult).then_inc(s["own"].sem, s["own"].add(1))
                dve.wait_ge(s["own"].sem, s["own"].at(b, s["own"].n))
                dve.reduce_sum(ksum[:], kn, AX.X).then_inc(s["sums"].sem, s["sums"].add(1))

                def inverse(length, dst, k, scale):
                    dve.wait_ge(s["lens"].sem, s["lens"].at(b, k))
                    dve.tensor_scalar(length, length, scale, NORM_EPS, ALU.mult, ALU.max).then_inc(s["own"].sem, s["own"].add(1))
                    dve.wait_ge(s["own"].sem, s["own"].at(b, s["own"].n))
                    dve.reciprocal(dst, length).then_inc(s["own"].sem, s["own"].add(1))
                    dve.wait_ge(s["own"].sem, s["own"].at(b, s["own"].n))

                inverse(klen[:], ksum[:], 1, 1.0)
                dve.scalar_tensor_tensor(out=kn, in0=kf, scalar=ROOT_SCALE,
                                                in1=ksum[:].unsqueeze(2).to_broadcast([P, NT, D1]), op0=ALU.mult,
                                                op1=ALU.mult).then_inc(s["own"].sem, s["own"].add(1))
                dve.wait_ge(s["own"].sem, s["own"].at(b, s["own"].n))
                twice = kn.unsqueeze(2).to_broadcast([P, NT, 2, D1])
                dve.tensor_copy(k_nat[:, 0].bitcast(F32R), twice).then_inc(s["own"].sem, s["own"].add(1))
                dve.wait_ge(s["own"].sem, s["own"].at(b, s["own"].n))
                dve.tensor_tensor(k_nat[:, 1], twice, k_nat[:, 0], ALU.subtract).then_inc(s["k_n"].sem, s["k_n"].add(1))

                def silu_up(c):
                    dve.wait_ge(s["A"].free.sem, s["A"].emptied(b, ("gu", c)))
                    dve.wait_ge(s["h1"].sem, s["h1"].at(b, c))
                    dve.scalar_tensor_tensor(out=full[:], in0=gu[:, 0, :], scalar=1.0, in1=gu[:, 1, :], op0=ALU.add,
                                                    op1=ALU.mult).then_inc(s["own"].sem, s["own"].add(1))
                    dve.wait_ge(s["own"].sem, s["own"].at(b, s["own"].n))
                    dve.scalar_tensor_tensor(out=h1[:, c, :], in0=full[:], scalar=0.5, in1=gu[:, 2, :],
                                                          op0=ALU.mult, op1=ALU.mult).then_inc(s["h1"].sem, s["h1"].add(1))

                def q_unit(i):
                    dve.wait_ge(s["A"].free.sem, s["A"].emptied(b, ("q", i)))
                    dve.reduce_sum(q_sum[:], q_sq, AX.X).then_inc(s["sums"].sem, s["sums"].add(1))
                    inverse(q_len[:], q_rn[:], 2 + i, QSCALE1)
                    if i:
                        dve.wait_ge(s["q_n"].sem, s["q_n"].at(b, i))
                    dve.scalar_tensor_tensor(
                        out=q_n, in0=q_raw, scalar=QSCALE1 * ROOT_SCALE,
                        in1=q_rn[:].unsqueeze(2).to_broadcast([P, H1, D1]), op0=ALU.mult, op1=ALU.mult).then_inc(s["q_used"].sem, s["q_used"].add(1))
                    dve.wait_ge(s["q_used"].sem, s["q_used"].at(b, i + 1))
                    if i:
                        dve.wait_ge(s["A"].full.sem, s["A"].full.at(b, s["A"].number["q.T", i - 1, 1] + 1))
                    dve.tensor_copy(q_nat[:, :, 0, :].bitcast(F32R), q_n).then_inc(s["own"].sem, s["own"].add(1))
                    dve.wait_ge(s["own"].sem, s["own"].at(b, s["own"].n))
                    dve.tensor_tensor(q_nat[:, :, 1, :], q_n, q_nat[:, :, 0, :], ALU.subtract).then_inc(s["q_n"].sem, s["q_n"].add(1))

                q_unit(0)
                silu_up(0)
                for i in range(1, NT):
                    q_unit(i)
                    if i < HC:
                        silu_up(i)
                for a in range(2):
                    dve.wait_ge(D.full.sem, D.filled(b, ("k.T", a)))
                    sl = D.slot(("k.T", a))
                    dve.tensor_copy(k_stack[:, a, :], sl[:]).then_inc(D.free.sem, D.free.add(1))
                dve.wait_ge(D.full.sem, D.filled(b, "ffn"))
                sl = D.slot("ffn")
                dve.tensor_tensor(acc[:], tiles(sl), x_b, ALU.add).then_inc(D.free.sem, D.free.add(1))
                dve.wait_ge(s["A"].free.sem, s["A"].emptied(b, ("q.T", NT - 1, 1)))
                for n in range(NP):
                    dve.wait_ge(D.full.sem, D.filled(b, ("o", n)))
                    sl = D.slot(("o", n))
                    dve.tensor_copy(o1[:, n, :], sl[:]).then_inc(D.free.sem, D.free.add(1))
                dve.wait_ge(s["pv"].sem, s["pv"].at(b, NP))
                dve.reciprocal(rsum, gather[:]).then_inc(s["g_free"].sem, s["g_free"].add(1))
                dve.wait_ge(D.free.sem, D.emptied(b, ("o", NP - 1)))
                for n in range(NP):
                    dve.wait_ge(D.full.sem, D.filled(b, ("1/sum", n)))
                    sl = D.slot(("1/sum", n))
                    dve.tensor_tensor(o1[:, n, :], sl[:], o1[:, n, :], ALU.mult).then_inc(D.free.sem, D.free.add(1))
                dve.wait_ge(D.full.sem, D.filled(b, "attended"))
                sl = D.slot("attended")
                normalise(s, 3, lambda i: sl[:, i * P:(i + 1) * P], y1, b).then_inc(s["own"].sem, s["own"].add(1))
                dve.wait_ge(s["own"].sem, s["own"].at(b, s["own"].n))
                dve.tensor_tensor(y1, y1, g2_all[:].unsqueeze(1).to_broadcast([P, NT, E]), ALU.mult).then_inc(D.free.sem, D.free.add(1))
                dve.wait_ge(D.free.sem, D.emptied(b, "attended"))
                dve.wait_ge(s["stored"].sem, s["stored"].at(b, 0))
                dve.tensor_tensor(fin, y1, acc[:], ALU.add).then_inc(s["fin"].sem, s["fin"].add(1))
                dve.wait_ge(s["fin"].sem, s["fin"].at(b, 1))

        counts = {v.name: (v.n, v.per) for s in (SA, SB, SC) for v in s.values() if isinstance(v, Signal)}
        assert all(n == per for n, per in counts.values()), {k: v for k, v in counts.items() if v[0] != v[1]}
        assert (n_pool[0], n_set[0], n_in[0]) == (N_POOL, N_SETUP, 16 * N_LOADS), (n_pool, n_set, n_in)


_INS = ["x", "wq", "bq", "wk", "bk", "wv", "bv", "wo", "bo", "w_router", "w1", "b1", "w2", "b2",
        "g1", "wq1_t", "wkv1_t", "wout1_t", "g2", "w_gate_t", "w_up_t", "w_down_t"]


def kernel(**inputs):
    import numpy as np
    import concourse.bacc as bacc
    from concourse.bass_utils import run_bass_kernel_spmd

    a0, f0, a1, f1 = "L0_attn_", "L0_ffn_", "L1_attn_", "L1_ffn_"
    laid = {"x": inputs[a0 + "hidden_states"], "w_router": inputs[f0 + "w_router"], "g1": inputs[a1 + "g1"],
            "g2": inputs[a1 + "g2"]}
    for n in ("wq", "bq", "wk", "bk", "wv", "bv", "wo", "bo"):
        laid[n] = inputs[a0 + n]
    for n in ("w1", "b1", "w2", "b2"):
        laid[n] = inputs[f0 + n]
    for n, k in (("wq1_t", a1 + "Wq"), ("wkv1_t", a1 + "Wkv"), ("wout1_t", a1 + "Wout"), ("w_gate_t", f1 + "w_gate"),
                 ("w_up_t", f1 + "w_up"), ("w_down_t", f1 + "w_down")):
        laid[n] = np.asarray(inputs[k]).T

    nc = bacc.Bacc("TRN2", target_bir_lowering=False, num_devices=1)
    arrays, args = {}, []
    for n in _INS:
        a = np.ascontiguousarray(laid[n])
        arrays[f"in_{n}"] = a
        args.append(nc.dram_tensor(f"in_{n}", a.shape, mybir.dt.from_np(a.dtype), kind="ExternalInput").ap())
    args.append(nc.dram_tensor("out_0", (B, T, E), F32, kind="ExternalOutput").ap())
    two_layers(nc, *args)
    r = run_bass_kernel_spmd(nc, [arrays], core_ids=[0])
    return r.results[0]["out_0"]
```

```python
from contextlib import ExitStack

import concourse.bass as bass
from concourse import mybir

ALU = mybir.AluOpType
ACT = mybir.ActivationFunctionType
AX = mybir.AxisListType
F32 = mybir.dt.float32
F32R = mybir.dt.float32r
BF16 = mybir.dt.bfloat16
I32 = mybir.dt.int32
U32 = mybir.dt.uint32

P = 128
B = 8
T = 512
E = 128
NT = T // P
EPS = 1e-5
NEG = -1e30
LOWEST = -3e38

H0, D0 = 16, 8
HG = 4
G = H0 // HG
ROW_KLO, ROW_QLO, ROW_MAX = 8, 16, 24
QSCALE0 = D0 ** -0.5
BAND = [(0, 384, 0, 128), (0, 512, 0, 0), (0, 512, 1, 0), (128, 384, 1, 0)]
BAND_T = [(0, 384, 0), (0, 512, 384), (0, 512, 896), (128, 384, 1408)]
HALF0 = 896
PV_ORDER = (1, 2, 0, 3)

NE, F0 = 8, 512
FC = F0 // P
TT = B * NT
TURN_B = 4
TURNS_B = -(-(TT + NE - 1) // TURN_B)
NS = TURNS_B * TURN_B
AT_B1, AT_W2, AT_B2, EXPERT = F0, F0 + FC, 2 * F0 + FC, 2 * F0 + FC + E
PAD = TT // 2
H1, D1 = 16, 64
NP = H1 // 2
PB = 3
QSCALE1, NORM_EPS, ROOT_SCALE = 16.0, 1e-12, 4.0
HID = 384
HC = HID // P
DEQUANT = 1.0 / 127.0
DR, AR = 3, 2

PER_A = dict(d_full=85, d_free=85, a_full=32, a_free=32, own=23, var=1, veps=1, rstd=1, xn=1, xcopied=1,
             k_ready=G, k_dma0=16 * HG, k_dma1=16 * HG, k_dma2=16 * HG, k_dma3=16 * HG, q_ready=G, lg=1, lge=1, gate=1, mcol=G, masked=32, pv=G, g_free=G)
PER_B = dict(xt_full=4, xt_free=4, staged=4, h_full=4, h_free=4, y_full=4, y_free=4,
             in0=16, in1=16, in2=16, in3=16, out0=16, out1=16, out2=16, out3=16)
PER_R = dict(r_full=5, r_free=5, own=7, var=2, veps=2, rstd=2, xn=1, xa=1, sums=1, lens=1, k_n=1)
PER_C = dict(squared=8, d_full=26, d_free=25, a_full=35, a_free=35, own=29, var=1, veps=1, rstd=1,
             sums=8, lens=8, q_n=8, h1=3, masked=24, pv=8, g_free=2, fin=1, stored=16)
CREDITED = dict(d_free=1, a_free=1, g_free=1, sums=1, h1=1, r_free=1, xcopied=1, stored=1, pv=1,
                xt_free=1, y_full=1, y_free=1, staged=2, out0=1, out1=1, out2=1, out3=1)


N_POOL, N_SETUP, N_LOADS = 42, 16, 39
N_SORT = 7


class Signal:

    def __init__(self, ctx, nc, phase, name, per):
        self.name = f"{phase}_{name}"
        self.sem = ctx.enter_context(nc.semaphore(self.name))
        self.per, self.credit, self.n = per, CREDITED.get(name, 0), 0

    def add(self, k):
        self.n += k
        return k

    def restart(self):
        self.n = 0

    def at(self, b, k):
        return b * self.per + (k + self.credit)


class Ring:

    def __init__(self, full, free, slots):
        self.full, self.free, self.slots = full, free, slots
        self.number = {}

    def fillable(self, b, what):
        n = self.number.setdefault(what, len(self.number))
        return self.free.at(b, max(n - len(self.slots) + 1, 0))

    def slot(self, what):
        return self.slots[self.number[what] % len(self.slots)]

    def filled(self, b, what):
        return self.full.at(b, self.number[what] + 1)

    def emptied(self, b, what, before=0):
        return self.free.at(b, self.number[what] + 1 - before)


def two_layers(nc, x, wq, bq, wk, bk, wv, bv, wo, bo, w_router, w1, b1, w2, b2,
               g1, wq1_t, wkv1_t, wout1_t, g2, w_gate_t, w_up_t, w_down_t, slots_x, slots_y, out):
    x_d = x.rearrange("b (i p) e -> p b i e", p=P)
    out_d = out.rearrange("b (i p) e -> b p i e", p=P)

    with ExitStack() as ctx:
        def sb(name, shape, dt=F32):
            return ctx.enter_context(nc.sbuf_tensor(name, shape, dt))

        def sem(name):
            return ctx.enter_context(nc.semaphore(name))

        banks_d = [ctx.enter_context(nc.psum_tensor(f"ring_d{n}", [P, T], F32)) for n in range(DR)]
        gather = ctx.enter_context(nc.psum_tensor("gather", [P, T], F32))
        banks_a = [ctx.enter_context(nc.psum_tensor(f"ring_a{n}", [P, 2 * T], F32)) for n in range(AR)]

        wq_rep, wk_rep = sb("wq_rep", [P, G, HG, 4, D0]), sb("wk_rep", [P, G, HG, 4, D0])
        wv_sb, wo_sb = sb("wv_sb", [P, E]), sb("wo_sb", [P, E])
        bq_col, bk_col, bk_in = sb("bq_col", [P, G]), sb("bk_col", [P, G]), sb("bk_in", [P, G])
        bv_all, bo_all, g2_all = sb("bv_all", [P, E]), sb("bo_all", [P, E]), sb("g2_all", [P, E])
        g1_col = sb("g1_col", [P, 1])
        router_sb = sb("router_sb", [P, NE])
        zeros = sb("zeros", [P, E])
        wq1_sb = sb("wq1_sb", [P, H1 * D1])
        wkv1_sb = sb("wkv1_sb", [P, 2 * D1])
        wout1_sb = sb("wout1_sb", [P, NP, E])
        wffn = sb("wffn", [P, 3, HID])
        ident = sb("ident", [P, P])
        qlo_neg, klo_neg, ones_row = sb("qlo_neg", [P, 1]), sb("klo_neg", [P, 1]), sb("ones_row", [P, 1])
        rows4 = sb("rows4", [P, 3, HG])
        masks = sb("masks", [P, 2, T], BF16)
        rev_e = sb("rev_e", [P, NT, NE])
        pick_sum = sb("pick_sum", [P, HG, 32])
        spread = sb("spread", [P, NP, P])

        x_all = sb("x_all", [P, B, NT, E])
        xn_all = sb("xn_all", [P, TT, E])
        gate_all = sb("gate_all", [P, TT, NE])
        wgt_all = sb("wgt_all", [P, TT])
        slots = sb("slots", [P, TT], U32)

        xn, xn_t = sb("xn", [P, NT, E]), sb("xn_t", [P, T])
        stats, mv = sb("stats", [P, NT, 6]), sb("mv", [P, NT, 2])
        veps, rstd = sb("veps", [P, NT]), sb("rstd", [P, NT])
        exponents = sb("exponents", [P, NT + H1])
        full, hi = sb("full", [P, T]), sb("hi", [P, T], F32R)
        k_rows, q_rows = sb("k_rows", [P, G, T], F32R), sb("q_rows", [P, G, T], F32R)
        q_max = sb("q_max", [P, 2, T], F32R)
        rows = sb("rows", [P, H0, T], F32R)
        v_aug = sb("v_aug", [P, NT, H0, 32])
        dump = sb("dump", [P, 2, T], BF16)
        mx = sb("mx", [P, HG, NT])
        m_cols = sb("m_cols", [P, NT, HG, 32])
        arena = sb("arena", [P, 16384])
        o_raw, o_t = sb("o_raw", [P, T]), sb("o_t", [P, T])
        rden = sb("rden", [P, NT, HG])
        o_n, acc = sb("o_n", [P, NT, E]), sb("acc", [P, NT, E])
        lg, lge, lg2, hot = (sb(n, [P, NT, NE]) for n in ("lg", "lge", "lg2", "hot"))
        lmx, cmx, lsum, wgt = (sb(n, [P, NT]) for n in ("lmx", "cmx", "lsum", "wgt"))
        xa_t = o_raw
        ksum, klen = sb("ksum", [P, NT]), sb("klen", [P, NT])
        k_stack = k_rows[:, 0:2, :]
        q_sum, q_len, q_rn = sb("q_sum", [P, H1]), sb("q_len", [P, H1]), sb("q_rn", [P, H1])

        probs = arena[:, 0:8 * 2 * HALF0].rearrange("p (h n) -> p h n", h=8)
        experts = arena[:, 0:NE * EXPERT].rearrange("p (e n) -> p e n", e=NE)
        b_at = NE * EXPERT
        staged = arena[:, b_at:b_at + TURN_B * EXPERT].rearrange("p (u n) -> p u n", u=TURN_B)
        sort_at = b_at + EXPERT
        b_at += TURN_B * EXPERT
        hidden = arena[:, b_at:b_at + 2 * F0].rearrange("p (u c t) -> p u c t", u=2, c=FC)
        x_in = arena[:, b_at + 1024:b_at + 1536].rearrange("p (u e) -> p u e", u=TURN_B)
        x_t = arena[:, b_at + 1536:b_at + 1792].rearrange("p (u t) -> p u t", u=2)
        y_out = arena[:, b_at + 1792:b_at + 2304].rearrange("p (u e) -> p u e", u=TURN_B)
        tile_expert = arena[:, b_at + 2304:b_at + 2304 + NS + 2].bitcast(I32)
        assert b_at + 2304 + NS + 2 <= 16384

        probs1 = arena[:, 0:7680].rearrange("p (n t) -> p n t", n=PB)
        o1 = arena[:, 7680:11776].rearrange("p (n t) -> p n t", n=NP)
        q_nat = arena[:, 11776:13824].rearrange("p (n g a d) -> p n g a d", n=2, a=2, d=D1)
        q_sq = arena[:, 13824:14336].rearrange("p (g d) -> p g d", d=D1)
        q_n = arena[:, 14336:14848].rearrange("p (g d) -> p g d", d=D1)
        k_nat = arena[:, 14848:15872].rearrange("p (a i r d) -> p a i r d", a=2, i=NT, r=2)
        kf, kn = (arena[:, at:at + 256].rearrange("p (i d) -> p i d", i=NT) for at in (15872, 16128))
        spare = xn_all[:].rearrange("p t e -> p (t e)")
        gu = spare[:, 0:3072].rearrange("p (n a t) -> p n a t", n=2, a=3)
        y1, xa = (spare[:, at:at + 512].rearrange("p (i e) -> p i e", i=NT) for at in (3072, 3584))
        spare = v_aug[:].rearrange("p j h d -> p (j h d)")
        v1 = spare[:, 0:NT * D1].rearrange("p (j d) -> p j d", j=NT)
        h1 = spare[:, 256:1792].rearrange("p (c t) -> p c t", c=HC)
        fin = o_t[:].rearrange("p (i e) -> p i e", i=NT)
        rsum = m_cols[:].rearrange("p i h r -> p (i h r)")
        wint = arena[:, 15360 - 1152:15360].bitcast(I32)
        nat = arena[:, 13000:13256].rearrange("p (a e) -> p a e", a=2)
        def sort_view(n):
            sort_views.append((sort_views[-1][1], sort_views[-1][1] + n))
            return arena[:, sort_views[-1][0]:sort_views[-1][1]]

        sort_views = [(0, sort_at)]
        ones, before, steps = sort_view(P), sort_view(P), sort_view(TT)
        lower = sort_view(NE * NE).rearrange("p (a c) -> p a c", a=NE)
        tile_no = sort_view((NS + 2) * NE).rearrange("p (s e) -> p s e", e=NE)
        hot_e = sort_view(NE * TT).rearrange("p (e t) -> p e t", e=NE)
        run = sort_view(2 * NE * (PAD + TT)).rearrange("p (a e t) -> p a e t", a=2, e=NE)
        worked = sort_view(NE * TT).rearrange("p (e t) -> p e t", e=NE)
        worked2 = sort_view(NE * NE).rearrange("p (a c) -> p a c", a=NE)
        tile_past = sort_view((NS + 2) * NE).rearrange("p (s e) -> p s e", e=NE)
        many_tiles, base_e, end_e = sort_view(NE), sort_view(NE), sort_view(NE)
        slot_f, expert_f = sort_view(TT), sort_view(NS + 2)
        assert sort_views[-1][1] <= b_at


        s_apart = [sem("apart_vector"), sem("apart_gpsimd")]
        s_win, s_w12 = sem("weights_in"), sem("experts_in")
        s_zero, s_sort_const, s_sort = sem("slots_zeroed"), sem("sort_constants"), sem("sort_steps")
        s_rank, s_slots, s_sent, s_back = sem("ranks"), sem("slots_known"), sem("tokens_sent"), sem("tokens_back")
        s_x, s_pool, s_set, s_phase = sem("x_in"), sem("pool_setup"), sem("dve_setup"), sem("phase_done")
        n_in, n_pool, n_set = [0], [0], [0]

        def signals(phase, per):
            s = {k: Signal(ctx, nc, phase, k, v) for k, v in per.items()}
            if phase == "B":
                s["in"] = [s["in0"], s["in1"], s["in2"], s["in3"]]
                s["out"] = [s["out0"], s["out1"], s["out2"], s["out3"]]
                return s
            if phase == "R":
                s["R"] = Ring(s["r_full"], s["r_free"], [banks_a[n][:, at:at + T] for n in range(AR) for at in (0, T)])
                return s
            s["D"] = Ring(s["d_full"], s["d_free"], banks_d)
            s["A"] = Ring(s["a_full"], s["a_free"], banks_a)
            if phase == "A":
                s["k_dma"] = [s["k_dma0"], s["k_dma1"], s["k_dma2"], s["k_dma3"]]
            return s

        SA, SB, SR, SC = signals("A", PER_A), signals("B", PER_B), signals("R", PER_R), signals("C", PER_C)

        def credit(eng, *names):
            for n in names:
                eng.sem_inc(n.sem, n.credit)

        def phase_end(eng, n):
            eng.drain().then_inc(s_phase, 1)
            eng.wait_ge(s_phase, 5 * n)

        def apart(eng):
            eng.sem_inc(s_apart[0 if eng is nc.vector else 1], 1)

        def tiles(slot):
            return slot[:, :].rearrange("p (i e) -> p i e", i=NT)

        block = ctx.enter_context(nc.Block())

        @block.tensor
        def _(pe):
            pe.wait_ge(s_pool, N_POOL)

            def mm(out, lhs, rhs, start=True, stop=True):
                return pe.matmul(out, lhs, rhs, start=start, stop=stop, skip_group_check=True)

            def turn(slot, tile_of, n=NT):
                return [pe.transpose(slot[:, i * P:(i + 1) * P], tile_of(i), ident[:]) for i in range(n)][-1]

            s = SA
            D, A = s["D"], s["A"]
            pe.wait_ge(s_set, N_SETUP)
            credit(pe, s["pv"])
            with pe.Fori(0, B) as b:
                pe.wait_ge(s["xn"].sem, s["xn"].at(b, 1))
                pe.wait_ge(D.free.sem, D.fillable(b, "xn.T"))
                sl = D.slot("xn.T")
                turn(sl, lambda i: xn[:, i, :]).then_inc(D.full.sem, D.full.add(1))
                pe.wait_ge(D.free.sem, D.emptied(b, "xn.T"))
                for g in range(G):
                    pe.wait_ge(D.free.sem, D.fillable(b, ("k", g)))
                    sl = D.slot(("k", g))
                    mm(sl[:], wk_rep[:, g].rearrange("p h c d -> p (h c d)"), xn_t[:]).then_inc(D.full.sem, D.full.add(1))
                for g in range(G):
                    pe.wait_ge(D.free.sem, D.fillable(b, ("q", g)))
                    sl = D.slot(("q", g))
                    mm(sl[:], wq_rep[:, g].rearrange("p h c d -> p (h c d)"), xn_t[:]).then_inc(D.full.sem, D.full.add(1))
                    if g == 0:
                        pe.wait_ge(D.free.sem, D.fillable(b, "v"))
                        sl = D.slot("v")
                        [mm(sl[:, i * P:(i + 1) * P], xn_t[:, i * P:(i + 1) * P], wv_sb[:])
                                                   for i in range(NT)][-1].then_inc(D.full.sem, D.full.add(1))
                pe.wait_ge(D.free.sem, D.fillable(b, "logits"))
                sl = D.slot("logits")
                [mm(sl[:, i * NE:(i + 1) * NE], xn_t[:, i * P:(i + 1) * P], router_sb[:])
                                                for i in range(NT)][-1].then_inc(D.full.sem, D.full.add(1))

                def score_rows(g, i):
                    first, many, _, _ = BAND[i]
                    for h in range(HG):
                        pe.wait_ge(D.free.sem, D.fillable(b, ("max", g, i, h)))
                        sl = D.slot(("max", g, i, h))
                        mm(
                            sl[:, 0:many], q_rows[:, g, i * P:(i + 1) * P], rows[:, HG * g + h, first:first + many]).then_inc(D.full.sem, D.full.add(1))

                def score_cols(g, h):
                    for half in range(2):
                        pe.wait_ge(A.free.sem, A.fillable(b, ("probs", HG * g + h, half)))
                        sl = A.slot(("probs", HG * g + h, half))
                        for j in (2 * half, 2 * half + 1):
                            first, many, at = BAND_T[j]
                            at += 128 if half == 0 else -HALF0
                            ins = mm(sl[:, at:at + many], rows[:, HG * g + h, j * P:(j + 1) * P],
                                     q_max[:, g % 2, first:first + many])
                        ins.then_inc(A.full.sem, A.full.add(1))

                def values(g, js):
                    if js[0] == PV_ORDER[0]:
                        pe.wait_ge(s["masked"].sem, s["masked"].at(b, 2 * HG * (g + 1)))
                        pe.wait_ge(s["g_free"].sem, s["g_free"].at(b, g))
                    for j in js:
                        first, many, at = BAND_T[j]
                        for h in range(HG):
                            ins = mm(gather[32 * h:32 * h + 32, first:first + many], v_aug[:, j, HG * g + h, :],
                                     probs[:, (HG * g + h) % 8, at:at + many],
                                     start=(j == PV_ORDER[0]), stop=(j == PV_ORDER[-1]))
                    if js[-1] == PV_ORDER[-1]:
                        ins.then_inc(s["pv"].sem, s["pv"].add(1))

                def turn_out(g):
                    pe.wait_ge(s["g_free"].sem, s["g_free"].at(b, g + 1))
                    pe.wait_ge(D.free.sem, D.fillable(b, ("o.T", g)))
                    sl = D.slot(("o.T", g))
                    turn(sl, lambda i: o_raw[:, i * P:(i + 1) * P]).then_inc(D.full.sem, D.full.add(1))

                pe.wait_ge(s["q_ready"].sem, s["q_ready"].at(b, 1))
                pe.wait_ge(s["k_dma"][0].sem, s["k_dma"][0].at(b, 16 * HG))
                for i in range(NT):
                    score_rows(0, i)
                for g in range(G):
                    pe.wait_ge(s["mcol"].sem, s["mcol"].at(b, g + 1))
                    pe.wait_ge(D.free.sem, D.fillable(b, ("q_max", g)))
                    sl = D.slot(("q_max", g))
                    turn(sl, lambda i: m_cols[:, i].rearrange("p h r -> p (h r)")).then_inc(D.full.sem, D.full.add(1))
                    if g + 1 < G:
                        pe.wait_ge(s["q_ready"].sem, s["q_ready"].at(b, g + 2))
                        pe.wait_ge(s["k_dma"][g + 1].sem, s["k_dma"][g + 1].at(b, 16 * HG))
                    for i in range(NT):
                        if g + 1 < G:
                            score_rows(g + 1, i)
                        if i == 0:
                            pe.wait_ge(D.free.sem, D.emptied(b, ("q_max", g)))
                        score_cols(g, i)
                        if g and i < 2:
                            values(g - 1, PV_ORDER[2 * i:2 * i + 2])
                    if g:
                        turn_out(g - 1)
                values(G - 1, PV_ORDER)
                turn_out(G - 1)
                pe.wait_ge(D.free.sem, D.emptied(b, ("o.T", G - 1)))
                pe.wait_ge(D.free.sem, D.fillable(b, "heads.T"))
                sl = D.slot("heads.T")
                turn(sl, lambda i: o_n[:, i, :]).then_inc(D.full.sem, D.full.add(1))
                pe.wait_ge(D.free.sem, D.emptied(b, "heads.T"))
                pe.wait_ge(D.free.sem, D.fillable(b, "attended"))
                sl = D.slot("attended")
                [mm(sl[:, i * P:(i + 1) * P], o_t[:, i * P:(i + 1) * P], wo_sb[:])
                                                  for i in range(NT)][-1].then_inc(D.full.sem, D.full.add(1))
            phase_end(pe, 1)

            s = SB
            pe.wait_ge(s_sort_const, 2)
            pe.wait_ge(s_sort, 1)
            mm(banks_d[0][:, 0:NE * TT], before, hot_e.rearrange("p e t -> p (e t)"))
            mm(banks_d[0][:, NE * TT:2 * NE * TT], ones, hot_e.rearrange("p e t -> p (e t)")).then_inc(s_rank, 1)
            credit(pe, s["y_full"])
            with pe.Fori(0, TURNS_B) as b:
                for u in range(TURN_B):
                    def x_turned(u):
                        pe.wait_ge(s["in"][u].sem, s["in"][u].at(b, 16))
                        pe.wait_ge(s["xt_free"].sem, s["xt_free"].at(b, max(u - 1, 0)))
                        pe.transpose(banks_d[u % 2][:, 0:P], x_in[:, u], ident[:]).then_inc(s["xt_full"].sem, s["xt_full"].add(1))

                    def up(u):
                        pe.wait_ge(s["xt_free"].sem, s["xt_free"].at(b, u + 1))
                        pe.wait_ge(s["staged"].sem, s["staged"].at(b, u - 1))
                        for c in range(FC):
                            ins = mm(banks_a[u % 2][:, c * P:(c + 1) * P],
                                     staged[:, u, 0:F0].rearrange("p (f c) -> p c f", c=FC)[:, c], x_t[:, u % 2])
                        ins.then_inc(s["h_full"].sem, s["h_full"].add(1))

                    def down(u):
                        pe.wait_ge(s["h_free"].sem, s["h_free"].at(b, u + 1))
                        pe.wait_ge(s["y_free"].sem, s["y_free"].at(b, max(u - 1, 0)))
                        for c in range(FC):
                            ins = mm(banks_a[u % 2][:, T:T + E], hidden[:, u % 2, c],
                                     staged[:, u, AT_W2 + c * E:AT_W2 + (c + 1) * E], start=(c == 0), stop=(c == FC - 1))
                        ins.then_inc(s["y_full"].sem, s["y_full"].add(1))

                    if u % 2:
                        x_turned(u - 1)
                        x_turned(u)
                        up(u - 1)
                        up(u)
                        down(u - 1)
                        down(u)
            phase_end(pe, 2)

            credit(pe, SC["pv"])

            def turn_x(b, behind=True):
                s = SR
                R = s["R"]
                if behind:
                    pe.wait_ge(SC["a_free"].sem, SC["A"].emptied(b - 1, ("probs", NP - 1, 2)))
                for name, src, ready in (("xn.T", xn, s["xn"]), ("xa.T", xa, s["xa"])):
                    pe.wait_ge(ready.sem, ready.at(b, 1))
                    pe.wait_ge(R.free.sem, R.fillable(b, name))
                    turn(R.slot(name), lambda i: src[:, i, :]).then_inc(R.full.sem, R.full.add(1))

            def project_kv(b):
                R = SR["R"]
                pe.wait_ge(R.free.sem, R.emptied(b, "xa.T"))
                pe.wait_ge(R.free.sem, R.fillable(b, "k|v"))
                sl = R.slot("k|v")
                [mm(sl[:, i * P:(i + 1) * P], xa_t[:, i * P:(i + 1) * P], wkv1_sb[:])
                 for i in range(NT)][-1].then_inc(R.full.sem, R.full.add(1))

            def turn_k(b):
                s = SR
                R = s["R"]
                pe.wait_ge(s["k_n"].sem, s["k_n"].at(b, 1))
                for a in range(2):
                    pe.wait_ge(R.free.sem, R.fillable(b, ("k.T", a)))
                    turn(R.slot(("k.T", a)),
                         lambda i: k_nat[:, a, i].rearrange("p r d -> p (r d)")).then_inc(R.full.sem, R.full.add(1))

            def attend(b, last):
                s = SC
                D, A = s["D"], s["A"]
                for name in ("d_full", "a_full", "pv"):
                    s[name].restart()
                if not last:
                    SR["r_full"].restart()

                def project_q(n):
                    pe.wait_ge(D.free.sem, D.fillable(b, ("q", n)))
                    sl = D.slot(("q", n))
                    [mm(sl[:, i * P:(i + 1) * P], xa_t[:, i * P:(i + 1) * P], wq1_sb[:, n * P:(n + 1) * P])
                     for i in range(NT)][-1].then_inc(D.full.sem, D.full.add(1))

                def gate_up(c):
                    pe.wait_ge(A.free.sem, A.fillable(b, ("gu", c)))
                    sl = A.slot(("gu", c))
                    [mm(sl[:, n * T:(n + 1) * T], wffn[:, n, c * P:(c + 1) * P], xn_t[:])
                     for n in range(2)][-1].then_inc(A.full.sem, A.full.add(1))

                def turn_q(n):
                    pe.wait_ge(s["q_n"].sem, s["q_n"].at(b, n + 1))
                    pe.wait_ge(A.free.sem, A.fillable(b, ("q.T", n)))
                    sl = A.slot(("q.T", n))
                    [pe.transpose(sl[:, c * T + i * P:c * T + (i + 1) * P],
                                  q_nat[:, n % 2, 2 * i + c].rearrange("p a d -> p (a d)"), ident[:])
                     for c in range(2) for i in range(NT)][-1].then_inc(A.full.sem, A.full.add(1))

                def stacked(out, j, q):
                    mm(out, k_stack[:, 0, j * P:(j + 1) * P], q, stop=False)
                    return mm(out, k_stack[:, 1, j * P:(j + 1) * P], q, start=False)

                def scores(n):
                    at = 2 * (n % PB)
                    pe.wait_ge(A.free.sem, A.emptied(b, ("q.T", n)))
                    for c in range(2):
                        pe.wait_ge(A.free.sem, A.fillable(b, ("probs", n, c)))
                        sl = A.slot(("probs", n, c))
                        stacked(sl[:, 0:512], 0, rows[:, at + c, :])
                        stacked(sl[:, 512:896], 1, rows[:, at + c, 128:512]).then_inc(A.full.sem, A.full.add(1))
                    pe.wait_ge(A.free.sem, A.fillable(b, ("probs", n, 2)))
                    sl = A.slot(("probs", n, 2))
                    stacked(sl[:, 0:512], 2, rows[:, at:at + 2, 256:512])
                    stacked(sl[:, 512:768], 3, rows[:, at:at + 2, 384:512]).then_inc(A.full.sem, A.full.add(1))

                def p_of(n, c, j):
                    at = ((c * 896, 512), (c * 896 + 512, 384), (1792 + c * 256, 256), (2304 + c * 128, 128))[j]
                    return probs1[:, n % PB, at[0]:at[0] + at[1]]

                def values1(n):
                    pe.wait_ge(s["masked"].sem, s["masked"].at(b, 3 * (n + 1)))
                    pe.wait_ge(D.free.sem, D.fillable(b, ("o", n)))
                    sl = D.slot(("o", n))
                    [mm(sl[D1 * c:D1 * c + D1, j * P:T], v1[:, j, :], p_of(n, c, j), start=(j == 0), stop=(j == NT - 1))
                     for j in range(NT) for c in range(2)][-1].then_inc(D.full.sem, D.full.add(1))

                def sums1(n):
                    if n == 0:
                        pe.wait_ge(s["g_free"].sem, s["g_free"].at(b, 0))
                    for j in range(NT):
                        for c in range(2):
                            h = 2 * n + c
                            ins = mm(gather[32 * (h % 4):32 * (h % 4) + 32, j * P:T], pick_sum[:, h // 4, :],
                                     p_of(n, c, j), start=(h < 4 and j == 0), stop=(n == NP - 1 and j == NT - 1))
                    ins.then_inc(s["pv"].sem, s["pv"].add(1))

                project_q(0)
                project_q(1)
                pe.wait_ge(SR["r_free"].sem, SR["R"].emptied(b, ("k.T", 1)))
                gate_up(0)
                gate_up(1)
                turn_q(0)
                for n in range(NP):
                    if n + 2 < NP:
                        project_q(n + 2)
                    if n + 1 < NP:
                        turn_q(n + 1)
                    scores(n)
                    if n == 0:
                        gate_up(2)
                    else:
                        values1(n - 1)
                        sums1(n - 1)
                values1(NP - 1)
                if not last:
                    turn_x(b + 1)
                sums1(NP - 1)
                pe.wait_ge(s["h1"].sem, s["h1"].at(b, HC))
                pe.wait_ge(D.free.sem, D.fillable(b, "ffn"))
                sl = D.slot("ffn")
                [mm(sl[:, i * P:(i + 1) * P], h1[:, c, i * P:(i + 1) * P],
                    wffn[:, 2, c * P:(c + 1) * P], start=(c == 0), stop=(c == HC - 1))
                 for i in range(NT) for c in range(HC)][-1].then_inc(D.full.sem, D.full.add(1))
                if not last:
                    project_kv(b + 1)

                def spread_sums(n):
                    pe.wait_ge(D.free.sem, D.fillable(b, ("1/sum", n)))
                    mm(D.slot(("1/sum", n))[:], spread[:, n, :], rsum).then_inc(D.full.sem, D.full.add(1))

                pe.wait_ge(s["g_free"].sem, s["g_free"].at(b, 1))
                spread_sums(0)
                spread_sums(1)
                for n in range(NP):
                    if n + 2 < NP:
                        spread_sums(n + 2)
                    pe.wait_ge(D.free.sem, D.emptied(b, ("1/sum", n)))
                    ins = [mm(gather[:, i * P:(i + 1) * P], o1[:, n, i * P:(i + 1) * P], wout1_sb[:, n, :],
                              start=(n == 0 and i == 0), stop=(n == NP - 1)) for i in range(NT)][-1]
                    if n == NP - 1:
                        ins.then_inc(D.full.sem, D.full.add(1))
                    if n == NP - 2 and not last:
                        turn_k(b + 1)

            turn_x(0, behind=False)
            project_kv(0)
            turn_k(0)
            with pe.Fori(0, B - 1) as b:
                attend(b, last=False)
            attend(B - 1, last=True)

        @block.sync
        def _(sp):
            def load(dst, src):
                sp.dma_start(dst, src, allow_slow_non_contiguous=True).then_inc(s_win, 16)
                n_in[0] += 16

            sp.dma_start(x_all[:, 0], x_d[:, 0]).then_inc(s_x, 16)
            load(nat[:, 0, :], wk)
            load(nat[:, 1, :], wq)
            sp.wait_ge(s_set, 4)
            for h in range(HG):
                for c in range(3):
                    r = 32 * h + D0 * c
                    load(bq_col[r:r + D0, :], bq.rearrange("(g h d) -> h d g", g=G, h=HG)[h])
                    load(bk_in[r:r + D0, :], bk.rearrange("(g h d) -> h d g", g=G, h=HG)[h])
            load(wv_sb[:], wv)
            load(wo_sb[:], wo)
            load(router_sb[:], w_router)
            for t, v in ((bv_all, bv), (bo_all, bo), (g2_all, g2)):
                load(t[:], v.rearrange("(a e) -> a e", a=1).to_broadcast([P, E]))
            load(g1_col[:], g1.rearrange("(e a) -> e a", a=1))
            for n, w in enumerate((w_gate_t, w_up_t)):
                load(wint[:, n * HID:(n + 1) * HID], w)
            load(wint[:, 2 * HID:3 * HID].rearrange("p (c e) -> p c e", c=HC), w_down_t.rearrange("(c p) e -> p c e", p=P))
            for n in range(1, B):
                sp.dma_start(x_all[:, n], x_d[:, n]).then_inc(s_x, 16)
            load(wq1_sb[:], wq1_t)
            load(wkv1_sb[:], wkv1_t)
            load(wout1_sb[:], wout1_t.rearrange("(n p) e -> p n e", p=P))

            sp.wait_ge(s_pool, N_POOL)
            sp.dma_start(slots_x.rearrange("(p n) e -> p n e", p=P),
                         zeros[:].unsqueeze(1).to_broadcast([P, NS, E])).then_inc(s_zero, 16)
            s = SA
            with sp.Fori(0, B) as b:
                sp.wait_ge(s["pv"].sem, s["pv"].at(b, 0))
                for g in range(G):
                    sp.wait_ge(s["k_ready"].sem, s["k_ready"].at(b, g + 1))
                    for h in range(HG):
                        sp.dma_start(rows[32 * h:32 * h + 32, HG * g + h, :].bitcast(F32),
                                                     k_rows[32 * h:32 * h + 32, g, :].bitcast(F32)).then_inc(s["k_dma"][g].sem, s["k_dma"][g].add(16))
            phase_end(sp, 1)
            for dst, src in ((experts[:, :, 0:F0], w1.rearrange("e d f -> d e f")),
                             (experts[:, :, AT_B1:AT_W2], b1.rearrange("e (f c) -> f e c", c=FC)),
                             (experts[:, :, AT_W2:AT_B2], w2.rearrange("e (f c) d -> f e (c d)", c=FC)),
                             (experts[:, :, AT_B2:EXPERT], b2.rearrange("(a e) d -> a e d", a=1).to_broadcast([P, NE, E]))):
                sp.dma_start(dst, src, allow_slow_non_contiguous=True).then_inc(s_w12, 16)
            s = SB
            credit(sp, *s["out"])
            x_rows = slots_x.rearrange("(b u p) e -> u p b e", u=TURN_B, p=P)
            y_rows = slots_y.rearrange("(b u p) e -> u p b e", u=TURN_B, p=P)
            sp.wait_ge(s_sent, 16 * TT)
            for u in range(TURN_B):
                sp.dma_start(x_in[:, u], x_rows[u, :, 0]).then_inc(s["in"][u].sem, s["in"][u].add(16))
            with sp.Fori(1, TURNS_B) as b:
                for u in range(TURN_B):
                    sp.wait_ge(s["xt_full"].sem, s["xt_full"].at(b, u - 3))
                    sp.dma_start(x_in[:, u], x_rows[u][:, bass.ds(b, 1)].rearrange("p o e -> p (o e)")).then_inc(s["in"][u].sem, 16)
                    sp.wait_ge(s["y_free"].sem, s["y_free"].at(b, u - 3))
                    sp.dma_start(y_rows[u][:, bass.ds(b - 1, 1)].rearrange("p o e -> p (o e)"), y_out[:, u]).then_inc(s["out"][u].sem, s["out"][u].add(16))
            for u in range(TURN_B):
                sp.wait_ge(s["y_free"].sem, s["y_free"].at(TURNS_B - 1, u + 1))
                sp.dma_start(y_rows[u, :, TURNS_B - 1], y_out[:, u]).then_inc(s["out"][u].sem, 16)
            phase_end(sp, 2)
            s = SC
            credit(sp, s["stored"])
            with sp.Fori(0, B) as b:
                sp.wait_ge(s["fin"].sem, s["fin"].at(b, 1))
                sp.dma_start(out_d[bass.ds(b, 1)].rearrange("o p i e -> (o p) i e"), fin).then_inc(s["stored"].sem, s["stored"].add(16))
            sp.wait_ge(s["stored"].sem, 16 * B + 1)

        @block.gpsimd
        def _(pool):
            def step(ins):
                ins.then_inc(s_pool, 1)
                n_pool[0] += 1
                pool.wait_ge(s_pool, n_pool[0])

            def keep(v, op, fill, base, pattern, mult):
                step(pool.affine_select(out=v, in_=v, compare_op=op, fill=fill, base=base, pattern=pattern,
                                        channel_multiplier=mult))

            for n, (row, many, val) in enumerate(((ROW_QLO, D0, -1.0), (ROW_KLO, D0, -1.0), (ROW_MAX, 2, 1.0))):
                step(pool.memset(rows4[:, n, :], val))
                keep(rows4[:, n, :], ALU.is_ge, 0.0, -row, [[-32, HG]], 1)
                keep(rows4[:, n, :], ALU.is_ge, 0.0, row + many - 1, [[32, HG]], -1)
            step(pool.memset(exponents[:, 0:NT], -0.5))
            step(pool.memset(exponents[:, NT:NT + H1], 0.5))
            step(pool.memset(zeros[:], 0.0))
            step(pool.memset(ident[:], 0.0))
            keep(ident[:], ALU.not_equal, 1.0, 0, [[-1, P]], 1)
            step(pool.memset(rows[:].bitcast(F32), 0.0))
            step(pool.memset(masks[:], 0.0))
            keep(masks[:, 0, 384:512], ALU.is_ge, NEG, 0, [[-1, P]], 1)
            keep(masks[:, 1, 0:128], ALU.is_ge, NEG, 0, [[1, P]], -1)
            step(pool.iota(rev_e[:], pattern=[[0, NT], [-1, NE]], base=NE, channel_multiplier=0,
                           allow_small_or_imprecise_dtypes=True))
            step(pool.memset(m_cols[:], 0.0))
            step(pool.memset(v_aug[:], 0.0))
            step(pool.memset(v_aug[:, :, :, D0:D0 + 1], 1.0))
            step(pool.memset(pick_sum[:], 1.0))
            step(pool.memset(pick_sum[:, :, 0:HG], 0.0))
            keep(pick_sum[:, :, 0:HG], ALU.not_equal, 1.0, 0, [[1, HG], [-1, HG]], 0)
            step(pool.memset(spread[:], 0.0))
            for n in range(NP):
                for c in range(2):
                    h = 2 * n + c
                    keep(spread[:, n, D1 * c:D1 * c + D1], ALU.not_equal, 1.0, -(32 * (h % 4) + h // 4), [[0, D1]], 1)

            def root(s, k, b):
                pool.wait_ge(s["var"].sem, s["var"].at(b, k))
                apart(pool)
                pool.tensor_scalar(veps[:], mv[:, :, 1], EPS, None, ALU.add).then_inc(s["veps"].sem, s["veps"].add(1))
                pool.wait_ge(s["veps"].sem, s["veps"].at(b, k))
                pool.tensor_tensor(rstd[:], veps[:], exponents[:, 0:NT], ALU.pow).then_inc(s["rstd"].sem, s["rstd"].add(1))

            s = SA
            credit(pool, s["xcopied"])
            with pool.Fori(0, B) as b:
                root(s, 1, b)
                pool.wait_ge(s["xn"].sem, s["xn"].at(b, 1))
                pool.tensor_copy(xn_all[:, bass.ds(b * NT, NT), :], xn[:]).then_inc(s["xcopied"].sem, s["xcopied"].add(1))
                for h in range(H0):
                    for half in range(2):
                        pool.wait_ge(s["A"].free.sem, s["A"].emptied(b, ("probs", h, half)))
                        apart(pool)
                        at = 256 if half == 0 else HALF0
                        v = arena[:, (h % 8) * 2 * HALF0 + at:(h % 8) * 2 * HALF0 + at + 1024] \
                            .rearrange("p (j t) -> p j t", j=2)[:, :, 0:P]
                        pool.affine_select(
                            out=v, in_=v, compare_op=ALU.is_ge, fill=0.0, base=0,
                            pattern=[[0, 2], [-1 if half == 0 else 1, P]], channel_multiplier=1 if half == 0 else -1).then_inc(s["masked"].sem, s["masked"].add(1))
            phase_end(pool, 1)

            n_const = 0
            for ins in (
                    lambda: pool.memset(ones, 1.0),
                    lambda: pool.affine_select(out=before, in_=ones, compare_op=ALU.is_gt, fill=0.0, base=0,
                                               pattern=[[1, P]], channel_multiplier=-1),
                    lambda: pool.iota(steps, pattern=[[P, TT]], base=0, channel_multiplier=0,
                                      allow_small_or_imprecise_dtypes=True),
                    lambda: pool.memset(lower, 1.0),
                    lambda: pool.affine_select(out=lower, in_=lower, compare_op=ALU.is_gt, fill=0.0, base=0,
                                               pattern=[[1, NE], [-1, NE]], channel_multiplier=0),
                    lambda: pool.iota(tile_no, pattern=[[1, NS + 2], [0, NE]], base=0, channel_multiplier=0,
                                      allow_small_or_imprecise_dtypes=True),
                    lambda: pool.memset(run, 0.0)):
                ins().then_inc(s_sort_const, 1)
                n_const += 1
                pool.wait_ge(s_sort_const, n_const)
            assert n_const == N_SORT
            pool.wait_ge(s_zero, 16)
            pool.wait_ge(s_slots, 1)
            for t in range(TT):
                pool.indirect_dma_start(slots_x, bass.IndirectOffsetOnAxis(ap=slots[:, t:t + 1], axis=0),
                                        xn_all[:, t, :], None).then_inc(s_sent, 16)
            pool.wait_ge(s_sent, 16 * TT)
            for u in range(TURN_B):
                pool.wait_ge(SB["out"][u].sem, SB["out"][u].at(TURNS_B, 0))
            for t in range(TT):
                pool.indirect_dma_start(xn_all[:, t, :], None, slots_y,
                                        bass.IndirectOffsetOnAxis(ap=slots[:, t:t + 1], axis=0)).then_inc(s_back, 16)
            phase_end(pool, 2)

            def k_length(b):
                s = SR
                pool.wait_ge(s["sums"].sem, s["sums"].at(b, 1))
                pool.tensor_tensor(klen[:], ksum[:], exponents[:, NT:2 * NT], ALU.pow).then_inc(s["lens"].sem, s["lens"].add(1))

            def attend(b, last):
                s = SC
                for name in ("veps", "rstd", "lens", "masked"):
                    s[name].restart()
                for name in () if last else ("veps", "rstd", "lens"):
                    SR[name].restart()

                def q_length(n):
                    pool.wait_ge(s["sums"].sem, s["sums"].at(b, n + 1))
                    pool.tensor_tensor(q_len[:, 0:2 * NT], q_sum[:, 0:2 * NT], exponents[:, NT:3 * NT],
                                       ALU.pow).then_inc(s["lens"].sem, s["lens"].add(1))

                q_length(0)
                q_length(1)
                for n in range(NP):
                    if n + 2 < NP:
                        q_length(n + 2)
                    at = (n % PB) * 2560
                    for third, spans in enumerate((((0, 512),), ((896, 512),), ((1792, 256), (2304, 128)))):
                        pool.wait_ge(s["A"].free.sem, s["A"].emptied(b, ("probs", n, third)))
                        apart(pool)
                        for lo, gap in spans:
                            v = arena[:, at + lo:at + lo + 2 * gap].rearrange("p (j t) -> p j t", j=2)[:, :, 0:P]
                            ins = pool.affine_select(out=v, in_=v, compare_op=ALU.is_ge, fill=0.0, base=0,
                                                     pattern=[[0, 2], [1, P]], channel_multiplier=-1)
                        ins.then_inc(s["masked"].sem, s["masked"].add(1))
                    if not last and n in (3, 4):
                        root(SR, n - 2, b + 1)
                if not last:
                    k_length(b + 1)
                root(s, 1, b)

            root(SR, 1, 0)
            root(SR, 2, 0)
            k_length(0)
            with pool.Fori(0, B - 1) as b:
                attend(b, last=False)
            attend(B - 1, last=True)

        @block.scalar
        def _(act):
            s = SA
            A = s["A"]
            credit(act, s["a_free"])
            with act.Fori(0, B) as b:
                act.wait_ge(s["lg"].sem, s["lg"].at(b, 1))
                act.activation(lge[:], lg[:], ACT.Exp).then_inc(s["lge"].sem, s["lge"].add(1))
                for h in range(H0):
                    for half in range(2):
                        act.wait_ge(A.full.sem, A.filled(b, ("probs", h, half)))
                        sl = A.slot(("probs", h, half))
                        if half == 0:
                            act.wait_ge(s["pv"].sem, s["pv"].at(b, max(h // HG - 1, 0)))
                        act.activation(probs[:, h % 8, half * HALF0:(half + 1) * HALF0],
                                                   sl[:, 128:1024] if half == 0 else sl[:, 0:HALF0], ACT.Exp).then_inc(A.free.sem, A.free.add(1))
            phase_end(act, 1)

            s = SB
            with act.Fori(0, TURNS_B) as b:
                for u in range(TURN_B):
                    act.wait_ge(s["h_full"].sem, s["h_full"].at(b, u + 1))
                    act.wait_ge(s["y_full"].sem, s["y_full"].at(b, max(u - 2 + 1, 0)))
                    for c in range(FC):
                        ins = act.activation(hidden[:, u % 2, c], banks_a[u % 2][:, c * P:(c + 1) * P], ACT.Relu,
                                             bias=staged[:, u, AT_B1 + c:AT_B1 + c + 1])
                    ins.then_inc(s["h_free"].sem, s["h_free"].add(1))
            phase_end(act, 2)

            credit(act, SC["a_free"])

            def attend(b):
                s = SC
                D, A = s["D"], s["A"]
                s["a_free"].restart()
                s["squared"].restart()

                def squares(n):
                    act.wait_ge(D.full.sem, D.filled(b, ("q", n)))
                    act.wait_ge(s["sums"].sem, s["sums"].at(b, n))
                    act.activation(q_sq.rearrange("p g d -> p (g d)"), D.slot(("q", n))[:],
                                   ACT.Square).then_inc(s["squared"].sem, s["squared"].add(1))

                def gate_up(c):
                    act.wait_ge(A.full.sem, A.filled(b, ("gu", c)))
                    sl = A.slot(("gu", c))
                    act.wait_ge(s["h1"].sem, s["h1"].at(b, max(c - 1, 0)))
                    act.activation(gu[:, c % 2, 0, :], sl[:, 0:T], ACT.Tanh, scale=0.5)
                    act.activation(gu[:, c % 2, 1:3, :], sl[:].rearrange("p (a t) -> p a t", a=2),
                                   ACT.Copy).then_inc(A.free.sem, A.free.add(1))

                def q_turned(n):
                    at = 2 * (n % PB)
                    act.wait_ge(A.full.sem, A.filled(b, ("q.T", n)))
                    act.activation(rows[:, at:at + 2, :], A.slot(("q.T", n))[:].rearrange("p (h t) -> p h t", h=2),
                                   ACT.Copy).then_inc(A.free.sem, A.free.add(1))

                squares(0)
                squares(1)
                gate_up(0)
                gate_up(1)
                q_turned(0)
                for n in range(NP):
                    if n + 2 < NP:
                        squares(n + 2)
                    if n + 1 < NP:
                        q_turned(n + 1)
                    for third, (lo, hi_, width) in enumerate(((0, 896, 896), (896, 1792, 896), (1792, 2560, 768))):
                        act.wait_ge(A.full.sem, A.filled(b, ("probs", n, third)))
                        sl = A.slot(("probs", n, third))
                        if third == 0:
                            act.wait_ge(s["pv"].sem, s["pv"].at(b, max(n - PB + 1, 0)))
                        act.activation(probs1[:, n % PB, lo:hi_], sl[:, 0:width], ACT.Exp).then_inc(A.free.sem, A.free.add(1))
                    if n == 0:
                        gate_up(2)

            with act.Fori(0, B - 1) as b:
                attend(b)
            attend(B - 1)

        @block.vector
        def _(dve):
            def setup(ins):
                ins.then_inc(s_set, 1)
                n_set[0] += 1

            setup(dve.memset(wq_rep[:], 0.0))
            setup(dve.memset(wk_rep[:], 0.0))
            setup(dve.memset(bq_col[:], 0.0))
            setup(dve.memset(bk_in[:], 0.0))
            dve.wait_ge(s_win, 16 * N_LOADS)
            dve.wait_ge(s_set, 4)
            for n, w in ((0, wk_rep), (1, wq_rep)):
                for c in range(3):
                    setup(dve.tensor_copy(w[:, :, :, c, :], nat[:, n, :].rearrange("p (g h d) -> p g h d", g=G, h=HG)))
            dve.wait_ge(s_pool, 9)
            setup(dve.reduce_sum(qlo_neg[:], rows4[:, 0, :], AX.X))
            setup(dve.reduce_sum(klo_neg[:], rows4[:, 1, :], AX.X))
            setup(dve.reduce_sum(ones_row[:], rows4[:, 2, :], AX.X))
            dve.wait_ge(s_set, n_set[0])
            setup(dve.tensor_scalar(bk_col[:], bk_in[:], ones_row[:, 0:1], None, ALU.add))
            setup(dve.tensor_copy(wffn[:].rearrange("p a f -> p (a f)"), wint))
            dve.wait_ge(s_set, n_set[0])
            setup(dve.tensor_scalar(wffn[:].rearrange("p a f -> p (a f)"), wffn[:].rearrange("p a f -> p (a f)"), DEQUANT,
                                    None, ALU.mult))
            dve.wait_ge(s_set, n_set[0])
            dve.wait_ge(s_x, 16 * B)
            dve.wait_ge(s_pool, N_POOL)

            def row_stats(s, src, b):
                for i in range(NT):
                    ins = dve.bn_stats(stats[:, i, :], src(i))
                ins.then_inc(s["own"].sem, s["own"].add(1))
                dve.wait_ge(s["own"].sem, s["own"].at(b, s["own"].n))
                apart(dve)
                for i in range(NT):
                    ins = dve.bn_aggr(mv[:, i, :], stats[:, i, :])
                ins.then_inc(s["var"].sem, s["var"].add(1))

            def row_apply(s, k, src, dst, b):
                dve.wait_ge(s["rstd"].sem, s["rstd"].at(b, k))
                dve.wait_ge(s["var"].sem, s["var"].at(b, k))
                for i in range(NT):
                    ins = dve.tensor_scalar(dst[:, i, :], src(i), mv[:, i, 0:1], rstd[:, i:i + 1], ALU.subtract, ALU.mult)
                return ins

            s = SA
            D = s["D"]
            credit(dve, s["d_free"], s["g_free"])
            with dve.Fori(0, B) as b:
                x_b = x_all[:, bass.ds(b, 1)].rearrange("p o i e -> p (o i) e")
                row_stats(s, lambda i: x_b[:, i, :], b)
                row_apply(s, 1, lambda i: x_b[:, i, :], xn, b).then_inc(s["xn"].sem, s["xn"].add(1))
                dve.wait_ge(D.full.sem, D.filled(b, "xn.T"))
                sl = D.slot("xn.T")
                dve.wait_ge(s["xcopied"].sem, s["xcopied"].at(b, 0))
                dve.tensor_copy(xn_t[:], sl[:]).then_inc(D.free.sem, D.free.add(1))

                def split(which, g, col, scale, neg, dst, ready):
                    dve.wait_ge(D.full.sem, D.filled(b, (which, g)))
                    sl = D.slot((which, g))
                    if g:
                        dve.wait_ge(ready.sem, ready.at(b, g))
                    elif which == "q":
                        dve.wait_ge(s["k_ready"].sem, s["k_ready"].at(b, G))
                    ins = dve.tensor_scalar(full[:], sl[:], col[:, g:g + 1], scale, ALU.add, ALU.mult)
                    ins.then_inc(D.free.sem, D.free.add(1))
                    dve.wait_ge(D.free.sem, D.emptied(b, (which, g)))
                    dve.tensor_copy(hi[:], full[:]).then_inc(s["own"].sem, s["own"].add(1))
                    dve.wait_ge(s["own"].sem, s["own"].at(b, s["own"].n))
                    dve.scalar_tensor_tensor(out=dst[:, g, :], in0=hi[:].bitcast(F32), scalar=neg[:, 0:1],
                                                        in1=full[:], op0=ALU.mult, op1=ALU.add).then_inc(ready.sem, ready.add(1))

                for g in range(G):
                    split("k", g, bk_col, 1.0, klo_neg, k_rows, s["k_ready"])
                for g in range(G):
                    split("q", g, bq_col, QSCALE0, qlo_neg, q_rows, s["q_ready"])
                    if g == 0:
                        dve.wait_ge(D.full.sem, D.filled(b, "v"))
                        sl = D.slot("v")
                        dve.tensor_tensor(
                            v_aug[:, :, :, 0:D0], sl[:].rearrange("p (i h d) -> p i h d", i=NT, h=H0),
                            bv_all[:].rearrange("p (o h d) -> p o h d", o=1, h=H0).to_broadcast([P, NT, H0, D0]), ALU.add).then_inc(D.free.sem, D.free.add(1))
                dve.wait_ge(D.full.sem, D.filled(b, "logits"))
                sl = D.slot("logits")
                lv = sl[:, 0:NT * NE].rearrange("p (i e) -> p i e", i=NT)
                dve.reduce_max(lmx[:], lv, AX.X).then_inc(s["own"].sem, s["own"].add(1))
                dve.wait_ge(s["own"].sem, s["own"].at(b, s["own"].n))
                ins = dve.tensor_tensor(lg[:], lv, lmx[:].unsqueeze(2).to_broadcast([P, NT, NE]), ALU.subtract)
                ins.then_inc(D.free.sem, D.free.add(1))
                dve.wait_ge(D.free.sem, D.emptied(b, "logits"))
                dve.scalar_tensor_tensor(out=lg2[:], in0=lg[:], scalar=0.0, in1=rev_e[:], op0=ALU.is_ge, op1=ALU.mult).then_inc(s["own"].sem, s["own"].add(1))
                dve.wait_ge(s["own"].sem, s["own"].at(b, s["own"].n))
                dve.reduce_max(cmx[:], lg2[:], AX.X).then_inc(s["lg"].sem, s["lg"].add(1))
                dve.wait_ge(s["lg"].sem, s["lg"].at(b, 1))
                dve.tensor_tensor(hot[:], lg2[:], cmx[:].unsqueeze(2).to_broadcast([P, NT, NE]), ALU.is_equal).then_inc(s["own"].sem, s["own"].add(1))
                dve.wait_ge(s["own"].sem, s["own"].at(b, s["own"].n))
                dve.wait_ge(s["lge"].sem, s["lge"].at(b, 1))
                dve.reduce_sum(lsum[:], lge[:], AX.X).then_inc(s["own"].sem, s["own"].add(1))
                dve.wait_ge(s["own"].sem, s["own"].at(b, s["own"].n))
                dve.reciprocal(wgt[:], lsum[:]).then_inc(s["own"].sem, s["own"].add(1))
                dve.wait_ge(s["own"].sem, s["own"].at(b, s["own"].n))
                dve.tensor_tensor(gate_all[:, bass.ds(b * NT, NT)], hot[:],
                                                 wgt[:].unsqueeze(2).to_broadcast([P, NT, NE]), ALU.mult).then_inc(s["gate"].sem, s["gate"].add(1))
                dve.wait_ge(s["gate"].sem, s["gate"].at(b, 1))

                def maxima(g, i):
                    first, many, m, at = BAND[i]
                    for h in range(HG):
                        dve.wait_ge(D.full.sem, D.filled(b, ("max", g, i, h)))
                        sl = D.slot(("max", g, i, h))
                        dve.wait_ge(D.free.sem, D.emptied(b, ("max", g, i, h), 2))
                        apart(dve)
                        dve.tensor_tensor_reduce(dump[:, h % 2, 0:many], sl[:, 0:many], masks[:, m, at:at + many], 1.0,
                                                             LOWEST, ALU.add, ALU.max, mx[:, h, i:i + 1]).then_inc(D.free.sem, D.free.add(1))

                def max_parts(g):
                    dve.wait_ge(D.free.sem, D.emptied(b, ("max", g, NT - 1, HG - 1)))
                    m_hi, m_lo = (m_cols[:, :, :, ROW_MAX + r].rearrange("p i h -> p h i") for r in (0, 1))
                    dve.tensor_scalar(m_hi.bitcast(F32R), mx[:], -1.0, None, ALU.mult).then_inc(s["own"].sem, s["own"].add(1))
                    dve.wait_ge(s["own"].sem, s["own"].at(b, s["own"].n))
                    dve.scalar_tensor_tensor(out=m_lo, in0=mx[:], scalar=-1.0, in1=m_hi, op0=ALU.mult,
                                                            op1=ALU.subtract).then_inc(s["mcol"].sem, s["mcol"].add(1))

                def out_rows(g):
                    dve.wait_ge(s["pv"].sem, s["pv"].at(b, g + 1))
                    dve.tensor_copy(o_raw[:], gather[:]).then_inc(s["g_free"].sem, s["g_free"].add(1))

                def divide(g):
                    dve.wait_ge(D.full.sem, D.filled(b, ("o.T", g)))
                    sl = D.slot(("o.T", g))
                    v = sl[:].rearrange("p (i h r) -> p i h r", i=NT, h=HG)
                    if g:
                        dve.wait_ge(D.free.sem, D.emptied(b, ("o.T", g - 1)))
                    dve.reciprocal(rden[:], v[:, :, :, D0]).then_inc(s["own"].sem, s["own"].add(1))
                    dve.wait_ge(s["own"].sem, s["own"].at(b, s["own"].n))
                    dve.tensor_tensor(
                        o_n[:, :, g * HG * D0:(g + 1) * HG * D0].rearrange("p i (h d) -> p i h d", h=HG),
                        v[:, :, :, 0:D0], rden[:].unsqueeze(3).to_broadcast([P, NT, HG, D0]), ALU.mult).then_inc(D.free.sem, D.free.add(1))

                for i in range(NT):
                    maxima(0, i)
                for g in range(G):
                    max_parts(g)
                    dve.wait_ge(D.full.sem, D.filled(b, ("q_max", g)))
                    sl = D.slot(("q_max", g))
                    if g >= 2:
                        dve.wait_ge(s["A"].full.sem, s["A"].full.at(b, 2 * HG * (g - 1)))
                    dve.wait_ge(s["q_ready"].sem, s["q_ready"].at(b, g + 1))
                    dve.tensor_tensor(q_max[:, g % 2, :], sl[:], q_rows[:, g, :].bitcast(F32), ALU.add).then_inc(D.free.sem, D.free.add(1))
                    for i in range(NT):
                        if g + 1 < G:
                            maxima(g + 1, i)
                        if g and i == 2:
                            out_rows(g - 1)
                    if g:
                        divide(g - 1)
                out_rows(G - 1)
                divide(G - 1)
                dve.wait_ge(D.full.sem, D.filled(b, "heads.T"))
                sl = D.slot("heads.T")
                dve.tensor_copy(o_t[:], sl[:]).then_inc(D.free.sem, D.free.add(1))
                dve.wait_ge(D.full.sem, D.filled(b, "attended"))
                sl = D.slot("attended")
                ins = dve.tensor_tensor(acc[:], tiles(sl), bo_all[:].unsqueeze(1).to_broadcast([P, NT, E]), ALU.add)
                ins.then_inc(D.free.sem, D.free.add(1))
                dve.wait_ge(D.free.sem, D.emptied(b, "attended"))
                dve.tensor_tensor(x_b, x_b, acc[:], ALU.add).then_inc(s["own"].sem, s["own"].add(1))
                dve.wait_ge(s["own"].sem, s["own"].at(b, s["own"].n))
            phase_end(dve, 1)

            s = SB
            n_sort = [0]

            def sorted_step(ins):
                ins.then_inc(s_sort, 1)
                n_sort[0] += 1

            sorted_step(dve.tensor_scalar(hot_e, gate_all[:].rearrange("p t e -> p e t"), 0.0, None, ALU.is_gt))
            sorted_step(dve.reduce_sum(wgt_all[:], gate_all[:], AX.X))
            rank = banks_d[0][:, 0:NE * TT].rearrange("p (e t) -> p e t", e=NE)
            total = banks_d[0][:, NE * TT:2 * NE * TT].rearrange("p (e t) -> p e t", e=NE)
            dve.wait_ge(s_sort_const, N_SORT)
            dve.wait_ge(s_rank, 1)
            sorted_step(dve.tensor_copy(run[:, 0, :, PAD:], total))
            for n in range(5):
                dve.wait_ge(s_sort, n_sort[0])
                sorted_step(dve.tensor_tensor(run[:, (n + 1) % 2, :, PAD:], run[:, n % 2, :, PAD:],
                                              run[:, n % 2, :, PAD - (1 << n):PAD + TT - (1 << n)], ALU.add))
            assert TT == 1 << 5
            up_to = run[:, 1]
            dve.wait_ge(s_sort, n_sort[0])
            sorted_step(dve.tensor_tensor(worked, up_to[:, :, PAD + TT - 1:PAD + TT].to_broadcast([P, NE, TT]),
                                          steps.unsqueeze(1).to_broadcast([P, NE, TT]), ALU.is_gt))
            dve.wait_ge(s_sort, n_sort[0])
            sorted_step(dve.reduce_sum(many_tiles, worked, AX.X))
            dve.wait_ge(s_sort, n_sort[0])
            sorted_step(dve.tensor_tensor(worked2, lower, many_tiles.unsqueeze(1).to_broadcast([P, NE, NE]), ALU.mult))
            dve.wait_ge(s_sort, n_sort[0])
            sorted_step(dve.reduce_sum(base_e, worked2, AX.X))
            sorted_step(dve.tensor_tensor(worked, rank, up_to[:, :, PAD - 1:PAD + TT - 1], ALU.add))
            dve.wait_ge(s_sort, n_sort[0])
            sorted_step(dve.scalar_tensor_tensor(out=run[:, 0, :, PAD:], in0=base_e.unsqueeze(2).to_broadcast([P, NE, TT]),
                                                 scalar=float(P), in1=worked, op0=ALU.mult, op1=ALU.add))
            dve.wait_ge(s_sort, n_sort[0])
            sorted_step(dve.tensor_tensor(worked, run[:, 0, :, PAD:], hot_e, ALU.mult))
            dve.wait_ge(s_sort, n_sort[0])
            sorted_step(dve.reduce_sum(slot_f, worked.rearrange("p e t -> p t e"), AX.X))
            dve.wait_ge(s_sort, n_sort[0])
            dve.tensor_copy(slots[:], slot_f).then_inc(s_slots, 1)
            sorted_step(dve.tensor_tensor(end_e, base_e, many_tiles, ALU.add))
            dve.wait_ge(s_sort, n_sort[0])
            sorted_step(dve.tensor_tensor(tile_past, tile_no, end_e.unsqueeze(1).to_broadcast([P, NS + 2, NE]), ALU.is_ge))
            dve.wait_ge(s_sort, n_sort[0])
            sorted_step(dve.reduce_sum(expert_f, tile_past, AX.X))
            dve.wait_ge(s_sort, n_sort[0])
            sorted_step(dve.tensor_scalar(tile_expert, expert_f, float(NE - 1), None, ALU.min))
            dve.wait_ge(s_sort, n_sort[0])

            def stage(tile, u):
                e = dve.value_load(tile_expert[0:1, tile], min_val=0, max_val=NE - 1)
                return dve.tensor_copy(staged[:, u], experts[:, bass.ds(e, 1)].rearrange("p o n -> p (o n)"))

            dve.wait_ge(s_w12, 64)
            for u in range(2):
                stage(slice(u, u + 1), u).then_inc(s["staged"].sem, 1)
            credit(dve, s["xt_free"], s["y_free"])
            with dve.Fori(0, TURNS_B) as b:
                for u in range(0, TURN_B, 2):
                    for v in (u, u + 1):
                        dve.wait_ge(s["xt_full"].sem, s["xt_full"].at(b, v + 1))
                        dve.tensor_copy(x_t[:, v % 2], banks_d[v % 2][:, 0:P]).then_inc(s["xt_free"].sem, s["xt_free"].add(1))
                    for v in (u, u + 1):
                        dve.wait_ge(s["y_free"].sem, s["y_free"].at(b, u))
                        stage(bass.ds(b * TURN_B + (v + 2), 1), (v + 2) % TURN_B).then_inc(s["staged"].sem, s["staged"].add(1))
                    for v in (u, u + 1):
                        dve.wait_ge(s["y_full"].sem, s["y_full"].at(b, v + 1))
                        dve.wait_ge(s["out"][v].sem, s["out"][v].at(b, 0))
                        dve.tensor_tensor(y_out[:, v], banks_a[v % 2][:, T:T + E], staged[:, v, AT_B2:EXPERT], ALU.add) \
                            .then_inc(s["y_free"].sem, s["y_free"].add(1))
            dve.wait_ge(s_back, 16 * TT)
            dve.tensor_tensor(xn_all[:], xn_all[:], wgt_all[:].unsqueeze(2).to_broadcast([P, TT, E]), ALU.mult).then_inc(s_sort, 1)
            dve.wait_ge(s_sort, n_sort[0] + 1)
            x_tiles = x_all[:].rearrange("p b i e -> p (b i) e")
            dve.tensor_tensor(x_tiles, x_tiles, xn_all[:], ALU.add)
            phase_end(dve, 2)

            credit(dve, SC["d_free"], SC["g_free"], SC["sums"], SC["h1"], SR["r_free"], SR["sums"])

            def x_of(b):
                return x_all[:, bass.ds(b, 1)].rearrange("p o i e -> p (o i) e")

            def inverse(s, length, dst, k, b, scale):
                dve.wait_ge(s["lens"].sem, s["lens"].at(b, k))
                dve.tensor_scalar(length, length, scale, NORM_EPS, ALU.mult, ALU.max).then_inc(s["own"].sem, s["own"].add(1))
                dve.wait_ge(s["own"].sem, s["own"].at(b, s["own"].n))
                dve.reciprocal(dst, length).then_inc(s["own"].sem, s["own"].add(1))
                dve.wait_ge(s["own"].sem, s["own"].at(b, s["own"].n))

            def x_turned(b):
                R = SR["R"]
                dve.wait_ge(R.full.sem, R.filled(b, "xn.T"))
                dve.tensor_copy(xn_t[:], R.slot("xn.T")).then_inc(R.free.sem, R.free.add(1))
                dve.wait_ge(R.full.sem, R.filled(b, "xa.T"))
                dve.tensor_scalar(xa_t[:], R.slot("xa.T"), g1_col[:, 0:1], None, ALU.mult).then_inc(R.free.sem, R.free.add(1))

            def kv_out(b):
                s = SR
                R = s["R"]
                dve.wait_ge(R.full.sem, R.filled(b, "k|v"))
                kv = tiles(R.slot("k|v"))
                dve.tensor_copy(v1, kv[:, :, D1:2 * D1])
                dve.tensor_copy(kf, kv[:, :, 0:D1]).then_inc(R.free.sem, R.free.add(1))
                dve.wait_ge(R.free.sem, R.emptied(b, "k|v"))
                dve.tensor_tensor(kn, kf, kf, ALU.mult).then_inc(s["own"].sem, s["own"].add(1))
                dve.wait_ge(s["own"].sem, s["own"].at(b, s["own"].n))
                dve.reduce_sum(ksum[:], kn, AX.X).then_inc(s["sums"].sem, s["sums"].add(1))

            def k_unit(b):
                s = SR
                inverse(s, klen[:], ksum[:], 1, b, 1.0)
                dve.scalar_tensor_tensor(out=kn, in0=kf, scalar=ROOT_SCALE, in1=ksum[:].unsqueeze(2).to_broadcast([P, NT, D1]),
                                         op0=ALU.mult, op1=ALU.mult).then_inc(s["own"].sem, s["own"].add(1))
                dve.wait_ge(s["own"].sem, s["own"].at(b, s["own"].n))
                twice = kn.unsqueeze(2).to_broadcast([P, NT, 2, D1])
                dve.tensor_copy(k_nat[:, 0].bitcast(F32R), twice).then_inc(s["own"].sem, s["own"].add(1))
                dve.wait_ge(s["own"].sem, s["own"].at(b, s["own"].n))
                dve.tensor_tensor(k_nat[:, 1], twice, k_nat[:, 0], ALU.subtract).then_inc(s["k_n"].sem, s["k_n"].add(1))

            def k_turned(b):
                R = SR["R"]
                for a in range(2):
                    dve.wait_ge(R.full.sem, R.filled(b, ("k.T", a)))
                    dve.tensor_copy(k_stack[:, a, :], R.slot(("k.T", a))).then_inc(R.free.sem, R.free.add(1))

            def attend(b, last):
                s = SC
                D, A = s["D"], s["A"]
                for name in ("d_free", "own", "var", "sums", "q_n", "h1", "g_free", "fin"):
                    s[name].restart()
                for name in () if last else ("r_free", "own", "var", "xn", "xa", "sums", "k_n"):
                    SR[name].restart()

                def q_unit(n):
                    dve.wait_ge(s["squared"].sem, s["squared"].at(b, n + 1))
                    dve.reduce_sum(q_sum[:, 0:2 * NT], q_sq, AX.X).then_inc(s["sums"].sem, s["sums"].add(1))
                    inverse(s, q_len[:, 0:2 * NT], q_rn[:, 0:2 * NT], n + 1, b, QSCALE1)
                    if n:
                        dve.wait_ge(s["q_n"].sem, s["q_n"].at(b, n))
                    dve.scalar_tensor_tensor(
                        out=q_n, in0=D.slot(("q", n))[:].rearrange("p (g d) -> p g d", d=D1), scalar=QSCALE1 * ROOT_SCALE,
                        in1=q_rn[:, 0:2 * NT].unsqueeze(2).to_broadcast([P, 2 * NT, D1]), op0=ALU.mult,
                        op1=ALU.mult).then_inc(D.free.sem, D.free.add(1))
                    dve.wait_ge(D.free.sem, D.emptied(b, ("q", n)))
                    if n > 1:
                        dve.wait_ge(A.full.sem, A.filled(b, ("q.T", n - 2)))
                    dve.tensor_copy(q_nat[:, n % 2, :, 0, :].bitcast(F32R), q_n).then_inc(s["own"].sem, s["own"].add(1))
                    dve.wait_ge(s["own"].sem, s["own"].at(b, s["own"].n))
                    dve.tensor_tensor(q_nat[:, n % 2, :, 1, :], q_n, q_nat[:, n % 2, :, 0, :],
                                      ALU.subtract).then_inc(s["q_n"].sem, s["q_n"].add(1))

                def silu_up(c):
                    dve.wait_ge(A.free.sem, A.emptied(b, ("gu", c)))
                    if c:
                        dve.wait_ge(s["h1"].sem, s["h1"].at(b, c))
                    dve.scalar_tensor_tensor(out=full[:], in0=gu[:, c % 2, 0, :], scalar=1.0, in1=gu[:, c % 2, 1, :], op0=ALU.add,
                                             op1=ALU.mult).then_inc(s["own"].sem, s["own"].add(1))
                    dve.wait_ge(s["own"].sem, s["own"].at(b, s["own"].n))
                    dve.scalar_tensor_tensor(out=h1[:, c, :], in0=full[:], scalar=0.5, in1=gu[:, c % 2, 2, :],
                                             op0=ALU.mult, op1=ALU.mult).then_inc(s["h1"].sem, s["h1"].add(1))

                def values_out(n):
                    dve.wait_ge(D.full.sem, D.filled(b, ("o", n)))
                    dve.tensor_copy(o1[:, n, :], D.slot(("o", n))[:]).then_inc(D.free.sem, D.free.add(1))

                q_unit(0)
                q_unit(1)
                silu_up(0)
                for n in range(NP):
                    if n + 2 < NP:
                        q_unit(n + 2)
                    if n < 2:
                        silu_up(n + 1)
                    if n:
                        values_out(n - 1)
                    if not last and n == 3:
                        row_stats(SR, lambda i: x_of(b + 1)[:, i, :], b + 1)
                    if not last and n == 4:
                        row_apply(SR, 1, lambda i: x_of(b + 1)[:, i, :], xn, b + 1).then_inc(SR["xn"].sem, SR["xn"].add(1))
                        dve.wait_ge(SR["xn"].sem, SR["xn"].at(b + 1, 1))
                        row_stats(SR, lambda i: xn[:, i, :], b + 1)
                    if not last and n == 5:
                        row_apply(SR, 2, lambda i: xn[:, i, :], xa, b + 1).then_inc(SR["xa"].sem, SR["xa"].add(1))
                values_out(NP - 1)
                if not last:
                    x_turned(b + 1)
                dve.wait_ge(s["pv"].sem, s["pv"].at(b, NP))
                dve.reciprocal(rsum, gather[:]).then_inc(s["g_free"].sem, s["g_free"].add(1))
                dve.wait_ge(D.full.sem, D.filled(b, "ffn"))
                dve.tensor_tensor(acc[:], tiles(D.slot("ffn")), x_of(b), ALU.add).then_inc(D.free.sem, D.free.add(1))
                dve.wait_ge(D.free.sem, D.emptied(b, "ffn"))
                if not last:
                    kv_out(b + 1)
                for n in range(NP):
                    dve.wait_ge(D.full.sem, D.filled(b, ("1/sum", n)))
                    dve.tensor_tensor(o1[:, n, :], D.slot(("1/sum", n))[:], o1[:, n, :], ALU.mult).then_inc(D.free.sem, D.free.add(1))
                    if n == 2 and not last:
                        k_unit(b + 1)
                if not last:
                    k_turned(b + 1)
                dve.wait_ge(D.full.sem, D.full.at(b, s["d_full"].per))
                row_stats(s, lambda i: gather[:, i * P:(i + 1) * P], b)
                row_apply(s, 1, lambda i: gather[:, i * P:(i + 1) * P], y1, b).then_inc(s["g_free"].sem, s["g_free"].add(1))
                dve.wait_ge(s["g_free"].sem, s["g_free"].at(b, 2))
                dve.tensor_tensor(y1, y1, g2_all[:].unsqueeze(1).to_broadcast([P, NT, E]), ALU.mult).then_inc(s["own"].sem, s["own"].add(1))
                dve.wait_ge(s["own"].sem, s["own"].at(b, s["own"].n))
                dve.wait_ge(s["stored"].sem, s["stored"].at(b, 0))
                dve.tensor_tensor(fin, y1, acc[:], ALU.add).then_inc(s["fin"].sem, s["fin"].add(1))
                dve.wait_ge(s["fin"].sem, s["fin"].at(b, 1))

            row_stats(SR, lambda i: x_of(0)[:, i, :], 0)
            row_apply(SR, 1, lambda i: x_of(0)[:, i, :], xn, 0).then_inc(SR["xn"].sem, SR["xn"].add(1))
            dve.wait_ge(SR["xn"].sem, SR["xn"].at(0, 1))
            row_stats(SR, lambda i: xn[:, i, :], 0)
            row_apply(SR, 2, lambda i: xn[:, i, :], xa, 0).then_inc(SR["xa"].sem, SR["xa"].add(1))
            x_turned(0)
            kv_out(0)
            k_unit(0)
            k_turned(0)
            with dve.Fori(0, B - 1) as b:
                attend(b, last=False)
            attend(B - 1, last=True)

        counts = {v.name: (v.n, v.per) for s in (SA, SB, SR, SC) for v in s.values() if isinstance(v, Signal)}
        assert all(n == per for n, per in counts.values()), {k: v for k, v in counts.items() if v[0] != v[1]}
        assert (n_pool[0], n_set[0], n_in[0]) == (N_POOL, N_SETUP, 16 * N_LOADS), (n_pool, n_set, n_in)


_INS = ["x", "wq", "bq", "wk", "bk", "wv", "bv", "wo", "bo", "w_router", "w1", "b1", "w2", "b2",
        "g1", "wq1_t", "wkv1_t", "wout1_t", "g2", "w_gate_t", "w_up_t", "w_down_t"]


def kernel(**inputs):
    import numpy as np
    import concourse.bacc as bacc
    from concourse.bass_utils import run_bass_kernel_spmd

    a0, f0, a1, f1 = "L0_attn_", "L0_ffn_", "L1_attn_", "L1_ffn_"
    laid = {"x": inputs[a0 + "hidden_states"], "w_router": inputs[f0 + "w_router"], "g1": inputs[a1 + "g1"],
            "g2": inputs[a1 + "g2"]}
    for n in ("wq", "bq", "wk", "bk", "wv", "bv", "wo", "bo"):
        laid[n] = inputs[a0 + n]
    for n in ("w1", "b1", "w2", "b2"):
        laid[n] = inputs[f0 + n]
    for n, k in (("wq1_t", a1 + "Wq"), ("wkv1_t", a1 + "Wkv"), ("wout1_t", a1 + "Wout"), ("w_gate_t", f1 + "w_gate"),
                 ("w_up_t", f1 + "w_up"), ("w_down_t", f1 + "w_down")):
        laid[n] = np.asarray(inputs[k]).T

    nc = bacc.Bacc("TRN2", target_bir_lowering=False, num_devices=1)
    arrays, args = {}, []
    for n in _INS:
        a = np.ascontiguousarray(laid[n])
        arrays[f"in_{n}"] = a
        args.append(nc.dram_tensor(f"in_{n}", a.shape, mybir.dt.from_np(a.dtype), kind="ExternalInput").ap())
    for n in ("slots_x", "slots_y"):
        args.append(nc.dram_tensor(n, (NS * P, E), F32, kind="Internal").ap())
    args.append(nc.dram_tensor("out_0", (B, T, E), F32, kind="ExternalOutput").ap())
    two_layers(nc, *args)
    r = run_bass_kernel_spmd(nc, [arrays], core_ids=[0])
    return r.results[0]["out_0"]
```

```python
from contextlib import ExitStack

import concourse.bass as bass
from concourse import mybir

ALU = mybir.AluOpType
ACT = mybir.ActivationFunctionType
AX = mybir.AxisListType
F32 = mybir.dt.float32
F32R = mybir.dt.float32r
BF16 = mybir.dt.bfloat16
I32 = mybir.dt.int32
U32 = mybir.dt.uint32

P = 128
B = 8
T = 512
E = 128
NT = T // P
EPS = 1e-5
NEG = -1e30
LOWEST = -3e38

H0, D0 = 16, 8
HG = 4
G = H0 // HG
ROW_KLO, ROW_QLO, ROW_MAX = 8, 16, 24
ROW_SUMLO = 4
QSCALE0 = D0 ** -0.5
BAND = [(0, 384, 0, 128), (0, 512, 0, 0), (0, 512, 1, 0), (128, 384, 1, 0)]
BAND_T = [(0, 384, 0), (0, 512, 384), (0, 512, 896), (128, 384, 1408)]
HALF0 = 896
PV_ORDER = (1, 2, 0, 3)

NE, F0 = 8, 512
FC = F0 // P
TT = B * NT
TURN_B = 4
TURNS_B = -(-(TT + NE - 1) // TURN_B)
NS = TURNS_B * TURN_B
AT_B1, AT_W2, AT_B2, EXPERT = F0, F0 + FC, 2 * F0 + FC, 2 * F0 + FC + E
INV = 8
ROUNDER = 1.5 * 2 ** 23
PAD = TT // 2
H1, D1 = 16, 64
NP = H1 // 2
QB, PB = 3, 4
QSCALE1, NORM_EPS, ROOT_SCALE = 16.0, 1e-12, 4.0
HID = 384
HC = HID // P
DEQUANT = 1.0 / 127.0
DR, AR = 3, 2

PER_N = dict(n_full=11, n_free=11, own=6, var=1, veps=1, rstd=1, xn=1, xcopied=1, halved=8, parted=8,
             k_dma0=16 * HG, k_dma1=16 * HG, k_dma2=16 * HG, k_dma3=16 * HG, lg=1, lge=1, gate=1)
PER_L = dict(d_full=17, d_free=17, own=1, mcol=1)
PER_A = dict(d_full=74, d_free=74, a_full=32, a_free=32, own=9, mcol=G, q_max=G, masked=32, pv=G, g_free=G)
PER_B = dict(xt_full=4, xt_free=4, staged=4, h_full=4 * 2, h_free=4, y_full=4, y_free=4,
             turn=1, in0=16, in1=16, in2=16, in3=16, out0=16, out1=16, out2=16, out3=16)
PER_R = dict(r_full=7, r_free=7, own=13, var=2, veps=2, rstd=2, xn=1, xa=1, squared=2, sums=3, lens=3, q_n=2, k_n=1, moved=4,
             picked=1, back=16 * NT, added=1)
PER_C = dict(squared=6, d_full=24, d_free=23, a_full=35, a_free=35, own=24, var=1, veps=1, rstd=1,
             sums=6, lens=6, q_n=6, h1=3, masked=24, pv=4, g_free=2, inverted=1, fin=1, stored=16)
CREDITED = dict(d_free=1, a_free=1, g_free=1, sums=1, h1=1, r_free=1, added=1, n_free=1, parted=1, q_max=1, xcopied=1, stored=1, pv=1,
                xt_free=1, y_full=1, y_free=1, staged=2, out0=1, out1=1, out2=1, out3=1)


N_POOL, N_SETUP, N_SETUP_ALL, N_FIRST, N_LATER = 23, 17, 19, 29, 10
N_LATE = 38
N_SORT = 9


class Signal:

    def __init__(self, ctx, nc, phase, name, per):
        self.name = f"{phase}_{name}"
        self.sem = ctx.enter_context(nc.semaphore(self.name))
        self.most = 0
        self.per, self.credit, self.n = per, CREDITED.get(name, 0), 0

    def add(self, k):
        self.n += k
        self.most = max(self.most, self.n)
        return k

    def restart(self):
        self.n = 0

    def at(self, b, k):
        return b * self.per + (k + self.credit)


class Ring:

    def __init__(self, full, free, slots):
        self.full, self.free, self.slots = full, free, slots
        self.number = {}

    def fillable(self, b, what):
        n = self.number.setdefault(what, len(self.number))
        return self.free.at(b, max(n - len(self.slots) + 1, 0))

    def slot(self, what):
        return self.slots[self.number[what] % len(self.slots)]

    def filled(self, b, what):
        return self.full.at(b, self.number[what] + 1)

    def before(self, b, what):
        return self.free.at(b, self.number[what])

    def emptied(self, b, what, before=0):
        return self.free.at(b, max(self.number[what] + 1 - before, 0))


def two_layers(nc, x, wq, bq, wk, bk, wv, bv, wo, bo, w_router, w1, b1, w2, b2,
               g1, wq1_t, wkv1_t, wout1_t, g2, w_gate_t, w_up_t, w_down_t, tokens_x, slots_y, out):
    x_d = x.rearrange("b (i p) e -> p b i e", p=P)
    out_d = out.rearrange("b (i p) e -> b p i e", p=P)

    with ExitStack() as ctx:
        def sb(name, shape, dt=F32):
            return ctx.enter_context(nc.sbuf_tensor(name, shape, dt))

        def sem(name):
            return ctx.enter_context(nc.semaphore(name))

        banks_d = [ctx.enter_context(nc.psum_tensor(f"ring_d{n}", [P, T], F32)) for n in range(DR)]
        gather = ctx.enter_context(nc.psum_tensor("gather", [P, T], F32))
        banks_a = [ctx.enter_context(nc.psum_tensor(f"ring_a{n}", [P, 2 * T], F32)) for n in range(AR)]

        def hidden_bank(u, c):
            half, at = divmod(c, FC // 2)
            return banks_a[u % 2][:, half * T + at * P:half * T + (at + 1) * P]

        def y_bank(u):
            return (banks_d[2], gather)[u % 2][:, 0:E]

        wq_rep, wk_rep = sb("wq_rep", [P, G, HG, 4, D0]), sb("wk_rep", [P, G, HG, 4, D0])
        wv_sb, wo_sb = sb("wv_sb", [P, E]), sb("wo_sb", [P, E])
        bq_col, bk_col, bk_in = sb("bq_col", [P, G]), sb("bk_col", [P, G]), sb("bk_in", [P, G])
        bv_all, bo_all, g2_all = sb("bv_all", [P, E]), sb("bo_all", [P, E]), sb("g2_all", [P, E])
        g1_col = sb("g1_col", [P, 1])
        router_sb = sb("router_sb", [P, NE])
        wq1_sb = sb("wq1_sb", [P, H1 * D1])
        wkv1_sb = sb("wkv1_sb", [P, 2 * D1])
        wout1_sb = sb("wout1_sb", [P, NP, E])
        wffn = sb("wffn", [P, 3, HID])
        ident = sb("ident", [P, P])
        qlo_neg, klo_neg, ones_row, sumlo_neg = (sb(n, [P, 1]) for n in ("qlo_neg", "klo_neg", "ones_row", "sumlo_neg"))
        rows4 = sb("rows4", [P, 4, HG])
        masks = sb("masks", [P, 2, T], BF16)
        rev_e = sb("rev_e", [P, NT, NE])
        pick_sum = sb("pick_sum", [P, HG, 32])
        spread = sb("spread", [P, NP, P], F32R)

        x_all = sb("x_all", [P, B, NT, E])
        xn_all = sb("xn_all", [P, TT, E])
        gate_all = sb("gate_all", [P, TT, NE])
        wgt_all = sb("wgt_all", [P, TT])
        slots, slots_now = sb("slots", [P, TT], U32), sb("slots_now", [P, NT], U32)
        tokens, tokens_now = sb("tokens", [P, NS], U32), sb("tokens_now", [P, TURN_B], U32)

        xn, xn_t = sb("xn", [P, NT, E]), sb("xn_t", [P, T])
        stats, mv = sb("stats", [P, NT, 6]), sb("mv", [P, NT, 2])
        veps, rstd = sb("veps", [P, NT]), sb("rstd", [P, NT])
        exponents = sb("exponents", [P, NT + H1])
        full, hi = sb("full", [P, T]), sb("hi", [P, T], F32R)
        k_rows, q_rows = sb("k_rows", [P, G, T], F32R), sb("q_rows", [P, G, T], F32R)
        q_max = sb("q_max", [P, 2, T], F32R)
        rows = sb("rows", [P, H0, T], F32R)
        v_aug = sb("v_aug", [P, NT, H0, 32])
        dump = sb("dump", [P, 2, T], BF16)
        mx = sb("mx", [P, HG, NT])
        m_cols = sb("m_cols", [P, NT, HG, 32])
        arena = sb("arena", [P, 16384])
        o_raw, o_t = sb("o_raw", [P, T]), sb("o_t", [P, T])
        rden = sb("rden", [P, NT, HG])
        o_n, acc = sb("o_n", [P, NT, E]), sb("acc", [P, NT, E])
        lg, lge, lg2, hot = (sb(n, [P, NT, NE]) for n in ("lg", "lge", "lg2", "hot"))
        lmx, cmx, lsum, wgt = (sb(n, [P, NT]) for n in ("lmx", "cmx", "lsum", "wgt"))
        xa_t = o_raw
        ksum, klen = sb("ksum", [P, NT]), sb("klen", [P, NT])
        k_stack = k_rows[:, 0:2, :]
        q_sum, q_len, q_rn = sb("q_sum", [P, H1]), sb("q_len", [P, H1]), sb("q_rn", [P, H1])

        probs = arena[:, 0:8 * 2 * HALF0].rearrange("p (h n) -> p h n", h=8)
        experts = arena[:, 0:NE * EXPERT].rearrange("p (e n) -> p e n", e=NE)
        b_at = NE * EXPERT
        staged = arena[:, b_at:b_at + TURN_B * EXPERT].rearrange("p (u n) -> p u n", u=TURN_B)
        sort_at = b_at + EXPERT
        b_at += TURN_B * EXPERT
        hidden = arena[:, b_at:b_at + 2 * F0].rearrange("p (u c t) -> p u c t", u=2, c=FC)
        at_tile = arena[:, b_at:b_at + TT * NS].rearrange("p (t s) -> p t s", t=TT)
        x_in = arena[:, b_at + 1024:b_at + 1536].rearrange("p (u e) -> p u e", u=TURN_B)
        x_t = arena[:, b_at + 1536:b_at + 1792].rearrange("p (u t) -> p u t", u=2)
        y_out = arena[:, b_at + 1792:b_at + 2304].rearrange("p (u e) -> p u e", u=TURN_B)
        tile_expert = arena[:, b_at + 2304:b_at + 2304 + NS + 2].bitcast(I32)
        assert b_at + 2304 + NS + 2 <= 16384

        at_place = rows[:, 0:TT * P // T, :].rearrange("p h (a c) -> p (h a) c", c=P)
        spare = rows[:, TT * P // T:, :].rearrange("p h t -> p (h t)")
        parts = spare[:, 0:2 * TT * NS].rearrange("p (t a s) -> p t a s", t=TT, a=2)
        tile_steps, tile_rows = parts[:, :, 0, :], parts[:, :, 1, :]

        probs1 = arena[:, 0:10240].rearrange("p (n t) -> p n t", n=PB)
        o1 = arena[:, 10240:14336].rearrange("p (n t) -> p n t", n=NP)
        q_sq = arena[:, 14336:14848].rearrange("p (g d) -> p g d", d=D1)
        q_n = arena[:, 14848:15360].rearrange("p (g d) -> p g d", d=D1)
        kf, kn = (arena[:, at:at + 256].rearrange("p (i d) -> p i d", i=NT) for at in (15360, 15616))
        y_back = arena[:, 15872:16384].rearrange("p (i e) -> p i e", i=NT)
        spare = rows[:, 2 * QB:2 * QB + 4, :].rearrange("p h t -> p (h t)")
        q_nat = spare.rearrange("p (n g a d) -> p n g a d", n=2, a=2, d=D1)
        spare = rows[:, 2 * QB + 4:2 * QB + 6, :].rearrange("p h t -> p (h t)")
        k_nat = spare.rearrange("p (a i r d) -> p a i r d", a=2, i=NT, r=2)
        spare = xn_all[:].rearrange("p t e -> p (t e)")
        gu = spare[:, 0:3072].rearrange("p (n a t) -> p n a t", n=2, a=3)
        y1, xa = (spare[:, at:at + 512].rearrange("p (i e) -> p i e", i=NT) for at in (3072, 3584))
        spare = v_aug[:].rearrange("p j h d -> p (j h d)")
        spread_made = spare[:, 0:NP * P].rearrange("p (n d) -> p n d", n=NP)
        v1 = spare[:, 0:NT * D1].rearrange("p (j d) -> p j d", j=NT)
        h1 = spare[:, 256:1792].rearrange("p (c t) -> p c t", c=HC)
        fin = o_t[:].rearrange("p (i e) -> p i e", i=NT)
        rsum = m_cols[:].rearrange("p i h r -> p (i h r)")
        rsum_rows = q_max[:, 0, :]
        wint = arena[:, 16384 - 1152:16384].bitcast(I32)
        nat = arena[:, 13000:13256].rearrange("p (a e) -> p a e", a=2)
        def sort_view(n):
            sort_views.append((sort_views[-1][1], sort_views[-1][1] + n))
            return arena[:, sort_views[-1][0]:sort_views[-1][1]]

        sort_views = [(0, sort_at)]
        ones, before, steps = sort_view(P), sort_view(P), sort_view(TT)
        lower = sort_view(NE * NE).rearrange("p (a c) -> p a c", a=NE)
        tile_no = sort_view((NS + 2) * NE).rearrange("p (s e) -> p s e", e=NE)
        hot_e = sort_view(NE * TT).rearrange("p (e t) -> p e t", e=NE)
        run = sort_view(2 * NE * (PAD + TT)).rearrange("p (a e t) -> p a e t", a=2, e=NE)
        worked = sort_view(NE * TT).rearrange("p (e t) -> p e t", e=NE)
        worked2 = sort_view(NE * NE).rearrange("p (a c) -> p a c", a=NE)
        tile_past = sort_view((NS + 2) * NE).rearrange("p (s e) -> p s e", e=NE)
        many_tiles, base_e, end_e = sort_view(NE), sort_view(NE), sort_view(NE)
        slot_f, expert_f = sort_view(TT), sort_view(NS + 2)
        column_no, token_no, token_f = sort_view(P), sort_view(TT), sort_view(NS)
        tile_half, tile_big, tile_f, place = (sort_view(TT) for _ in range(4))
        assert sort_views[-1][1] <= b_at


        s_apart = [sem("apart_vector"), sem("apart_gpsimd")]
        s_first, s_later, s_w12 = sem("first_weights_in"), sem("later_weights_in"), sem("experts_in")
        s_late = sem("phase_c_constants")
        s_sort_const, s_sort, s_rank = sem("sort_constants"), sem("sort_steps"), sem("ranks")
        s_sent, s_hot = sem("inputs_in_dram"), sem("token_tiles_placed")
        s_tiled, s_rows = sem("tiles_compared"), sem("rows_placed")
        s_inverse, s_tokens = sem("tokens_summed"), sem("tokens_known")
        s_x0, s_x, s_pool, s_set, s_phase = sem("first_x_in"), sem("x_in"), sem("pool_setup"), sem("dve_setup"), sem("phase_done")
        n_first, n_later, n_pool, n_set = [0], [0], [0], [0]

        def signals(phase, per):
            s = {k: Signal(ctx, nc, phase, k, v) for k, v in per.items()}
            if phase == "B":
                s["in"] = [s["in0"], s["in1"], s["in2"], s["in3"]]
                s["out"] = [s["out0"], s["out1"], s["out2"], s["out3"]]
                return s
            if phase == "R":
                s["R"] = Ring(s["r_full"], s["r_free"], [banks_a[n][:, at:at + T] for n in range(AR) for at in (0, T)])
                return s
            if phase == "N":
                s["N"] = Ring(s["n_full"], s["n_free"], banks_d[2:])
                s["k_dma"] = [s["k_dma0"], s["k_dma1"], s["k_dma2"], s["k_dma3"]]
                return s
            s["D"] = Ring(s["d_full"], s["d_free"], banks_d if phase == "C" else banks_d[:2])
            if phase != "L":
                s["A"] = Ring(s["a_full"], s["a_free"], banks_a)
            return s

        SN, SL, SA = signals("N", PER_N), signals("L", PER_L), signals("A", PER_A)
        SB, SR, SC = signals("B", PER_B), signals("R", PER_R), signals("C", PER_C)

        def credit(eng, *names):
            for n in names:
                eng.sem_inc(n.sem, n.credit)

        def phase_end(eng, n):
            eng.drain().then_inc(s_phase, 1)
            eng.wait_ge(s_phase, 5 * n)

        def apart(eng):
            eng.sem_inc(s_apart[0 if eng is nc.vector else 1], 1)

        def tiles(slot):
            return slot[:, :].rearrange("p (i e) -> p i e", i=NT)

        block = ctx.enter_context(nc.Block())

        @block.tensor
        def _(pe):
            pe.wait_ge(s_pool, N_POOL)

            def mm(out, lhs, rhs, start=True, stop=True):
                return pe.matmul(out, lhs, rhs, start=start, stop=stop, skip_group_check=True)

            def turn(slot, tile_of, n=NT):
                return [pe.transpose(slot[:, i * P:(i + 1) * P], tile_of(i), ident[:]) for i in range(n)][-1]

            pe.wait_ge(s_set, N_SETUP)
            credit(pe, SA["pv"])

            def turn_x0(b):
                N = SN["N"]
                SN["n_full"].restart()
                pe.wait_ge(SN["xn"].sem, SN["xn"].at(b, 1))
                pe.wait_ge(N.free.sem, N.fillable(b, "xn.T"))
                turn(N.slot("xn.T"), lambda i: xn[:, i, :]).then_inc(N.full.sem, N.full.add(1))

            def project(b, which, g, w):
                N = SN["N"]
                pe.wait_ge(N.free.sem, N.emptied(b, "xn.T"))
                pe.wait_ge(N.free.sem, N.fillable(b, (which, g)))
                mm(N.slot((which, g))[:], w[:, g].rearrange("p h c d -> p (h c d)"), xn_t[:]).then_inc(N.full.sem, N.full.add(1))

            def project_v(b):
                N = SN["N"]
                pe.wait_ge(N.free.sem, N.fillable(b, "v"))
                [mm(N.slot("v")[:, i * P:(i + 1) * P], xn_t[:, i * P:(i + 1) * P], wv_sb[:])
                 for i in range(NT)][-1].then_inc(N.full.sem, N.full.add(1))

            def route(b):
                N = SN["N"]
                pe.wait_ge(N.free.sem, N.fillable(b, "logits"))
                [mm(N.slot("logits")[:, i * NE:(i + 1) * NE], xn_t[:, i * P:(i + 1) * P], router_sb[:])
                 for i in range(NT)][-1].then_inc(N.full.sem, N.full.add(1))

            def score_rows(s, t, b, g, i, heads):
                D = s["D"]
                if i == 0 and heads[0] == 0:
                    pe.wait_ge(SN["parted"].sem, SN["parted"].at(b, 2 * g + 2))
                    pe.wait_ge(SN["k_dma"][g].sem, SN["k_dma"][g].at(b, 16 * HG))
                first, many, _, _ = BAND[i]
                for h in heads:
                    pe.wait_ge(D.free.sem, D.fillable(t, ("max", g, i, h)))
                    mm(D.slot(("max", g, i, h))[:, 0:many], q_rows[:, g, i * P:(i + 1) * P],
                       rows[:, HG * g + h, first:first + many]).then_inc(D.full.sem, D.full.add(1))

            def turn_max(s, t, g):
                D = s["D"]
                pe.wait_ge(s["mcol"].sem, s["mcol"].at(t, (g - 1) % G + 1 if s is SA else 1))
                pe.wait_ge(D.free.sem, D.fillable(t, ("q_max", g)))
                turn(D.slot(("q_max", g)), lambda i: m_cols[:, i].rearrange("p h r -> p (h r)")).then_inc(D.full.sem, D.full.add(1))

            def attend(b, last):
                s = SA
                D, A = s["D"], s["A"]
                for name in ("d_full", "a_full", "pv"):
                    s[name].restart()

                def score_cols(g, h, half):
                    pe.wait_ge(A.free.sem, A.fillable(b, ("probs", HG * g + h, half)))
                    sl = A.slot(("probs", HG * g + h, half))
                    for j in (2 * half, 2 * half + 1):
                        first, many, at = BAND_T[j]
                        at += 128 if half == 0 else -HALF0
                        ins = mm(sl[:, at:at + many], rows[:, HG * g + h, j * P:(j + 1) * P],
                                 q_max[:, g % 2, first:first + many])
                    ins.then_inc(A.full.sem, A.full.add(1))

                def values(g, js):
                    if js[0] == PV_ORDER[0]:
                        pe.wait_ge(s["masked"].sem, s["masked"].at(b, 2 * HG * (g + 1)))
                        pe.wait_ge(s["g_free"].sem, s["g_free"].at(b, g))
                        pe.wait_ge(SN["n_free"].sem, SN["N"].emptied(b, "v"))
                    for j in js:
                        first, many, at = BAND_T[j]
                        for h in range(HG):
                            ins = mm(gather[32 * h:32 * h + 32, first:first + many], v_aug[:, j, HG * g + h, :],
                                     probs[:, (HG * g + h) % 8, at:at + many],
                                     start=(j == PV_ORDER[0]), stop=(j == PV_ORDER[-1]))
                    if js[-1] == PV_ORDER[-1]:
                        ins.then_inc(s["pv"].sem, s["pv"].add(1))

                def turn_out(g):
                    pe.wait_ge(s["g_free"].sem, s["g_free"].at(b, g + 1))
                    pe.wait_ge(D.free.sem, D.fillable(b, ("o.T", g)))
                    turn(D.slot(("o.T", g)), lambda i: o_raw[:, i * P:(i + 1) * P]).then_inc(D.full.sem, D.full.add(1))

                for g in range(G):
                    ahead = g + 2 < G or not last
                    b_next, b_ahead = b + (g + 1) // G, b + (g + 2) // G
                    if g == 0:
                        pe.wait_ge(s["q_max"].sem, s["q_max"].at(b, g))
                    for i in range(NT):
                        for heads, half in (((0, 1), 0), ((2,), 1), ((3,), None)):
                            if g + 1 < G or not last:
                                score_rows(s, b, b_next, (g + 1) % G, i, heads)
                            elif heads[0] == 0:
                                pe.wait_ge(D.free.sem, D.before(b, ("max", 0, i, 0)))
                                pe.sem_inc(D.full.sem, D.full.add(HG))
                            if g and i == 0 and half == 0:
                                pe.wait_ge(s["q_max"].sem, s["q_max"].at(b, g))
                            if half is not None:
                                score_cols(g, i, half)
                        if i == 0 and ahead:
                            project(b_ahead, "k", (g + 2) % G, wk_rep)
                        if g > 1 and i == 2:
                            turn_out(g - 2)
                        if 0 < g < G - 1 and i:
                            values(g - 1, PV_ORDER[i - 1:i])
                        if g + 1 == G and i in (1, 2):
                            values(g - 1, PV_ORDER[2 * i - 2:2 * i])
                        if i == 2 and ahead:
                            project(b_ahead, "q", (g + 2) % G, wq_rep)
                        if g + 1 == G and i == 3:
                            turn_out(g - 1)
                    if g + 1 == G and not last:
                        route(b + 1)
                    if g + 1 < G or not last:
                        turn_max(s, b, (g + 1) % G)
                    else:
                        pe.wait_ge(D.free.sem, D.before(b, ("q_max", 0)))
                        pe.sem_inc(D.full.sem, D.full.add(1))
                    if 0 < g < G - 1:
                        values(g - 1, PV_ORDER[3:4])
                    if g == 1 and not last:
                        turn_x0(b + 1)
                values(G - 1, PV_ORDER)
                if not last:
                    project_v(b + 1)
                turn_out(G - 1)
                pe.wait_ge(D.free.sem, D.emptied(b, ("o.T", G - 1)))
                pe.wait_ge(D.free.sem, D.fillable(b, "heads.T"))
                turn(D.slot("heads.T"), lambda i: o_n[:, i, :]).then_inc(D.full.sem, D.full.add(1))
                pe.wait_ge(D.free.sem, D.emptied(b, "heads.T"))
                pe.wait_ge(D.free.sem, D.fillable(b, "attended"))
                [mm(D.slot("attended")[:, i * P:(i + 1) * P], o_t[:, i * P:(i + 1) * P], wo_sb[:])
                 for i in range(NT)][-1].then_inc(D.full.sem, D.full.add(1))

            turn_x0(0)
            for g in range(2):
                project(0, "k", g, wk_rep)
                project(0, "q", g, wq_rep)
            for i in range(NT):
                score_rows(SL, 0, 0, 0, i, range(HG))
            route(0)
            project_v(0)
            turn_max(SL, 0, 0)
            pe.wait_ge(s_later, 16 * N_LATER)
            with pe.Fori(0, B - 1) as b:
                attend(b, last=False)
            attend(B - 1, last=True)
            phase_end(pe, 1)

            s = SB
            pe.wait_ge(s_sort_const, 2)
            pe.wait_ge(s_sort, 1)
            mm(banks_d[0][:, 0:NE * TT], before, hot_e.rearrange("p e t -> p (e t)"))
            mm(banks_d[0][:, NE * TT:2 * NE * TT], ones, hot_e.rearrange("p e t -> p (e t)")).then_inc(s_rank, 1)
            for t in range(TT):
                if t % INV == 0:
                    pe.wait_ge(s_hot, t // INV + 1)
                    pe.wait_ge(s_rows, t // INV + 1)
                ins = mm(banks_d[2][:, 0:2 * NS], at_place[:, t], parts[:, t].rearrange("p a s -> p (a s)"),
                         start=(t == 0), stop=(t == TT - 1))
            ins.then_inc(s_inverse, 1)
            credit(pe, s["y_full"])
            def x_turned(b, u):
                pe.wait_ge(s["in"][u].sem, s["in"][u].at(b, 16))
                pe.wait_ge(s["xt_free"].sem, s["xt_free"].at(b, max(u - 1, 0)))
                pe.transpose(banks_d[u % 2][:, 0:P], x_in[:, u], ident[:]).then_inc(s["xt_full"].sem, s["xt_full"].add(1))

            def up(b, u):
                pe.wait_ge(s["xt_free"].sem, s["xt_free"].at(b, u + 1))
                pe.wait_ge(s["staged"].sem, s["staged"].at(b, u - 1))
                for c in range(FC):
                    ins = mm(hidden_bank(u, c), staged[:, u, 0:F0].rearrange("p (f c) -> p c f", c=FC)[:, c], x_t[:, u % 2])
                    if (c + 1) % (FC // 2) == 0:
                        ins.then_inc(s["h_full"].sem, s["h_full"].add(1))

            def down(b, u):
                pe.wait_ge(s["h_free"].sem, s["h_free"].at(b, u + 1))
                pe.wait_ge(s["y_free"].sem, s["y_free"].at(b, max(u - 1, 0)))
                for c in range(FC):
                    ins = mm(y_bank(u), hidden[:, u % 2, c],
                             staged[:, u, AT_W2 + c * E:AT_W2 + (c + 1) * E], start=(c == 0), stop=(c == FC - 1))
                ins.then_inc(s["y_full"].sem, s["y_full"].add(1))

            def run_experts(b, last):
                for name in ("xt_full", "h_full", "y_full"):
                    s[name].restart()
                up(b, 0)
                up(b, 1)
                x_turned(b, 2)
                x_turned(b, 3)
                down(b, 0)
                down(b, 1)
                up(b, 2)
                up(b, 3)
                if not last:
                    x_turned(b + 1, 0)
                    x_turned(b + 1, 1)
                down(b, 2)
                down(b, 3)

            x_turned(0, 0)
            x_turned(0, 1)
            with pe.Fori(0, TURNS_B - 1) as b:
                run_experts(b, last=False)
            run_experts(TURNS_B - 1, last=True)
            phase_end(pe, 2)

            credit(pe, SC["pv"])

            def turn_x(b, behind=True):
                s = SR
                R = s["R"]
                if behind:
                    pe.wait_ge(SC["a_free"].sem, SC["A"].emptied(b - 1, ("probs", NP - 1, 2)))
                for name, src, ready in (("xn.T", xn, s["xn"]), ("xa.T", xa, s["xa"])):
                    pe.wait_ge(ready.sem, ready.at(b, 1))
                    pe.wait_ge(R.free.sem, R.fillable(b, name))
                    turn(R.slot(name), lambda i: src[:, i, :]).then_inc(R.full.sem, R.full.add(1))

            def project_kv(b):
                R = SR["R"]
                pe.wait_ge(R.free.sem, R.emptied(b, "xa.T"))
                pe.wait_ge(R.free.sem, R.fillable(b, "k|v"))
                sl = R.slot("k|v")
                [mm(sl[:, i * P:(i + 1) * P], xa_t[:, i * P:(i + 1) * P], wkv1_sb[:])
                 for i in range(NT)][-1].then_inc(R.full.sem, R.full.add(1))

            def q_of(n, slot):
                return [mm(slot[:, i * P:(i + 1) * P], xa_t[:, i * P:(i + 1) * P], wq1_sb[:, n * P:(n + 1) * P])
                        for i in range(NT)][-1]

            def first_q(b):
                R = SR["R"]
                for n in range(2):
                    pe.wait_ge(R.free.sem, R.fillable(b, ("q", n)))
                    q_of(n, R.slot(("q", n))).then_inc(R.full.sem, R.full.add(1))

            def turn_k(b):
                s = SR
                R = s["R"]
                pe.wait_ge(s["k_n"].sem, s["k_n"].at(b, 1))
                for a in range(2):
                    pe.wait_ge(R.free.sem, R.fillable(b, ("k.T", a)))
                    turn(R.slot(("k.T", a)),
                         lambda i: k_nat[:, a, i].rearrange("p r d -> p (r d)").bitcast(F32)).then_inc(R.full.sem, R.full.add(1))

            def attend(b, last):
                s = SC
                D, A = s["D"], s["A"]
                for name in ("d_full", "a_full", "pv"):
                    s[name].restart()
                if not last:
                    SR["r_full"].restart()

                def project_q(n):
                    pe.wait_ge(D.free.sem, D.fillable(b, ("q", n)))
                    q_of(n, D.slot(("q", n))).then_inc(D.full.sem, D.full.add(1))

                def gate_up(c):
                    pe.wait_ge(A.free.sem, A.fillable(b, ("gu", c)))
                    sl = A.slot(("gu", c))
                    [mm(sl[:, n * T:(n + 1) * T], wffn[:, n, c * P:(c + 1) * P], xn_t[:])
                     for n in range(2)][-1].then_inc(A.full.sem, A.full.add(1))

                def turn_q(n):
                    if n < 2:
                        pe.wait_ge(SR["q_n"].sem, SR["q_n"].at(b, n + 1))
                    else:
                        pe.wait_ge(s["q_n"].sem, s["q_n"].at(b, n - 1))
                    pe.wait_ge(A.free.sem, A.fillable(b, ("q.T", n)))
                    sl = A.slot(("q.T", n))
                    [pe.transpose(sl[:, c * T + i * P:c * T + (i + 1) * P],
                                  q_nat[:, n % 2, 2 * i + c].rearrange("p a d -> p (a d)").bitcast(F32), ident[:])
                     for c in range(2) for i in range(NT)][-1].then_inc(A.full.sem, A.full.add(1))

                def stacked(out, j, q):
                    mm(out, k_stack[:, 0, j * P:(j + 1) * P], q, stop=False)
                    return mm(out, k_stack[:, 1, j * P:(j + 1) * P], q, start=False)

                def scores(n):
                    at = 2 * (n % QB)
                    pe.wait_ge(A.free.sem, A.emptied(b, ("q.T", n)))
                    for c in range(2):
                        pe.wait_ge(A.free.sem, A.fillable(b, ("probs", n, c)))
                        sl = A.slot(("probs", n, c))
                        stacked(sl[:, 0:512], 0, rows[:, at + c, :])
                        stacked(sl[:, 512:896], 1, rows[:, at + c, 128:512]).then_inc(A.full.sem, A.full.add(1))
                    pe.wait_ge(A.free.sem, A.fillable(b, ("probs", n, 2)))
                    sl = A.slot(("probs", n, 2))
                    stacked(sl[:, 0:512], 2, rows[:, at:at + 2, 256:512])
                    stacked(sl[:, 512:768], 3, rows[:, at:at + 2, 384:512]).then_inc(A.full.sem, A.full.add(1))

                def p_of(n, c, j):
                    at = ((c * 896, 512), (c * 896 + 512, 384), (1792 + c * 256, 256), (2304 + c * 128, 128))[j]
                    return probs1[:, n % PB, at[0]:at[0] + at[1]]

                def values1(n):
                    pe.wait_ge(s["masked"].sem, s["masked"].at(b, 3 * (n + 1)))
                    pe.wait_ge(D.free.sem, D.fillable(b, ("o", n)))
                    sl = D.slot(("o", n))
                    [mm(sl[D1 * c:D1 * c + D1, j * P:T], v1[:, j, :], p_of(n, c, j), start=(j == 0), stop=(j == NT - 1))
                     for j in range(NT) for c in range(2)][-1].then_inc(D.full.sem, D.full.add(1))

                def sums1(m):
                    if m == 0:
                        pe.wait_ge(s["g_free"].sem, s["g_free"].at(b, 0))
                    for j in range(NT):
                        for h in range(HG):
                            ins = mm(gather[32 * h:32 * h + 32, j * P:T], pick_sum[:, m, :], p_of(2 * m + h // 2, h % 2, j),
                                     start=(m == 0 and j == 0), stop=(m == NP // 2 - 1 and j == NT - 1))
                    ins.then_inc(s["pv"].sem, s["pv"].add(1))

                pe.wait_ge(SR["moved"].sem, SR["moved"].at(b, 4))
                pe.wait_ge(SR["r_free"].sem, SR["R"].emptied(b, ("k.T", 1)))
                turn_q(0)
                gate_up(0)
                for n in range(NP):
                    if n + 2 < NP:
                        project_q(n + 2)
                    if n + 1 < NP:
                        turn_q(n + 1)
                    scores(n)
                    if n < 2:
                        gate_up(n + 1)
                    if n:
                        values1(n - 1)
                        if n % 2 == 0:
                            sums1(n // 2 - 1)
                values1(NP - 1)
                if not last:
                    turn_x(b + 1)
                sums1(NP // 2 - 1)
                pe.wait_ge(s["h1"].sem, s["h1"].at(b, HC))
                pe.wait_ge(D.free.sem, D.fillable(b, "ffn"))
                sl = D.slot("ffn")
                [mm(sl[:, i * P:(i + 1) * P], h1[:, c, i * P:(i + 1) * P],
                    wffn[:, 2, c * P:(c + 1) * P], start=(c == 0), stop=(c == HC - 1))
                 for i in range(NT) for c in range(HC)][-1].then_inc(D.full.sem, D.full.add(1))
                if not last:
                    project_kv(b + 1)
                    first_q(b + 1)

                def spread_sums(n):
                    pe.wait_ge(D.free.sem, D.fillable(b, ("1/sum", n)))
                    mm(D.slot(("1/sum", n))[:], spread[:, n, :], rsum_rows).then_inc(D.full.sem, D.full.add(1))

                pe.wait_ge(s["g_free"].sem, s["g_free"].at(b, 1))
                pe.wait_ge(s["inverted"].sem, s["inverted"].at(b, 1))
                spread_sums(0)
                spread_sums(1)
                for n in range(NP):
                    if n + 2 < NP:
                        spread_sums(n + 2)
                    pe.wait_ge(D.free.sem, D.emptied(b, ("1/sum", n)))
                    ins = [mm(gather[:, i * P:(i + 1) * P], o1[:, n, i * P:(i + 1) * P], wout1_sb[:, n, :],
                              start=(n == 0 and i == 0), stop=(n == NP - 1)) for i in range(NT)][-1]
                    if n == NP - 1:
                        ins.then_inc(D.full.sem, D.full.add(1))
                    if n == NP - 2 and not last:
                        turn_k(b + 1)

            turn_x(0, behind=False)
            project_kv(0)
            first_q(0)
            turn_k(0)
            pe.wait_ge(s_late, N_LATE)
            with pe.Fori(0, B - 1) as b:
                attend(b, last=False)
            attend(B - 1, last=True)

        @block.sync
        def _(sp):
            def first(dst, src):
                sp.dma_start(dst, src, allow_slow_non_contiguous=True).then_inc(s_first, 16)
                n_first[0] += 1

            def later(dst, src):
                sp.dma_start(dst, src, allow_slow_non_contiguous=True).then_inc(s_later, 16)
                n_later[0] += 1

            sp.dma_start(x_all[:, 0], x_d[:, 0]).then_inc(s_x0, 16)
            first(nat[:, 0, :], wk)
            first(nat[:, 1, :], wq)
            sp.wait_ge(s_set, 2)
            for h in range(HG):
                for c in range(3):
                    r = 32 * h + D0 * c
                    first(bk_in[r:r + D0, :], bk.rearrange("(g h d) -> h d g", g=G, h=HG)[h])
            first(wv_sb[:], wv)
            first(router_sb[:], w_router)
            first(bv_all[:], bv.rearrange("(a e) -> a e", a=1).to_broadcast([P, E]))
            sp.wait_ge(s_set, 5)

            def pad_k(b, g):
                s = SN
                s["k_dma"][g].restart()
                sp.wait_ge(s["parted"].sem, s["parted"].at(b, 2 * g + 1))
                for h in range(HG):
                    sp.dma_start(rows[32 * h:32 * h + 32, HG * g + h, :].bitcast(F32),
                                 k_rows[32 * h:32 * h + 32, g, :].bitcast(F32)).then_inc(s["k_dma"][g].sem, s["k_dma"][g].add(16))

            pad_k(0, 0)
            pad_k(0, 1)
            for n in range(1, B):
                sp.dma_start(x_all[:, n], x_d[:, n]).then_inc(s_x, 16)
            later(wo_sb[:], wo)
            for t, v in ((bo_all, bo), (g2_all, g2)):
                later(t[:], v.rearrange("(a e) -> a e", a=1).to_broadcast([P, E]))
            later(g1_col[:], g1.rearrange("(e a) -> e a", a=1))
            for n, w in enumerate((w_gate_t, w_up_t)):
                later(wint[:, n * HID:(n + 1) * HID], w)
            later(wint[:, 2 * HID:3 * HID].rearrange("p (c e) -> p c e", c=HC), w_down_t.rearrange("(c p) e -> p c e", p=P))
            later(wq1_sb[:], wq1_t)
            later(wkv1_sb[:], wkv1_t)
            later(wout1_sb[:], wout1_t.rearrange("(n p) e -> p n e", p=P))
            with sp.Fori(0, B - 1) as b:
                pad_k(b, 2)
                pad_k(b, 3)
                pad_k(b + 1, 0)
                pad_k(b + 1, 1)
            pad_k(B - 1, 2)
            pad_k(B - 1, 3)
            phase_end(sp, 1)
            sp.dma_start(tokens_x.rearrange("(t p) e -> p t e", p=P), xn_all[:]).then_inc(s_sent, 16)
            for dst, src in ((experts[:, :, 0:F0], w1.rearrange("e d f -> d e f")),
                             (experts[:, :, AT_B1:AT_W2], b1.rearrange("e (f c) -> f e c", c=FC)),
                             (experts[:, :, AT_W2:AT_B2], w2.rearrange("e (f c) d -> f e (c d)", c=FC)),
                             (experts[:, :, AT_B2:EXPERT], b2.rearrange("(a e) d -> a e d", a=1).to_broadcast([P, NE, E]))):
                sp.dma_start(dst, src, allow_slow_non_contiguous=True).then_inc(s_w12, 16)
            s = SB
            credit(sp, *s["out"])
            y_rows = slots_y.rearrange("(b u p) e -> u p b e", u=TURN_B, p=P)
            with sp.Fori(1, TURNS_B) as b:
                for u in range(TURN_B):
                    sp.wait_ge(s["y_free"].sem, s["y_free"].at(b, u - 3))
                    sp.dma_start(y_rows[u][:, bass.ds(b - 1, 1)].rearrange("p o e -> p (o e)"), y_out[:, u]).then_inc(s["out"][u].sem, s["out"][u].add(16))
            for u in range(TURN_B):
                sp.wait_ge(s["y_free"].sem, s["y_free"].at(TURNS_B - 1, u + 1))
                sp.dma_start(y_rows[u, :, TURNS_B - 1], y_out[:, u]).then_inc(s["out"][u].sem, 16)
            phase_end(sp, 2)
            s = SC
            credit(sp, s["stored"])
            with sp.Fori(0, B) as b:
                sp.wait_ge(s["fin"].sem, s["fin"].at(b, 1))
                sp.dma_start(out_d[bass.ds(b, 1)].rearrange("o p i e -> (o p) i e"), fin).then_inc(s["stored"].sem, s["stored"].add(16))
            sp.wait_ge(s["stored"].sem, 16 * B + 1)

        @block.gpsimd
        def _(pool):
            def step(ins):
                ins.then_inc(s_pool, 1)
                n_pool[0] += 1
                pool.wait_ge(s_pool, n_pool[0])

            def keep(v, op, fill, base, pattern, mult):
                step(pool.affine_select(out=v, in_=v, compare_op=op, fill=fill, base=base, pattern=pattern,
                                        channel_multiplier=mult))

            for n, (row, many, val) in enumerate(((ROW_QLO, D0, -1.0), (ROW_KLO, D0, -1.0), (ROW_MAX, 2, 1.0),
                                                (ROW_SUMLO, NP // 2, -1.0))):
                step(pool.memset(rows4[:, n, :], val))
                keep(rows4[:, n, :], ALU.is_ge, 0.0, -row, [[-32, HG]], 1)
                keep(rows4[:, n, :], ALU.is_ge, 0.0, row + many - 1, [[32, HG]], -1)
            step(pool.memset(exponents[:, 0:NT], -0.5))
            step(pool.memset(exponents[:, NT:NT + H1], 0.5))
            step(pool.memset(ident[:], 0.0))
            keep(ident[:], ALU.not_equal, 1.0, 0, [[-1, P]], 1)
            step(pool.memset(masks[:], 0.0))
            keep(masks[:, 0, 384:512], ALU.is_ge, NEG, 0, [[-1, P]], 1)
            keep(masks[:, 1, 0:128], ALU.is_ge, NEG, 0, [[1, P]], -1)
            step(pool.iota(rev_e[:], pattern=[[0, NT], [-1, NE]], base=NE, channel_multiplier=0,
                           allow_small_or_imprecise_dtypes=True))
            step(pool.memset(m_cols[:], 0.0))
            step(pool.memset(v_aug[:], 0.0))
            step(pool.memset(v_aug[:, :, :, D0:D0 + 1], 1.0))

            def root(s, k, b):
                pool.wait_ge(s["var"].sem, s["var"].at(b, k))
                apart(pool)
                pool.tensor_scalar(veps[:], mv[:, :, 1], EPS, None, ALU.add).then_inc(s["veps"].sem, s["veps"].add(1))
                pool.wait_ge(s["veps"].sem, s["veps"].at(b, k))
                pool.tensor_tensor(rstd[:], veps[:], exponents[:, 0:NT], ALU.pow).then_inc(s["rstd"].sem, s["rstd"].add(1))

            credit(pool, SN["xcopied"])

            def x_root(b):
                for name in ("veps", "rstd", "xcopied"):
                    SN[name].restart()
                root(SN, 1, b)

            def keep_x(b):
                s = SN
                pool.wait_ge(s["xn"].sem, s["xn"].at(b, 1))
                pool.tensor_copy(xn_all[:, bass.ds(b * NT, NT), :], xn[:]).then_inc(s["xcopied"].sem, s["xcopied"].add(1))

            def attend(b, last):
                s = SA
                s["masked"].restart()
                for h in range(H0):
                    for half in range(2):
                        pool.wait_ge(s["A"].free.sem, s["A"].emptied(b, ("probs", h, half)))
                        apart(pool)
                        at = 256 if half == 0 else HALF0
                        v = arena[:, (h % 8) * 2 * HALF0 + at:(h % 8) * 2 * HALF0 + at + 1024] \
                            .rearrange("p (j t) -> p j t", j=2)[:, :, 0:P]
                        pool.affine_select(
                            out=v, in_=v, compare_op=ALU.is_ge, fill=0.0, base=0,
                            pattern=[[0, 2], [-1 if half == 0 else 1, P]], channel_multiplier=1 if half == 0 else -1).then_inc(s["masked"].sem, s["masked"].add(1))
                    if h == 3 and not last:
                        x_root(b + 1)
                    if h == 8 and not last:
                        keep_x(b + 1)

            x_root(0)
            keep_x(0)
            n_late = [0]

            def late(ins):
                ins.then_inc(s_late, 1)
                n_late[0] += 1
                pool.wait_ge(s_late, n_late[0])

            def keep_late(v, op, fill, base, pattern, mult):
                late(pool.affine_select(out=v, in_=v, compare_op=op, fill=fill, base=base, pattern=pattern,
                                        channel_multiplier=mult))

            late(pool.memset(pick_sum[:], 1.0))
            late(pool.memset(pick_sum[:, :, 0:2 * HG], 0.0))
            for r in (0, ROW_SUMLO):
                keep_late(pick_sum[:, :, r:r + HG], ALU.not_equal, 1.0, 0, [[1, HG], [-1, HG]], 0)
            with pool.Fori(0, B - 1) as b:
                attend(b, last=False)
            attend(B - 1, last=True)
            phase_end(pool, 1)

            n_const = 0
            for ins in (
                    lambda: pool.memset(ones, 1.0),
                    lambda: pool.affine_select(out=before, in_=ones, compare_op=ALU.is_gt, fill=0.0, base=0,
                                               pattern=[[1, P]], channel_multiplier=-1),
                    lambda: pool.memset(run, 0.0),
                    lambda: pool.iota(steps, pattern=[[P, TT]], base=0, channel_multiplier=0,
                                      allow_small_or_imprecise_dtypes=True),
                    lambda: pool.memset(lower, 1.0),
                    lambda: pool.affine_select(out=lower, in_=lower, compare_op=ALU.is_gt, fill=0.0, base=0,
                                               pattern=[[1, NE], [-1, NE]], channel_multiplier=0),
                    lambda: pool.iota(tile_no, pattern=[[1, NS + 2], [0, NE]], base=0, channel_multiplier=0,
                                      allow_small_or_imprecise_dtypes=True),
                    lambda: pool.iota(column_no, pattern=[[1, P]], base=0, channel_multiplier=0,
                                      allow_small_or_imprecise_dtypes=True),
                    lambda: pool.iota(token_no, pattern=[[P, TT]], base=0, channel_multiplier=1,
                                      allow_small_or_imprecise_dtypes=True)):
                ins().then_inc(s_sort_const, 1)
                n_const += 1
                pool.wait_ge(s_sort_const, n_const)
            assert n_const == N_SORT
            late(pool.memset(spread_made, 0.0))
            for n in range(NP):
                for c in range(2):
                    h = 2 * n + c
                    for r in (0, ROW_SUMLO):
                        keep_late(spread_made[:, n, D1 * c:D1 * c + D1], ALU.not_equal, 1.0,
                                  -(32 * (h % 4) + h // 4 + r), [[0, D1]], 1)
            late(pool.tensor_copy(spread[:], spread_made))
            assert n_late[0] == N_LATE

            def fetch_tokens(turn):
                pool.tensor_copy(tokens_now[:], turn).then_inc(SB["turn"].sem, SB["turn"].add(1))

            def fetch_inputs(u):
                pool.indirect_dma_start(x_in[:, u, :], None, tokens_x, bass.IndirectOffsetOnAxis(
                    ap=tokens_now[:, u:u + 1], axis=0)).then_inc(SB["in"][u].sem, 16)

            pool.wait_ge(s_sent, 16)
            pool.wait_ge(s_tokens, 1)
            fetch_tokens(tokens[:, 0:TURN_B])
            pool.wait_ge(SB["turn"].sem, SB["turn"].at(0, 1))
            for u in range(TURN_B):
                fetch_inputs(u)
            SB["turn"].restart()
            with pool.Fori(1, TURNS_B) as b:
                for u in range(TURN_B):
                    pool.wait_ge(SB["in"][u].sem, SB["in"][u].at(b, 0))
                apart(pool)
                fetch_tokens(tokens[:, bass.ds(b * TURN_B, TURN_B)])
                for u in range(TURN_B):
                    pool.wait_ge(SB["turn"].sem, SB["turn"].at(b, 1))
                    pool.wait_ge(SB["xt_full"].sem, SB["xt_full"].at(b, u - 3))
                    apart(pool)
                    fetch_inputs(u)
            for u in range(TURN_B):
                SB["in"][u].add(16)
            for u in range(TURN_B):
                pool.wait_ge(SB["out"][u].sem, SB["out"][u].at(TURNS_B, 0))
            phase_end(pool, 2)

            def fetch_slots(b):
                s = SR
                s["picked"].restart()
                s["back"].restart()
                pool.wait_ge(s["added"].sem, s["added"].at(b, 0))
                apart(pool)
                pool.tensor_copy(slots_now[:], slots[:, bass.ds(b * NT, NT)]).then_inc(s["picked"].sem, s["picked"].add(1))

            def fetch(b, tiles_of):
                s = SR
                pool.wait_ge(s["picked"].sem, s["picked"].at(b, 1))
                apart(pool)
                for i in tiles_of:
                    pool.indirect_dma_start(y_back[:, i, :], None, slots_y, bass.IndirectOffsetOnAxis(
                        ap=slots_now[:, i:i + 1], axis=0)).then_inc(s["back"].sem, s["back"].add(16))

            def q_length(s, k, b):
                pool.wait_ge(s["sums"].sem, s["sums"].at(b, k))
                pool.tensor_tensor(q_len[:, 0:2 * NT], q_sum[:, 0:2 * NT], exponents[:, NT:3 * NT],
                                   ALU.pow).then_inc(s["lens"].sem, s["lens"].add(1))

            def k_length(b):
                s = SR
                pool.wait_ge(s["sums"].sem, s["sums"].at(b, 1))
                pool.tensor_tensor(klen[:], ksum[:], exponents[:, NT:2 * NT], ALU.pow).then_inc(s["lens"].sem, s["lens"].add(1))

            def attend(b, last):
                s = SC
                for name in ("veps", "rstd", "lens", "masked"):
                    s[name].restart()
                for name in () if last else ("veps", "rstd", "lens"):
                    SR[name].restart()

                for n in range(NP):
                    if n + 2 < NP:
                        q_length(s, n + 1, b)
                    at = (n % PB) * 2560
                    for third, spans in enumerate((((0, 512),), ((896, 512),), ((1792, 256), (2304, 128)))):
                        pool.wait_ge(s["A"].free.sem, s["A"].emptied(b, ("probs", n, third)))
                        apart(pool)
                        for lo, gap in spans:
                            v = arena[:, at + lo:at + lo + 2 * gap].rearrange("p (j t) -> p j t", j=2)[:, :, 0:P]
                            ins = pool.affine_select(out=v, in_=v, compare_op=ALU.is_ge, fill=0.0, base=0,
                                                     pattern=[[0, 2], [1, P]], channel_multiplier=-1)
                        ins.then_inc(s["masked"].sem, s["masked"].add(1))
                    if not last and n == 0:
                        fetch_slots(b + 1)
                    if not last and n in (1, 2):
                        fetch(b + 1, (2 * n - 2, 2 * n - 1))
                    if not last and n in (4, 5):
                        root(SR, n - 3, b + 1)
                if not last:
                    k_length(b + 1)
                    q_length(SR, 2, b + 1)
                    q_length(SR, 3, b + 1)
                root(s, 1, b)

            fetch_slots(0)
            fetch(0, range(NT))
            root(SR, 1, 0)
            root(SR, 2, 0)
            k_length(0)
            q_length(SR, 2, 0)
            q_length(SR, 3, 0)
            with pool.Fori(0, B - 1) as b:
                attend(b, last=False)
            attend(B - 1, last=True)

        @block.scalar
        def _(act):
            credit(act, SA["a_free"], SA["g_free"], SN["n_free"])
            act.wait_ge(s_set, 2)
            for h in range(HG):
                for c in range(3):
                    r = 32 * h + D0 * c
                    act.dma_start(bq_col[r:r + D0, :], bq.rearrange("(g h d) -> h d g", g=G, h=HG)[h],
                                  allow_slow_non_contiguous=True).then_inc(s_first, 16)
                    n_first[0] += 1
            act.wait_ge(s_set, N_SETUP)

            def x_turned0(b):
                N = SN["N"]
                SN["halved"].restart()
                act.wait_ge(N.full.sem, N.filled(b, "xn.T"))
                act.activation(xn_t[:], N.slot("xn.T")[:], ACT.Copy).then_inc(N.free.sem, 1)

            def halve(b, which, g, col, scale):
                s = SN
                N = s["N"]
                act.wait_ge(N.full.sem, N.filled(b, (which, g)))
                act.wait_ge(s["parted"].sem, s["parted"].at(b, 2 * g + (which == "q")))
                sl = N.slot((which, g))
                act.activation(full[:], sl[:], ACT.Identity, bias=col[:, g:g + 1], scale=scale)
                act.activation(hi[:], sl[:], ACT.Identity, bias=col[:, g:g + 1], scale=scale).then_inc(s["halved"].sem, s["halved"].add(1))
                act.wait_ge(s["halved"].sem, s["halved"].at(b, s["halved"].n))
                act.sem_inc(N.free.sem, 1)

            def expl(b):
                s = SN
                s["lge"].restart()
                act.wait_ge(s["lg"].sem, s["lg"].at(b, 1))
                act.activation(lge[:], lg[:], ACT.Exp).then_inc(s["lge"].sem, s["lge"].add(1))

            def attend(b, last):
                s = SA
                A = s["A"]
                s["a_free"].restart()
                s["g_free"].restart()

                def out_rows(g):
                    act.wait_ge(s["pv"].sem, s["pv"].at(b, g + 1))
                    if g:
                        act.wait_ge(s["D"].full.sem, s["D"].filled(b, ("o.T", g - 1)))
                    act.activation(o_raw[:], gather[:], ACT.Copy).then_inc(s["g_free"].sem, s["g_free"].add(1))

                for g in range(G):
                    ahead = g + 2 < G or not last
                    b_ahead = b + (g + 2) // G
                    for i in range(HG):
                        h = HG * g + i
                        for half in range(2):
                            act.wait_ge(A.full.sem, A.filled(b, ("probs", h, half)))
                            sl = A.slot(("probs", h, half))
                            if half == 0:
                                act.wait_ge(s["pv"].sem, s["pv"].at(b, max(g - 1, 0)))
                            act.activation(probs[:, h % 8, half * HALF0:(half + 1) * HALF0],
                                           sl[:, 128:1024] if half == 0 else sl[:, 0:HALF0], ACT.Exp).then_inc(A.free.sem, A.free.add(1))
                        if i == 0 and ahead:
                            halve(b_ahead, "k", (g + 2) % G, bk_col, 1.0)
                        if g > 1 and i == 0:
                            out_rows(g - 2)
                        if g + 1 == G and i == 2:
                            out_rows(g - 1)
                        if i == 2 and ahead:
                            halve(b_ahead, "q", (g + 2) % G, bq_col, QSCALE0)
                    if g == 1 and not last:
                        x_turned0(b + 1)
                if not last:
                    expl(b + 1)
                out_rows(G - 1)

            x_turned0(0)
            for g in range(2):
                halve(0, "k", g, bk_col, 1.0)
                halve(0, "q", g, bq_col, QSCALE0)
            expl(0)
            with act.Fori(0, B - 1) as b:
                attend(b, last=False)
            attend(B - 1, last=True)
            phase_end(act, 1)

            s = SB
            for t in range(0, TT, INV):
                act.wait_ge(s_tiled, t // INV + 1)
                act.activation(tile_rows[:, t:t + INV], at_tile[:, t:t + INV], ACT.Copy, scale=token_no[:, 0:1]).then_inc(s_rows, 1)
            with act.Fori(0, TURNS_B) as b:
                for u in range(TURN_B):
                    act.wait_ge(s["y_full"].sem, s["y_full"].at(b, max(u - 2 + 1, 0)))
                    for c in range(FC):
                        if c % (FC // 2) == 0:
                            act.wait_ge(s["h_full"].sem, s["h_full"].at(b, 2 * u + c // (FC // 2) + 1))
                        ins = act.activation(hidden[:, u % 2, c], hidden_bank(u, c), ACT.Relu,
                                             bias=staged[:, u, AT_B1 + c:AT_B1 + c + 1])
                    ins.then_inc(s["h_free"].sem, s["h_free"].add(1))
            phase_end(act, 2)

            credit(act, SC["a_free"])

            def move_x(b):
                s = SR
                s["moved"].restart()
                act.wait_ge(s["r_full"].sem, s["R"].filled(b, "xn.T"))
                act.activation(xn_t[:], s["R"].slot("xn.T"), ACT.Copy).then_inc(s["moved"].sem, s["moved"].add(1))

            def move_kv(b):
                s = SR
                act.wait_ge(s["r_full"].sem, s["R"].filled(b, "k|v"))
                kv = tiles(s["R"].slot("k|v"))
                act.activation(v1, kv[:, :, D1:2 * D1], ACT.Copy)
                act.activation(kf, kv[:, :, 0:D1], ACT.Copy)
                act.activation(kn, kv[:, :, 0:D1], ACT.Square).then_inc(s["moved"].sem, s["moved"].add(1))

            def move_k(b):
                s = SR
                for a in range(2):
                    act.wait_ge(s["r_full"].sem, s["R"].filled(b, ("k.T", a)))
                    act.activation(k_stack[:, a, :], s["R"].slot(("k.T", a)), ACT.Copy).then_inc(s["moved"].sem, s["moved"].add(1))

            def first_squares(b):
                s = SR
                s["squared"].restart()
                for n in range(2):
                    act.wait_ge(s["r_full"].sem, s["R"].filled(b, ("q", n)))
                    if n:
                        act.wait_ge(s["sums"].sem, s["sums"].at(b, 2))
                    act.activation(q_sq.rearrange("p g d -> p (g d)"), s["R"].slot(("q", n)),
                                   ACT.Square).then_inc(s["squared"].sem, s["squared"].add(1))

            def attend(b, last):
                s = SC
                D, A = s["D"], s["A"]
                s["a_free"].restart()
                s["squared"].restart()

                def squares(n):
                    act.wait_ge(D.full.sem, D.filled(b, ("q", n)))
                    if n == 2:
                        act.wait_ge(SR["sums"].sem, SR["sums"].at(b, 3))
                    else:
                        act.wait_ge(s["sums"].sem, s["sums"].at(b, n - 2))
                    act.activation(q_sq.rearrange("p g d -> p (g d)"), D.slot(("q", n))[:],
                                   ACT.Square).then_inc(s["squared"].sem, s["squared"].add(1))

                def gate_up(c):
                    act.wait_ge(A.full.sem, A.filled(b, ("gu", c)))
                    sl = A.slot(("gu", c))
                    act.wait_ge(s["h1"].sem, s["h1"].at(b, max(c - 1, 0)))
                    act.activation(gu[:, c % 2, 0, :], sl[:, 0:T], ACT.Tanh, scale=0.5)
                    act.activation(gu[:, c % 2, 1:3, :], sl[:].rearrange("p (a t) -> p a t", a=2),
                                   ACT.Copy).then_inc(A.free.sem, A.free.add(1))

                def q_turned(n):
                    at = 2 * (n % QB)
                    act.wait_ge(A.full.sem, A.filled(b, ("q.T", n)))
                    act.activation(rows[:, at:at + 2, :], A.slot(("q.T", n))[:].rearrange("p (h t) -> p h t", h=2),
                                   ACT.Copy).then_inc(A.free.sem, A.free.add(1))

                q_turned(0)
                gate_up(0)
                for n in range(NP):
                    if n + 2 < NP:
                        squares(n + 2)
                    if n + 1 < NP:
                        q_turned(n + 1)
                    for third, (lo, hi_, width) in enumerate(((0, 896, 896), (896, 1792, 896), (1792, 2560, 768))):
                        act.wait_ge(A.full.sem, A.filled(b, ("probs", n, third)))
                        sl = A.slot(("probs", n, third))
                        if third == 0:
                            act.wait_ge(s["pv"].sem, s["pv"].at(b, max(n // 2 - 1, 0)))
                        act.activation(probs1[:, n % PB, lo:hi_], sl[:, 0:width], ACT.Exp).then_inc(A.free.sem, A.free.add(1))
                    if n < 2:
                        gate_up(n + 1)
                if not last:
                    move_x(b + 1)
                    move_kv(b + 1)
                    first_squares(b + 1)
                    move_k(b + 1)

            move_x(0)
            move_kv(0)
            first_squares(0)
            move_k(0)
            with act.Fori(0, B - 1) as b:
                attend(b, last=False)
            attend(B - 1, last=True)

        @block.vector
        def _(dve):
            def setup(ins):
                ins.then_inc(s_set, 1)
                n_set[0] += 1

            setup(dve.memset(bq_col[:], 0.0))
            setup(dve.memset(bk_in[:], 0.0))
            setup(dve.memset(wq_rep[:], 0.0))
            setup(dve.memset(wk_rep[:], 0.0))
            def row_stats(s, src, b):
                for i in range(NT):
                    ins = dve.bn_stats(stats[:, i, :], src(i))
                ins.then_inc(s["own"].sem, s["own"].add(1))
                dve.wait_ge(s["own"].sem, s["own"].at(b, s["own"].n))
                apart(dve)
                for i in range(NT):
                    ins = dve.bn_aggr(mv[:, i, :], stats[:, i, :])
                ins.then_inc(s["var"].sem, s["var"].add(1))

            def row_apply(s, k, src, dst, b):
                dve.wait_ge(s["rstd"].sem, s["rstd"].at(b, k))
                dve.wait_ge(s["var"].sem, s["var"].at(b, k))
                for i in range(NT):
                    ins = dve.tensor_scalar(dst[:, i, :], src(i), mv[:, i, 0:1], rstd[:, i:i + 1], ALU.subtract, ALU.mult)
                return ins

            credit(dve, SA["d_free"], SL["d_free"], SN["parted"])

            def x_of(b):
                return x_all[:, bass.ds(b, 1)].rearrange("p o i e -> p (o i) e")

            def x_stats(b):
                for name in ("own", "var"):
                    SN[name].restart()
                row_stats(SN, lambda i: x_of(b)[:, i, :], b)

            def normalise_x(b):
                s = SN
                for name in ("xn", "parted", "lg", "gate"):
                    s[name].restart()
                dve.wait_ge(s["xcopied"].sem, s["xcopied"].at(b, 0))
                row_apply(s, 1, lambda i: x_of(b)[:, i, :], xn, b).then_inc(s["xn"].sem, s["xn"].add(1))

            def part(b, which, g, neg, dst):
                s = SN
                dve.wait_ge(s["halved"].sem, s["halved"].at(b, 2 * g + 1 + (which == "q")))
                dve.scalar_tensor_tensor(out=dst[:, g, :], in0=hi[:].bitcast(F32), scalar=neg[:, 0:1],
                                         in1=full[:], op0=ALU.mult, op1=ALU.add).then_inc(s["parted"].sem, s["parted"].add(1))

            def v_out(b):
                N = SN["N"]
                dve.wait_ge(N.full.sem, N.filled(b, "v"))
                dve.tensor_tensor(
                    v_aug[:, :, :, 0:D0], N.slot("v")[:].rearrange("p (i h d) -> p i h d", i=NT, h=H0),
                    bv_all[:].rearrange("p (o h d) -> p o h d", o=1, h=H0).to_broadcast([P, NT, H0, D0]), ALU.add).then_inc(N.free.sem, 1)

            def gate(b):
                s = SN
                N = s["N"]
                dve.wait_ge(N.full.sem, N.filled(b, "logits"))
                lv = N.slot("logits")[:, 0:NT * NE].rearrange("p (i e) -> p i e", i=NT)
                dve.reduce_max(lmx[:], lv, AX.X).then_inc(s["own"].sem, s["own"].add(1))
                dve.wait_ge(s["own"].sem, s["own"].at(b, s["own"].n))
                ins = dve.tensor_tensor(lg[:], lv, lmx[:].unsqueeze(2).to_broadcast([P, NT, NE]), ALU.subtract)
                ins.then_inc(N.free.sem, 1)
                dve.wait_ge(N.free.sem, N.emptied(b, "logits"))
                dve.scalar_tensor_tensor(out=lg2[:], in0=lg[:], scalar=0.0, in1=rev_e[:], op0=ALU.is_ge, op1=ALU.mult).then_inc(s["own"].sem, s["own"].add(1))
                dve.wait_ge(s["own"].sem, s["own"].at(b, s["own"].n))
                dve.reduce_max(cmx[:], lg2[:], AX.X).then_inc(s["lg"].sem, s["lg"].add(1))
                dve.wait_ge(s["lg"].sem, s["lg"].at(b, 1))
                dve.tensor_tensor(hot[:], lg2[:], cmx[:].unsqueeze(2).to_broadcast([P, NT, NE]), ALU.is_equal).then_inc(s["own"].sem, s["own"].add(1))
                dve.wait_ge(s["own"].sem, s["own"].at(b, s["own"].n))
                dve.wait_ge(s["lge"].sem, s["lge"].at(b, 1))
                dve.reduce_sum(lsum[:], lge[:], AX.X).then_inc(s["own"].sem, s["own"].add(1))
                dve.wait_ge(s["own"].sem, s["own"].at(b, s["own"].n))
                dve.reciprocal(wgt[:], lsum[:]).then_inc(s["own"].sem, s["own"].add(1))
                dve.wait_ge(s["own"].sem, s["own"].at(b, s["own"].n))
                dve.tensor_tensor(gate_all[:, bass.ds(b * NT, NT)], hot[:],
                                  wgt[:].unsqueeze(2).to_broadcast([P, NT, NE]), ALU.mult).then_inc(s["gate"].sem, s["gate"].add(1))
                dve.wait_ge(s["gate"].sem, s["gate"].at(b, 1))

            def maxima(s, t, g, i):
                D = s["D"]
                first, many, m, at = BAND[i]
                for h in range(HG):
                    dve.wait_ge(D.full.sem, D.filled(t, ("max", g, i, h)))
                    dve.wait_ge(D.free.sem, D.emptied(t, ("max", g, i, h), 2))
                    apart(dve)
                    dve.tensor_tensor_reduce(dump[:, h % 2, 0:many], D.slot(("max", g, i, h))[:, 0:many], masks[:, m, at:at + many],
                                             1.0, LOWEST, ALU.add, ALU.max, mx[:, h, i:i + 1]).then_inc(D.free.sem, D.free.add(1))

            def max_cols(s, t, g):
                D = s["D"]
                dve.wait_ge(D.free.sem, D.emptied(t, ("max", g, NT - 1, HG - 1)))
                m_hi, m_lo = (m_cols[:, :, :, ROW_MAX + r].rearrange("p i h -> p h i") for r in (0, 1))
                dve.tensor_scalar(m_hi.bitcast(F32R), mx[:], -1.0, None, ALU.mult).then_inc(s["own"].sem, s["own"].add(1))
                dve.wait_ge(s["own"].sem, s["own"].at(t, s["own"].n))
                dve.scalar_tensor_tensor(out=m_lo, in0=mx[:], scalar=-1.0, in1=m_hi, op0=ALU.mult,
                                         op1=ALU.subtract).then_inc(s["mcol"].sem, s["mcol"].add(1))

            def max_rows(s, t, g):
                D = s["D"]
                dve.wait_ge(D.full.sem, D.filled(t, ("q_max", g)))
                dve.tensor_tensor(q_max[:, g % 2, :], D.slot(("q_max", g))[:], q_rows[:, g, :].bitcast(F32),
                                  ALU.add).then_inc(D.free.sem, D.free.add(1))
                dve.wait_ge(D.free.sem, D.emptied(t, ("q_max", g)))
                dve.sem_inc(SA["q_max"].sem, SA["q_max"].add(1) if s is SA else 1)

            def attend(b, last):
                s = SA
                D, A = s["D"], s["A"]
                for name in ("d_free", "own", "mcol", "q_max"):
                    s[name].restart()

                def divide(g):
                    dve.wait_ge(D.full.sem, D.filled(b, ("o.T", g)))
                    v = D.slot(("o.T", g))[:].rearrange("p (i h r) -> p i h r", i=NT, h=HG)
                    if g:
                        dve.wait_ge(D.free.sem, D.emptied(b, ("o.T", g - 1)))
                    dve.reciprocal(rden[:], v[:, :, :, D0]).then_inc(s["own"].sem, s["own"].add(1))
                    dve.wait_ge(s["own"].sem, s["own"].at(b, s["own"].n))
                    dve.tensor_tensor(
                        o_n[:, :, g * HG * D0:(g + 1) * HG * D0].rearrange("p i (h d) -> p i h d", h=HG),
                        v[:, :, :, 0:D0], rden[:].unsqueeze(3).to_broadcast([P, NT, HG, D0]), ALU.mult).then_inc(D.free.sem, D.free.add(1))

                for g in range(G):
                    ahead = g + 2 < G or not last
                    b_ahead = b + (g + 2) // G
                    for i in range(NT):
                        if g + 1 < G or not last:
                            maxima(s, b, (g + 1) % G, i)
                        else:
                            dve.wait_ge(D.full.sem, D.filled(b, ("max", 0, i, HG - 1)))
                            dve.sem_inc(D.free.sem, D.free.add(HG))
                        if i == 1 and ahead:
                            part(b_ahead, "k", (g + 2) % G, klo_neg, k_rows)
                        if g > 1 and i == 2:
                            divide(g - 2)
                        if g + 1 == G and i == 3:
                            divide(g - 1)
                    if g + 1 < G or not last:
                        max_cols(s, b, (g + 1) % G)
                    if ahead:
                        part(b_ahead, "q", (g + 2) % G, qlo_neg, q_rows)
                    if g + 1 < G or not last:
                        max_rows(s, b, (g + 1) % G)
                    else:
                        dve.wait_ge(D.full.sem, D.filled(b, ("q_max", 0)))
                        dve.sem_inc(D.free.sem, D.free.add(1))
                    if g == 0 and not last:
                        x_stats(b + 1)
                    if g == 1 and not last:
                        normalise_x(b + 1)
                if not last:
                    gate(b + 1)
                    v_out(b + 1)
                divide(G - 1)
                dve.wait_ge(D.full.sem, D.filled(b, "heads.T"))
                dve.tensor_copy(o_t[:], D.slot("heads.T")[:]).then_inc(D.free.sem, D.free.add(1))
                dve.wait_ge(D.full.sem, D.filled(b, "attended"))
                ins = dve.tensor_tensor(acc[:], tiles(D.slot("attended")), bo_all[:].unsqueeze(1).to_broadcast([P, NT, E]), ALU.add)
                ins.then_inc(D.free.sem, D.free.add(1))
                dve.wait_ge(D.free.sem, D.emptied(b, "attended"))
                dve.tensor_tensor(x_of(b), x_of(b), acc[:], ALU.add).then_inc(s["own"].sem, s["own"].add(1))
                dve.wait_ge(s["own"].sem, s["own"].at(b, s["own"].n))

            dve.wait_ge(s_x0, 16)
            x_stats(0)
            setup(dve.memset(rows[:].bitcast(F32), 0.0))
            normalise_x(0)
            dve.wait_ge(s_first, 16 * N_FIRST)
            dve.wait_ge(s_set, 5)
            for n, w in ((0, wk_rep), (1, wq_rep)):
                for c in range(3):
                    setup(dve.tensor_copy(w[:, :, :, c, :], nat[:, n, :].rearrange("p (g h d) -> p g h d", g=G, h=HG)))
            dve.wait_ge(s_pool, 12)
            setup(dve.reduce_sum(qlo_neg[:], rows4[:, 0, :], AX.X))
            setup(dve.reduce_sum(klo_neg[:], rows4[:, 1, :], AX.X))
            setup(dve.reduce_sum(ones_row[:], rows4[:, 2, :], AX.X))
            setup(dve.reduce_sum(sumlo_neg[:], rows4[:, 3, :], AX.X))
            dve.wait_ge(s_set, n_set[0])
            setup(dve.tensor_scalar(bk_col[:], bk_in[:], ones_row[:, 0:1], None, ALU.add))
            setup(dve.tensor_scalar(bq_col[:], bq_col[:], QSCALE0, None, ALU.mult))
            assert n_set[0] == N_SETUP
            dve.wait_ge(s_set, n_set[0])
            dve.wait_ge(s_pool, N_POOL)
            for g in range(2):
                part(0, "k", g, klo_neg, k_rows)
                part(0, "q", g, qlo_neg, q_rows)
            for i in range(NT):
                maxima(SL, 0, 0, i)
            gate(0)
            v_out(0)
            max_cols(SL, 0, 0)
            max_rows(SL, 0, 0)
            dve.wait_ge(s_x, 16 * (B - 1))
            dve.wait_ge(s_later, 16 * N_LATER)
            setup(dve.tensor_copy(wffn[:].rearrange("p a f -> p (a f)"), wint))
            dve.wait_ge(s_set, n_set[0])
            setup(dve.tensor_scalar(wffn[:].rearrange("p a f -> p (a f)"), wffn[:].rearrange("p a f -> p (a f)"), DEQUANT,
                                    None, ALU.mult))
            dve.wait_ge(s_set, n_set[0])
            with dve.Fori(0, B - 1) as b:
                attend(b, last=False)
            attend(B - 1, last=True)
            SN["n_free"].add(len(SN["N"].number))
            phase_end(dve, 1)

            s = SB
            n_sort = [0]

            def sorted_step(ins):
                ins.then_inc(s_sort, 1)
                n_sort[0] += 1

            sorted_step(dve.tensor_scalar(hot_e, gate_all[:].rearrange("p t e -> p e t"), 0.0, None, ALU.is_gt))
            sorted_step(dve.reduce_sum(wgt_all[:], gate_all[:], AX.X))
            rank = banks_d[0][:, 0:NE * TT].rearrange("p (e t) -> p e t", e=NE)
            total = banks_d[0][:, NE * TT:2 * NE * TT].rearrange("p (e t) -> p e t", e=NE)
            dve.wait_ge(s_sort_const, 3)
            dve.wait_ge(s_rank, 1)
            sorted_step(dve.tensor_copy(run[:, 0, :, PAD:], total))
            for n in range(5):
                dve.wait_ge(s_sort, n_sort[0])
                sorted_step(dve.tensor_tensor(run[:, (n + 1) % 2, :, PAD:], run[:, n % 2, :, PAD:],
                                              run[:, n % 2, :, PAD - (1 << n):PAD + TT - (1 << n)], ALU.add))
            assert TT == 1 << 5
            dve.wait_ge(s_sort_const, N_SORT)
            up_to = run[:, 1]
            dve.wait_ge(s_sort, n_sort[0])
            sorted_step(dve.tensor_tensor(worked, up_to[:, :, PAD + TT - 1:PAD + TT].to_broadcast([P, NE, TT]),
                                          steps.unsqueeze(1).to_broadcast([P, NE, TT]), ALU.is_gt))
            dve.wait_ge(s_sort, n_sort[0])
            sorted_step(dve.reduce_sum(many_tiles, worked, AX.X))
            dve.wait_ge(s_sort, n_sort[0])
            sorted_step(dve.tensor_tensor(worked2, lower, many_tiles.unsqueeze(1).to_broadcast([P, NE, NE]), ALU.mult))
            dve.wait_ge(s_sort, n_sort[0])
            sorted_step(dve.reduce_sum(base_e, worked2, AX.X))
            sorted_step(dve.tensor_tensor(worked, rank, up_to[:, :, PAD - 1:PAD + TT - 1], ALU.add))
            dve.wait_ge(s_sort, n_sort[0])
            sorted_step(dve.scalar_tensor_tensor(out=run[:, 0, :, PAD:], in0=base_e.unsqueeze(2).to_broadcast([P, NE, TT]),
                                                 scalar=float(P), in1=worked, op0=ALU.mult, op1=ALU.add))
            dve.wait_ge(s_sort, n_sort[0])
            sorted_step(dve.tensor_tensor(worked, run[:, 0, :, PAD:], hot_e, ALU.mult))
            dve.wait_ge(s_sort, n_sort[0])
            sorted_step(dve.reduce_sum(slot_f, worked.rearrange("p e t -> p t e"), AX.X))
            dve.wait_ge(s_sort, n_sort[0])
            sorted_step(dve.tensor_copy(slots[:], slot_f))
            sorted_step(dve.tensor_scalar(tile_half, slot_f, -(P - 1) / 2, 1.0 / P, ALU.add, ALU.mult))
            dve.wait_ge(s_sort, n_sort[0])
            sorted_step(dve.tensor_scalar(tile_big, tile_half, ROUNDER, None, ALU.add))
            dve.wait_ge(s_sort, n_sort[0])
            sorted_step(dve.tensor_scalar(tile_f, tile_big, -ROUNDER, None, ALU.add))
            dve.wait_ge(s_sort, n_sort[0])
            sorted_step(dve.scalar_tensor_tensor(out=place, in0=tile_f, scalar=-float(P), in1=slot_f, op0=ALU.mult, op1=ALU.add))
            dve.wait_ge(s_sort, n_sort[0])
            for t in range(0, TT, INV):
                some = slice(t, t + INV)
                dve.tensor_tensor(at_tile[:, some], tile_no[:, 0:NS, 0].unsqueeze(1).to_broadcast([P, INV, NS]),
                                  tile_f[:, some].unsqueeze(2).to_broadcast([P, INV, NS]), ALU.is_equal).then_inc(s_tiled, 1)
                sorted_step(dve.tensor_tensor(at_place[:, some], column_no.unsqueeze(1).to_broadcast([P, INV, P]),
                                              place[:, some].unsqueeze(2).to_broadcast([P, INV, P]), ALU.is_equal))
                dve.wait_ge(s_tiled, t // INV + 1)
                dve.wait_ge(s_sort, n_sort[0])
                dve.tensor_tensor(tile_steps[:, some], at_tile[:, some], steps[:, some].unsqueeze(2).to_broadcast([P, INV, NS]),
                                  ALU.mult).then_inc(s_hot, 1)
            sorted_step(dve.tensor_tensor(end_e, base_e, many_tiles, ALU.add))
            dve.wait_ge(s_sort, n_sort[0])
            sorted_step(dve.tensor_tensor(tile_past, tile_no, end_e.unsqueeze(1).to_broadcast([P, NS + 2, NE]), ALU.is_ge))
            dve.wait_ge(s_sort, n_sort[0])
            sorted_step(dve.reduce_sum(expert_f, tile_past, AX.X))
            dve.wait_ge(s_sort, n_sort[0])
            sorted_step(dve.tensor_scalar(tile_expert, expert_f, float(NE - 1), None, ALU.min))
            dve.wait_ge(s_sort, n_sort[0])

            def stage(tile, u):
                e = dve.value_load(tile_expert[0:1, tile], min_val=0, max_val=NE - 1)
                return dve.tensor_copy(staged[:, u], experts[:, bass.ds(e, 1)].rearrange("p o n -> p (o n)"))

            dve.wait_ge(s_inverse, 1)
            sorted_step(dve.tensor_copy(token_f, banks_d[2][:, NS:2 * NS]))
            dve.wait_ge(s_sort, n_sort[0])
            sorted_step(dve.tensor_tensor(token_f, banks_d[2][:, 0:NS], token_f, ALU.add))
            dve.wait_ge(s_sort, n_sort[0])
            dve.tensor_copy(tokens[:], token_f).then_inc(s_tokens, 1)
            dve.wait_ge(s_w12, 64)
            for u in range(2):
                stage(slice(u, u + 1), u).then_inc(s["staged"].sem, 1)
            credit(dve, s["xt_free"], s["y_free"])

            def x_copied(b, u):
                dve.wait_ge(s["xt_full"].sem, s["xt_full"].at(b, u + 1))
                dve.tensor_copy(x_t[:, u % 2], banks_d[u % 2][:, 0:P]).then_inc(s["xt_free"].sem, s["xt_free"].add(1))

            def stage_ahead(b, u):
                dve.wait_ge(s["y_free"].sem, s["y_free"].at(b, u - u % 2))
                stage(bass.ds(b * TURN_B + (u + 2), 1), (u + 2) % TURN_B).then_inc(s["staged"].sem, s["staged"].add(1))

            def y_stored(b, u):
                dve.wait_ge(s["y_full"].sem, s["y_full"].at(b, u + 1))
                dve.wait_ge(s["out"][u].sem, s["out"][u].at(b, 0))
                dve.tensor_tensor(y_out[:, u], y_bank(u), staged[:, u, AT_B2:EXPERT], ALU.add) \
                    .then_inc(s["y_free"].sem, s["y_free"].add(1))

            def run_experts(b, last):
                for name in ("xt_free", "staged", "y_free"):
                    s[name].restart()
                stage_ahead(b, 0)
                stage_ahead(b, 1)
                x_copied(b, 2)
                x_copied(b, 3)
                y_stored(b, 0)
                y_stored(b, 1)
                stage_ahead(b, 2)
                stage_ahead(b, 3)
                if not last:
                    x_copied(b + 1, 0)
                    x_copied(b + 1, 1)
                y_stored(b, 2)
                y_stored(b, 3)

            x_copied(0, 0)
            x_copied(0, 1)
            with dve.Fori(0, TURNS_B - 1) as b:
                run_experts(b, last=False)
            run_experts(TURNS_B - 1, last=True)
            phase_end(dve, 2)

            credit(dve, SC["d_free"], SC["g_free"], SC["sums"], SC["h1"], SR["added"], SR["r_free"], SR["sums"])

            def inverse(s, length, dst, k, b, scale):
                dve.wait_ge(s["lens"].sem, s["lens"].at(b, k))
                dve.tensor_scalar(length, length, scale, NORM_EPS, ALU.mult, ALU.max).then_inc(s["own"].sem, s["own"].add(1))
                dve.wait_ge(s["own"].sem, s["own"].at(b, s["own"].n))
                dve.reciprocal(dst, length).then_inc(s["own"].sem, s["own"].add(1))
                dve.wait_ge(s["own"].sem, s["own"].at(b, s["own"].n))

            def add_experts(b):
                s = SR
                dve.wait_ge(s["back"].sem, s["back"].at(b, 16 * NT))
                dve.tensor_tensor(y_back, y_back, wgt_all[:, bass.ds(b * NT, NT)].unsqueeze(2).to_broadcast([P, NT, E]),
                                  ALU.mult).then_inc(s["own"].sem, s["own"].add(1))
                dve.wait_ge(s["own"].sem, s["own"].at(b, s["own"].n))
                dve.tensor_tensor(x_of(b), x_of(b), y_back, ALU.add).then_inc(s["added"].sem, s["added"].add(1))
                dve.wait_ge(s["added"].sem, s["added"].at(b, 1))

            def x_turned(b):
                R = SR["R"]
                dve.wait_ge(SR["moved"].sem, SR["moved"].at(b, 1))
                dve.sem_inc(R.free.sem, R.free.add(1))
                dve.wait_ge(R.full.sem, R.filled(b, "xa.T"))
                dve.tensor_scalar(xa_t[:], R.slot("xa.T"), g1_col[:, 0:1], None, ALU.mult).then_inc(R.free.sem, R.free.add(1))

            def kv_out(b):
                s = SR
                R = s["R"]
                dve.wait_ge(s["moved"].sem, s["moved"].at(b, 2))
                dve.sem_inc(R.free.sem, R.free.add(1))
                dve.reduce_sum(ksum[:], kn, AX.X).then_inc(s["sums"].sem, s["sums"].add(1))

            def k_unit(b):
                s = SR
                inverse(s, klen[:], ksum[:], 1, b, 1.0)
                dve.scalar_tensor_tensor(out=kn, in0=kf, scalar=ROOT_SCALE, in1=ksum[:].unsqueeze(2).to_broadcast([P, NT, D1]),
                                         op0=ALU.mult, op1=ALU.mult).then_inc(s["own"].sem, s["own"].add(1))
                dve.wait_ge(s["own"].sem, s["own"].at(b, s["own"].n))
                twice = kn.unsqueeze(2).to_broadcast([P, NT, 2, D1])
                dve.tensor_copy(k_nat[:, 0], twice).then_inc(s["own"].sem, s["own"].add(1))
                dve.wait_ge(s["own"].sem, s["own"].at(b, s["own"].n))
                dve.tensor_tensor(k_nat[:, 1], twice, k_nat[:, 0].bitcast(F32), ALU.subtract).then_inc(s["k_n"].sem, s["k_n"].add(1))

            def q_sums(s, k, b):
                dve.wait_ge(s["squared"].sem, s["squared"].at(b, k))
                dve.reduce_sum(q_sum[:, 0:2 * NT], q_sq, AX.X).then_inc(s["sums"].sem, s["sums"].add(1))

            def q_unit(s, n, b):
                ring, k = (s["R"], n) if s is SR else (s["D"], n - 2)
                inverse(s, q_len[:, 0:2 * NT], q_rn[:, 0:2 * NT], k + 2 if s is SR else k + 1, b, QSCALE1)
                if k:
                    dve.wait_ge(s["q_n"].sem, s["q_n"].at(b, k))
                dve.scalar_tensor_tensor(
                    out=q_n, in0=ring.slot(("q", n))[:, :].rearrange("p (g d) -> p g d", d=D1), scalar=QSCALE1 * ROOT_SCALE,
                    in1=q_rn[:, 0:2 * NT].unsqueeze(2).to_broadcast([P, 2 * NT, D1]), op0=ALU.mult,
                    op1=ALU.mult).then_inc(ring.free.sem, ring.free.add(1))
                dve.wait_ge(ring.free.sem, ring.emptied(b, ("q", n)))
                if n > 1:
                    dve.wait_ge(SC["a_full"].sem, SC["A"].filled(b, ("q.T", n - 2)))
                dve.tensor_copy(q_nat[:, n % 2, :, 0, :], q_n).then_inc(s["own"].sem, s["own"].add(1))
                dve.wait_ge(s["own"].sem, s["own"].at(b, s["own"].n))
                dve.tensor_tensor(q_nat[:, n % 2, :, 1, :], q_n, q_nat[:, n % 2, :, 0, :].bitcast(F32),
                                  ALU.subtract).then_inc(s["q_n"].sem, s["q_n"].add(1))

            def k_turned(b):
                R = SR["R"]
                dve.wait_ge(SR["moved"].sem, SR["moved"].at(b, 4))
                dve.sem_inc(R.free.sem, R.free.add(2))

            def attend(b, last):
                s = SC
                D, A = s["D"], s["A"]
                for name in ("d_free", "own", "var", "sums", "q_n", "h1", "g_free", "inverted", "fin"):
                    s[name].restart()
                for name in () if last else ("r_free", "own", "var", "xn", "xa", "sums", "q_n", "k_n", "added"):
                    SR[name].restart()

                def silu_up(c):
                    dve.wait_ge(A.free.sem, A.emptied(b, ("gu", c)))
                    if c:
                        dve.wait_ge(s["h1"].sem, s["h1"].at(b, c))
                    dve.scalar_tensor_tensor(out=full[:], in0=gu[:, c % 2, 0, :], scalar=1.0, in1=gu[:, c % 2, 1, :], op0=ALU.add,
                                             op1=ALU.mult).then_inc(s["own"].sem, s["own"].add(1))
                    dve.wait_ge(s["own"].sem, s["own"].at(b, s["own"].n))
                    dve.scalar_tensor_tensor(out=h1[:, c, :], in0=full[:], scalar=0.5, in1=gu[:, c % 2, 2, :],
                                             op0=ALU.mult, op1=ALU.mult).then_inc(s["h1"].sem, s["h1"].add(1))

                def values_out(n):
                    dve.wait_ge(D.full.sem, D.filled(b, ("o", n)))
                    dve.tensor_copy(o1[:, n, :], D.slot(("o", n))[:]).then_inc(D.free.sem, D.free.add(1))

                for n in range(NP):
                    if n + 2 < NP:
                        q_sums(s, n + 1, b)
                        q_unit(s, n + 2, b)
                    if n < 3:
                        silu_up(n)
                    if n:
                        values_out(n - 1)
                    if not last and n == 3:
                        add_experts(b + 1)
                    if not last and n == 4:
                        row_stats(SR, lambda i: x_of(b + 1)[:, i, :], b + 1)
                    if not last and n == 5:
                        row_apply(SR, 1, lambda i: x_of(b + 1)[:, i, :], xn, b + 1).then_inc(SR["xn"].sem, SR["xn"].add(1))
                        dve.wait_ge(SR["xn"].sem, SR["xn"].at(b + 1, 1))
                        row_stats(SR, lambda i: xn[:, i, :], b + 1)
                    if not last and n == 6:
                        row_apply(SR, 2, lambda i: xn[:, i, :], xa, b + 1).then_inc(SR["xa"].sem, SR["xa"].add(1))
                values_out(NP - 1)
                if not last:
                    x_turned(b + 1)
                dve.wait_ge(s["pv"].sem, s["pv"].at(b, NP // 2))
                dve.reciprocal(rsum, gather[:]).then_inc(s["g_free"].sem, s["g_free"].add(1))
                dve.wait_ge(s["g_free"].sem, s["g_free"].at(b, 1))
                dve.tensor_copy(hi[:], rsum).then_inc(s["own"].sem, s["own"].add(1))
                dve.wait_ge(s["own"].sem, s["own"].at(b, s["own"].n))
                dve.scalar_tensor_tensor(out=rsum_rows, in0=hi[:].bitcast(F32), scalar=sumlo_neg[:, 0:1], in1=rsum,
                                         op0=ALU.mult, op1=ALU.add).then_inc(s["inverted"].sem, s["inverted"].add(1))
                dve.wait_ge(D.full.sem, D.filled(b, "ffn"))
                dve.tensor_tensor(acc[:], tiles(D.slot("ffn")), x_of(b), ALU.add).then_inc(D.free.sem, D.free.add(1))
                dve.wait_ge(D.free.sem, D.emptied(b, "ffn"))
                if not last:
                    kv_out(b + 1)
                    q_sums(SR, 1, b + 1)
                for n in range(NP):
                    dve.wait_ge(D.full.sem, D.filled(b, ("1/sum", n)))
                    dve.tensor_tensor(o1[:, n, :], D.slot(("1/sum", n))[:], o1[:, n, :], ALU.mult).then_inc(D.free.sem, D.free.add(1))
                    if n == 2 and not last:
                        q_unit(SR, 0, b + 1)
                        q_sums(SR, 2, b + 1)
                    if n == 4 and not last:
                        k_unit(b + 1)
                if not last:
                    q_unit(SR, 1, b + 1)
                    k_turned(b + 1)
                dve.wait_ge(D.full.sem, D.full.at(b, s["d_full"].per))
                row_stats(s, lambda i: gather[:, i * P:(i + 1) * P], b)
                row_apply(s, 1, lambda i: gather[:, i * P:(i + 1) * P], y1, b).then_inc(s["g_free"].sem, s["g_free"].add(1))
                dve.wait_ge(s["g_free"].sem, s["g_free"].at(b, 2))
                dve.tensor_tensor(y1, y1, g2_all[:].unsqueeze(1).to_broadcast([P, NT, E]), ALU.mult).then_inc(s["own"].sem, s["own"].add(1))
                dve.wait_ge(s["own"].sem, s["own"].at(b, s["own"].n))
                dve.wait_ge(s["stored"].sem, s["stored"].at(b, 0))
                dve.tensor_tensor(fin, y1, acc[:], ALU.add).then_inc(s["fin"].sem, s["fin"].add(1))
                dve.wait_ge(s["fin"].sem, s["fin"].at(b, 1))

            add_experts(0)
            row_stats(SR, lambda i: x_of(0)[:, i, :], 0)
            row_apply(SR, 1, lambda i: x_of(0)[:, i, :], xn, 0).then_inc(SR["xn"].sem, SR["xn"].add(1))
            dve.wait_ge(SR["xn"].sem, SR["xn"].at(0, 1))
            row_stats(SR, lambda i: xn[:, i, :], 0)
            row_apply(SR, 2, lambda i: xn[:, i, :], xa, 0).then_inc(SR["xa"].sem, SR["xa"].add(1))
            x_turned(0)
            kv_out(0)
            q_sums(SR, 1, 0)
            q_unit(SR, 0, 0)
            q_sums(SR, 2, 0)
            k_unit(0)
            q_unit(SR, 1, 0)
            k_turned(0)
            with dve.Fori(0, B - 1) as b:
                attend(b, last=False)
            attend(B - 1, last=True)

        counts = {v.name: (v.most, v.per) for s in (SN, SL, SA, SB, SR, SC) for v in s.values() if isinstance(v, Signal)}
        assert all(n == per for n, per in counts.values()), {k: v for k, v in counts.items() if v[0] != v[1]}
        assert (n_pool[0], n_set[0], n_first[0], n_later[0]) == (N_POOL, N_SETUP_ALL, N_FIRST, N_LATER), \
            (n_pool, n_set, n_first, n_later)


_INS = ["x", "wq", "bq", "wk", "bk", "wv", "bv", "wo", "bo", "w_router", "w1", "b1", "w2", "b2",
        "g1", "wq1_t", "wkv1_t", "wout1_t", "g2", "w_gate_t", "w_up_t", "w_down_t"]


def kernel(**inputs):
    import numpy as np
    import concourse.bacc as bacc
    from concourse.bass_utils import run_bass_kernel_spmd

    a0, f0, a1, f1 = "L0_attn_", "L0_ffn_", "L1_attn_", "L1_ffn_"
    laid = {"x": inputs[a0 + "hidden_states"], "w_router": inputs[f0 + "w_router"], "g1": inputs[a1 + "g1"],
            "g2": inputs[a1 + "g2"]}
    for n in ("wq", "bq", "wk", "bk", "wv", "bv", "wo", "bo"):
        laid[n] = inputs[a0 + n]
    for n in ("w1", "b1", "w2", "b2"):
        laid[n] = inputs[f0 + n]
    for n, k in (("wq1_t", a1 + "Wq"), ("wkv1_t", a1 + "Wkv"), ("wout1_t", a1 + "Wout"), ("w_gate_t", f1 + "w_gate"),
                 ("w_up_t", f1 + "w_up"), ("w_down_t", f1 + "w_down")):
        laid[n] = np.asarray(inputs[k]).T

    nc = bacc.Bacc("TRN2", target_bir_lowering=False, num_devices=1)
    arrays, args = {}, []
    for n in _INS:
        a = np.ascontiguousarray(laid[n])
        arrays[f"in_{n}"] = a
        args.append(nc.dram_tensor(f"in_{n}", a.shape, mybir.dt.from_np(a.dtype), kind="ExternalInput").ap())
    args.append(nc.dram_tensor("tokens_x", (TT * P, E), F32, kind="Internal").ap())
    args.append(nc.dram_tensor("slots_y", (NS * P, E), F32, kind="Internal").ap())
    args.append(nc.dram_tensor("out_0", (B, T, E), F32, kind="ExternalOutput").ap())
    two_layers(nc, *args)
    r = run_bass_kernel_spmd(nc, [arrays], core_ids=[0])
    return r.results[0]["out_0"]
```
